# Optimizing a Trainium2 kernel written in Bass

```python
import numpy as np
import jax
import jax.numpy as jnp

def _softmax(x, axis=-1):
    return jax.nn.softmax(x, axis=axis)

def _gelu(x):
    return jax.nn.gelu(x, approximate=True)

def _silu(x):
    return jax.nn.silu(x)

def _sigmoid(x):
    return jax.nn.sigmoid(x)

def _layernorm(x, axis=-1, eps=1e-05):
    m = jnp.mean(x, axis=axis, keepdims=True)
    v = jnp.var(x, axis=axis, keepdims=True)
    return (x - m) / jnp.sqrt(v + eps)

def _scatter_add(tgt, idx, src, axis=0):
    return tgt.at[idx].add(src)

def _segment_sum(src, seg, n):
    return jax.ops.segment_sum(src, seg, n)
kernel_name = 'mk_gps_d1_gnn_r8_2c2545'

def setup_inputs(seed: int=0):
    np.random.seed(seed)
    _w = jnp.asarray

    def _rec_inputs():
        import jax
        import jax.numpy as jnp
        _gk = jax.random.key(seed)
        x = -0.0003713 + 1 * jax.random.normal(jax.random.fold_in(_gk, 1), (6250, 256), jnp.float32)
        _s = jax.random.randint(jax.random.fold_in(_gk, 2), (50000,), 0, 6250, jnp.int32)
        _d = jax.random.randint(jax.random.fold_in(_gk, 3), (50000,), 0, 6250, jnp.int32)
        _loop = jnp.arange(6250, dtype=jnp.int32)
        src = jnp.concatenate([_s, _d, _loop])
        dst = jnp.concatenate([_d, _s, _loop])
        _o = jnp.argsort(dst, stable=True)
        src = src[_o]
        dst = dst[_o]
        return (x, src, dst)
    x, src, dst = _rec_inputs()

    def _L0_gnn_setup():
        import jax, jax.numpy as jnp
        import numpy as np
        N_NODES = 6250

        def _graph_conv(x, edges, W0, b0, W1, b1):
            src = jnp.concatenate([edges[:, 0], edges[:, 1]])
            dst = jnp.concatenate([edges[:, 1], edges[:, 0]])
            deg = jax.ops.segment_sum(jnp.ones_like(dst, dtype=x.dtype), dst, num_segments=N_NODES)
            deg = jnp.maximum(deg, 1.0)
            agg = jax.ops.segment_sum(x[src], dst, num_segments=N_NODES) / deg[:, None]
            return x @ W0 + b0 + agg @ W1 + b1
        key = jax.random.key(seed)
        ks = jax.random.split(key, 10)
        feats = [256, 512, 256]
        inp = {'vert_features': jax.random.normal(ks[0], (N_NODES, feats[0]), dtype=jnp.float32), 'edges': jax.random.randint(ks[1], (50000, 2), 0, N_NODES, dtype=jnp.int64)}
        kidx = 2
        for l, (fi, fo) in enumerate(zip(feats[:-1], feats[1:])):
            s = 1.0 / np.sqrt(fi)
            inp[f'W0_{l}'] = jax.random.normal(ks[kidx], (fi, fo), dtype=jnp.float32) * s
            inp[f'b0_{l}'] = jnp.zeros((fo,), dtype=jnp.float32)
            inp[f'W1_{l}'] = jax.random.normal(ks[kidx + 1], (fi, fo), dtype=jnp.float32) * s
            inp[f'b1_{l}'] = jnp.zeros((fo,), dtype=jnp.float32)
            kidx += 2
        return inp
    _L0_gnn_all = _L0_gnn_setup()
    _L0_gnn_in = {k: v for k, v in _L0_gnn_all.items() if k in ('W0_0', 'b0_0', 'W1_0', 'b1_0', 'W0_1', 'b0_1', 'W1_1', 'b1_1')}
    del _L0_gnn_all

    def _L0_mix_setup():
        import jax, jax.numpy as jnp
        import numpy as np
        B, L, D, H = (4, 2048, 256, 8)
        DK = D // H

        def _heads(t):
            b, l, d = t.shape
            return t.reshape(b, l, H, DK).transpose(0, 2, 1, 3)
        key = jax.random.key(seed)
        ks = jax.random.split(key, 9)
        s = 0.02
        return {'x': jax.random.normal(ks[0], (B, L, D), dtype=jnp.float32), 'Wq': jax.random.normal(ks[1], (D, D), dtype=jnp.float32) * s, 'bq': jnp.zeros((D,), dtype=jnp.float32), 'Wk': jax.random.normal(ks[2], (D, D), dtype=jnp.float32) * s, 'bk': jnp.zeros((D,), dtype=jnp.float32), 'Wv': jax.random.normal(ks[3], (D, D), dtype=jnp.float32) * s, 'bv': jnp.zeros((D,), dtype=jnp.float32), 'Wfc': jax.random.normal(ks[4], (D, D), dtype=jnp.float32) * s, 'bfc': jnp.zeros((D,), dtype=jnp.float32)}
    _L0_mix_all = _L0_mix_setup()
    _L0_mix_in = {k: v for k, v in _L0_mix_all.items() if k in ('Wq', 'bq', 'Wk', 'bk', 'Wv', 'bv', 'Wfc', 'bfc')}
    del _L0_mix_all

    def _L0_ffn_setup():
        import jax, jax.numpy as jnp
        import numpy as np
        D_MODEL = 256
        EXPERT_DIM = 512
        NUM_EXPERTS = 8
        TOP_K = 2
        SEQ_LEN = 256
        BATCH = 2
        key = jax.random.key(seed)
        ks = jax.random.split(key, 8)
        s = 0.02
        x = jax.random.normal(ks[0], (SEQ_LEN, BATCH, D_MODEL), dtype=jnp.float32)
        Wg = jax.random.normal(ks[1], (D_MODEL, NUM_EXPERTS), dtype=jnp.float32) * s
        bg = jax.random.normal(ks[2], (NUM_EXPERTS,), dtype=jnp.float32) * s
        bias = jnp.zeros((NUM_EXPERTS,), dtype=jnp.float32)
        W1 = jax.random.normal(ks[3], (NUM_EXPERTS, D_MODEL, EXPERT_DIM), dtype=jnp.float32) * s
        b1 = jax.random.normal(ks[4], (NUM_EXPERTS, EXPERT_DIM), dtype=jnp.float32) * s
        W2 = jax.random.normal(ks[5], (NUM_EXPERTS, EXPERT_DIM, D_MODEL), dtype=jnp.float32) * s
        b2 = jax.random.normal(ks[6], (NUM_EXPERTS, D_MODEL), dtype=jnp.float32) * s
        return {'x': x, 'Wg': Wg, 'bg': bg, 'bias': bias, 'W1': W1, 'b1': b1, 'W2': W2, 'b2': b2}
    _L0_ffn_all = _L0_ffn_setup()
    _L0_ffn_in = {k: v for k, v in _L0_ffn_all.items() if k in ('Wg', 'bg', 'bias', 'W1', 'b1', 'W2', 'b2')}
    del _L0_ffn_all
    return {'x': x, 'src': src, 'dst': dst, 'L0_gnn_W0_0': _L0_gnn_in['W0_0'], 'L0_gnn_b0_0': _L0_gnn_in['b0_0'], 'L0_gnn_W1_0': _L0_gnn_in['W1_0'], 'L0_gnn_b1_0': _L0_gnn_in['b1_0'], 'L0_gnn_W0_1': _L0_gnn_in['W0_1'], 'L0_gnn_b0_1': _L0_gnn_in['b0_1'], 'L0_gnn_W1_1': _L0_gnn_in['W1_1'], 'L0_gnn_b1_1': _L0_gnn_in['b1_1'], 'L0_mix_Wq': _L0_mix_in['Wq'], 'L0_mix_bq': _L0_mix_in['bq'], 'L0_mix_Wk': _L0_mix_in['Wk'], 'L0_mix_bk': _L0_mix_in['bk'], 'L0_mix_Wv': _L0_mix_in['Wv'], 'L0_mix_bv': _L0_mix_in['bv'], 'L0_mix_Wfc': _L0_mix_in['Wfc'], 'L0_mix_bfc': _L0_mix_in['bfc'], 'L0_ffn_Wg': _L0_ffn_in['Wg'], 'L0_ffn_bg': _L0_ffn_in['bg'], 'L0_ffn_bias': _L0_ffn_in['bias'], 'L0_ffn_W1': _L0_ffn_in['W1'], 'L0_ffn_b1': _L0_ffn_in['b1'], 'L0_ffn_W2': _L0_ffn_in['W2'], 'L0_ffn_b2': _L0_ffn_in['b2']}

def reference(x, src, dst, L0_gnn_W0_0, L0_gnn_b0_0, L0_gnn_W1_0, L0_gnn_b1_0, L0_gnn_W0_1, L0_gnn_b0_1, L0_gnn_W1_1, L0_gnn_b1_1, L0_mix_Wq, L0_mix_bq, L0_mix_Wk, L0_mix_bk, L0_mix_Wv, L0_mix_bv, L0_mix_Wfc, L0_mix_bfc, L0_ffn_Wg, L0_ffn_bg, L0_ffn_bias, L0_ffn_W1, L0_ffn_b1, L0_ffn_W2, L0_ffn_b2):
    import jax
    import jax.numpy as jnp

    def _L0_gnn_ref(vert_features, edges, W0_0, b0_0, W1_0, b1_0, W0_1, b0_1, W1_1, b1_1):
        import jax, jax.numpy as jnp
        import numpy as np
        N_NODES = 6250

        def _graph_conv(x, edges, W0, b0, W1, b1):
            src = jnp.concatenate([edges[:, 0], edges[:, 1]])
            dst = jnp.concatenate([edges[:, 1], edges[:, 0]])
            deg = jax.ops.segment_sum(jnp.ones_like(dst, dtype=x.dtype), dst, num_segments=N_NODES)
            deg = jnp.maximum(deg, 1.0)
            agg = jax.ops.segment_sum(x[src], dst, num_segments=N_NODES) / deg[:, None]
            return x @ W0 + b0 + agg @ W1 + b1
        x = _graph_conv(vert_features, edges, W0_0, b0_0, W1_0, b1_0)
        x = jax.nn.relu(x)
        x = _graph_conv(x, edges, W0_1, b0_1, W1_1, b1_1)
        return x

    def _L0_mix_ref(x, Wq, bq, Wk, bk, Wv, bv, Wfc, bfc):
        import jax, jax.numpy as jnp
        import numpy as np
        B, L, D, H = (4, 2048, 256, 8)
        DK = D // H

        def _heads(t):
            b, l, d = t.shape
            return t.reshape(b, l, H, DK).transpose(0, 2, 1, 3)
        q = _heads(x @ Wq.T + bq)
        k = _heads(x @ Wk.T + bk)
        v = _heads(x @ Wv.T + bv)
        seq_len = q.shape[-2]
        p_attn = jnp.einsum('bhnd,bhne->bhde', k, v) / seq_len
        out = jnp.einsum('bhnd,bhde->bhne', q, p_attn)
        out = out.transpose(0, 2, 1, 3).reshape(x.shape[0], seq_len, H * DK)
        return out @ Wfc.T + bfc

    def _L0_ffn_ref(x, Wg, bg, bias, W1, b1, W2, b2):
        import jax, jax.numpy as jnp
        import numpy as np
        D_MODEL = 256
        EXPERT_DIM = 512
        NUM_EXPERTS = 8
        TOP_K = 2
        SEQ_LEN = 256
        BATCH = 2
        x_flat = x.reshape(-1, D_MODEL)
        gate_logits = x_flat @ Wg + bg + bias
        topk_vals, topk_idx = jax.lax.top_k(gate_logits, TOP_K)
        topk_w = jax.nn.softmax(topk_vals, axis=-1)
        combine = (jax.nn.one_hot(topk_idx, NUM_EXPERTS, dtype=x.dtype) * topk_w[..., None]).sum(axis=1)
        h = jax.nn.relu(jnp.einsum('td,edh->teh', x_flat, W1) + b1)
        y = jnp.einsum('teh,ehd->ted', h, W2) + b2
        out = jnp.einsum('ted,te->td', y, combine)
        return out.reshape(x.shape)
    edge_index_t = jnp.stack([src, dst], axis=1)
    xn = _layernorm(x, axis=-1)
    x = x + _L0_gnn_ref(xn, edge_index_t, L0_gnn_W0_0, L0_gnn_b0_0, L0_gnn_W1_0, L0_gnn_b1_0, L0_gnn_W0_1, L0_gnn_b0_1, L0_gnn_W1_1, L0_gnn_b1_1) + _L0_mix_ref(xn[None], L0_mix_Wq, L0_mix_bq, L0_mix_Wk, L0_mix_bk, L0_mix_Wv, L0_mix_bv, L0_mix_Wfc, L0_mix_bfc)[0]
    x = x + _L0_ffn_ref(_layernorm(x, axis=-1)[None], L0_ffn_Wg, L0_ffn_bg, L0_ffn_bias, L0_ffn_W1, L0_ffn_b1, L0_ffn_W2, L0_ffn_b2)[0]
    return x

_drawn_inputs = setup_inputs


def setup_inputs(seed=0):
    import zlib

    import numpy as np

    out = dict(_drawn_inputs(seed))
    spreads = {'L0_gnn_b0_0': (0.0, 0.8),
     'L0_gnn_b1_0': (0.0, 0.8),
     'L0_gnn_b0_1': (0.0, 0.8),
     'L0_gnn_b1_1': (0.0, 2.0),
     'L0_mix_bq': (0.0, 0.8),
     'L0_mix_bk': (0.0, 0.8),
     'L0_mix_bv': (0.0, 0.8),
     'L0_mix_bfc': (0.0, 2.0),
     'L0_ffn_bias': (0.0, 0.8)}
    factors = {'L0_mix_Wq': 8.0,
     'L0_mix_Wk': 8.0,
     'L0_mix_Wv': 8.0,
     'L0_mix_Wfc': 8.0,
     'L0_ffn_bg': 43.112,
     'L0_ffn_b1': 64.0,
     'L0_ffn_b2': 43.16,
     'L0_gnn_W0_0': 2.678,
     'L0_gnn_W1_0': 8.0,
     'L0_gnn_W1_1': 3.474,
     'L0_ffn_Wg': 8.0,
     'L0_ffn_W1': 8.0,
     'L0_ffn_W2': 8.0}
    for name, (base, spread) in spreads.items():
        noise = np.random.default_rng([zlib.crc32(name.encode()), seed]).standard_normal(out[name].shape)
        drawn = base * np.exp(spread * noise) if base else spread * noise
        out[name] = jnp.asarray(drawn.astype(out[name].dtype))
    for name, factor in factors.items():
        out[name] = (out[name] * factor).astype(out[name].dtype)
    return out
```

```python
import concourse.bass as bass
from concourse import mybir
from contextlib import ExitStack

F32, F16, I32 = mybir.dt.float32, mybir.dt.float16, mybir.dt.int32
U32 = mybir.dt.uint32
ALU, ACT, AX = mybir.AluOpType, mybir.ActivationFunctionType, mybir.AxisListType

P = 128
N, D, F, EXPERTS, HEADS = 6250, 256, 512, 8, 8
EDGES = 106250
T = -(-N // P)
LAST = N - (T - 1) * P
E = 832
EP = E + 8
G = 8
GROUPS = E // G
LASTE = EDGES - (P - 1) * E
PADNODE = 8191
BINS = T * T
COLS = BINS + T
TRASH = P * COLS
SLOTS = TRASH + P * EP
TC = T + 3
QB = 4
Q = TC // QB
LEAD = 3
S = 2048.0
W = 7
HALF = ((0, 4), (4, 3))
OVROW = T * P
EPS = 1e-5


def gps_layer(nc, io):
    ctx = ExitStack()
    with ctx:
        ctx.enter_context(nc.allow_non_contiguous_dma(reason="bias columns"))

        def sb(name, shape, dt=F32):
            return ctx.enter_context(nc.sbuf_tensor(name, shape, dt))

        def sem(name):
            return ctx.enter_context(nc.semaphore(name))

        slots_dram = nc.dram_tensor("slots_dram", [SLOTS, 1], I32).ap()
        feat_dram = nc.dram_tensor("feat_dram", [(T + 1) * P, 2 * D], F16).ap()
        sum_dram = nc.dram_tensor("sum_dram", [(T + 2) * P, 2 * D], F32).ap()
        ends_dram = nc.dram_tensor("ends_dram", [2, P, EP], I32).ap()
        xT_dram = nc.dram_tensor("xT_dram", [T // W, P, W * D], F32).ap()

        R2 = sb("R2", [P, T * 2 * D], F16)
        R3 = sb("R3", [P, T * D])
        R2f = R2[:, :].bitcast(F32)
        R3i = R3[:, :].bitcast(I32)
        R3h = R3[:, :].bitcast(F16)

        def words(i):
            return slice(i * EP, (i + 1) * EP)

        eS, eD = R3i[:, words(0)], R3i[:, words(1)]
        eHi, eLo = R3i[:, words(2)], R3i[:, words(3)]
        eTi, eTj = R3i[:, words(4)], R3i[:, words(5)]
        rank, posI = R3[:, words(4)], R3i[:, words(5)]
        rec = R3i[:, words(6)]
        binb, diag = R3[:, words(7)], R3[:, words(8)]
        delta = R3[:, words(9)]
        inval = R3[:, words(10)]
        half0 = 11 * EP * 2
        fTi, fTj, fHi, fLo = (R3h[:, half0 + i * EP:half0 + (i + 1) * EP] for i in range(4))
        assert half0 + 4 * EP <= 2 * T * D

        trash = sb("trash", [P, EP], I32)
        TT = sb("TT", [P, (T + 1) * TC], F16)
        TU = sb("TU", [P, (T + 1) * TC], F16)
        iota128 = sb("iota128", [P, P, G], F16)
        iota49 = sb("iota49", [P, T, G], F16)
        iotaB = sb("iotaB", [P, P, QB], F16)
        ident16 = sb("ident16", [P, P], F16)
        ident = sb("ident", [P, P])
        zeros16 = sb("zeros16", [P, P], F16)
        neg4 = sb("neg4", [P, 4, P], F16)
        ones = sb("ones", [P, P])
        epsc = sb("epsc", [P, 1])
        W0s = sb("W0s", [P, 2, F])
        W1s = sb("W1s", [P, 2, F])
        Wc = sb("Wc", [P, 4, 2 * D])
        bh = sb("bh", [P, 2, 4])
        bhs = sb("bhs", [P, 4])
        zb = sb("zb", [P, D])
        Ms = sb("Ms", [P, 2, D])
        deg = sb("deg", [P, T])
        rdeg = sb("rdeg", [P, T])
        rd1 = sb("rd1", [P, T])
        rd2 = sb("rd2", [P, T])
        stats = sb("stats", [P, W, 6])
        iota8 = sb("iota8", [P, 8])
        zeros32 = sb("zeros32", [P, D])
        cred = sb("cred", [P, 2])
        zrow = sb("zrow", [P, 1])
        flag = sb("flag", [P, 1], I32)
        pwait = sb("pwait", [P, 1])
        mv = sb("mv", [P, T, 2])
        rstd = sb("rstd", [P, T])
        small = sb("small", [P, 64])
        smalli = small[:, :].bitcast(I32)
        BIG = 17330
        big = sb("big", [P, BIG])
        bigh = big[:, :].bitcast(F16)
        bigi = big[:, :].bitcast(I32)

        def BB(q):
            return q % 4 if q < 12 else 4

        def Y4(i):
            return 4 + (i % 3 if i < 6 else 3)

        BUF5 = (0, 1, 0, 1, 0, 1, 2)

        banks = [ctx.enter_context(nc.psum_tensor(f"bank{i}", [P, 512], F32)) for i in range(8)]

        bank0h = banks[0][:, :].bitcast(F16)

        class Space:
            def __init__(self, at=0):
                self.at = at

            def f32(self, *shape):
                n = 1
                for s in shape:
                    n *= s
                ap = big[:, self.at:self.at + n]
                self.at += n
                assert self.at <= BIG, self.at
                return ap

            def f16(self, *shape):
                n = 1
                for s in shape:
                    n *= s
                ap = bigh[:, 2 * self.at:2 * self.at + n]
                self.at += -(-n // 2)
                assert self.at <= BIG, self.at
                return ap

            def i32(self, *shape):
                n = 1
                for s in shape:
                    n *= s
                ap = bigi[:, self.at:self.at + n]
                self.at += n
                assert self.at <= BIG, self.at
                return ap

        sp1 = Space()
        OHi = [sp1.f16(T * G).rearrange("p (m g) -> p m g", g=G) for _ in range(2)]
        OHj = [sp1.f16(T * G).rearrange("p (m g) -> p m g", g=G) for _ in range(2)]
        at_L = sp1.at
        LHi = [sp1.f16(P * G).rearrange("p (m g) -> p m g", g=G) for _ in range(2)]
        LLo = [sp1.f16(P * G).rearrange("p (m g) -> p m g", g=G) for _ in range(2)]
        at_T = sp1.at
        OHiT = [sp1.f16(G * P) for _ in range(2)]
        sqs = big[:, at_T:at_T + 1024]
        Mm = [sp1.f16(G * P).rearrange("p (g e) -> p g e", g=G) for _ in range(2)]
        Tsn = [sp1.f16((G + 1) * T).rearrange("p (g j) -> p g j", j=T) for _ in range(2)]
        prod = sp1.f32(G * T).rearrange("p (g j) -> p g j", j=T)
        d1 = sp1.f32(G)
        rr = sp1.f32(G)
        ee = sp1.f32(G)
        bb = sp1.f32(G)
        pp = sp1.f32(G)
        ov = sp1.f32(G)
        tq = sp1.f32(G)
        tr = sp1.f32(G)
        stP = [sb(f"stP{i}", [P, G], I32) for i in range(2)]
        stR = [sb(f"stR{i}", [P, G], I32) for i in range(2)]
        xs = [sp1.f32(D + 1) for _ in range(W)]
        xlo = [sp1.f32(D) for _ in range(2)]
        Gs = sp1.f32(2 * (D + 1)).rearrange("p (k n) -> p k n", k=2)
        Wq, Wk, Wv, Wfc = (sp1.f32(2 * D).rearrange("p (k n) -> p k n", k=2) for _ in range(4))
        hmask = sp1.f32(2 * D).rearrange("p (k n) -> p k n", k=2)
        xin = sp1.f32(W * D)
        xst = sp1.f32(W * D)
        sp2 = Space(at_L)
        WkT, WvT, B1s, PTs = (sp2.f32(2 * D).rearrange("p (k n) -> p k n", k=2) for _ in range(4))
        assert sp2.at <= at_T
        sp2 = Space(at_T + 1024)
        WfT, Rs = (sp2.f32(2 * D).rearrange("p (k n) -> p k n", k=2) for _ in range(2))
        bqc = sp1.f32(2)
        rows = sp1.f32(9 * D).rearrange("p (r n) -> p r n", r=9)
        BK, BV, BFC, B01, B11, SV, SK, ZB, SPARE = range(9)
        degT = sp1.f32(P)

        sp3 = Space()
        slotI = sp3.i32(COLS)
        hiI = sp3.i32(COLS)
        HI = sp3.f16(COLS)
        LO = sp3.f16(COLS)
        sp3b = Space()
        OT = [sp3b.f16(P * QB).rearrange("p (m b) -> p m b", b=QB) for _ in range(Q)]
        OU = [sp3b.f16(P * QB).rearrange("p (m b) -> p m b", b=QB) for _ in range(Q)]
        Ab = [sp3b.f16(QB * P) for _ in range(Q)]
        aggr = sp3b.f32(2 * D)
        aggc = sp3b.f32(D)
        aggn = sp3b.f32(D)
        xres = sp3b.f32(D)
        spo = Space(sp3b.at)
        oX = spo.f16(2 * D)
        oA = spo.f32(2 * D)
        oN = spo.f32(2 * D)
        oSel = spo.f16(P)
        oB = spo.f32(P)
        oM = spo.f32(P)
        oa, ob, ow = (spo.i32(1) for _ in range(3))
        obf, oc, od, oe = (spo.f32(1) for _ in range(4))
        sp4 = Space()
        hT = sp4.f32(4 * W * P).rearrange("p (f n) -> p f n", f=4)
        xT4 = [sp4.f32(W * D) for _ in range(2)]
        ylo = [sp4.f32(D) for _ in range(2)]
        sp5 = Space()
        x2n = [sp5.f32(D) for _ in range(3)]
        x2T = sp5.f32(W * D).rearrange("p (t k n) -> p t k n", t=W, k=2)
        h5 = [sp5.f32(4 * W * P).rearrange("p (f n) -> p f n", f=4) for _ in range(2)]
        acc = sp5.f32(W * D).rearrange("p (t n) -> p t n", t=W)
        Wgs = sp5.f32(2 * 8).rearrange("p (k n) -> p k n", k=2)
        gb = sp5.f32(8)
        grows = sp5.f32(3 * 8).rearrange("p (r n) -> p r n", r=3)
        b1c = sp5.f32(EXPERTS * 4).rearrange("p (e f) -> p e f", e=EXPERTS)
        b2s = sp5.f32(D)
        lg = sp5.f32(W * 8).rearrange("p (t n) -> p t n", t=W)
        mx = sp5.f32(W * 8).rearrange("p (t n) -> p t n", t=W)
        mi = sp5.i32(W * 8).bitcast(U32).rearrange("p (t n) -> p t n", t=W)
        mif = sp5.f32(W * 2).rearrange("p (t n) -> p t n", t=W)
        gw = sp5.f32(W * 4).rearrange("p (t n) -> p t n", t=W)
        c0 = sp5.f32(W * 8).rearrange("p (t n) -> p t n", t=W)
        c1 = sp5.f32(W * 8).rearrange("p (t n) -> p t n", t=W)
        comb = sp5.f32(W * 8).rearrange("p (t n) -> p t n", t=W)
        combT = sp5.f32(W * P).rearrange("p (t n) -> p t n", t=W)
        R2k = [R2f[:, 4 * D * i:4 * D * (i + 1)] for i in range(12)]
        W1e = [(R2k[8 + e] if e < 4 else sp5.f32(2 * F)).rearrange("p (k n) -> p k n", k=2) for e in range(EXPERTS)]
        W2e = [R2k[e].rearrange("p (k n) -> p k n", k=4) for e in range(EXPERTS)]

        slotZ = R2[:, 0:2 * COLS].bitcast(I32)

        s_const = sem("s_const")
        s_blank = sem("s_blank")
        s_edges = sem("s_edges")
        s_zero = sem("s_zero")
        s_table = sem("s_table")
        s_x = sem("s_x")
        s_w = sem("s_w")
        s_keys = sem("s_keys")
        s_oh = sem("s_oh")
        s_tp = sem("s_tp")
        s_ot = sem("s_ot")
        s_eq = sem("s_eq")
        s_h = sem("s_h")
        s_m = sem("s_m")
        s_t = sem("s_t")
        s_r = sem("s_r")
        s_rk = sem("s_rk")
        s_pos = sem("s_pos")
        s_stage = sem("s_stage")
        s_sc = [sem("s_sc0"), sem("s_sc1")]

        s_stat = sem("s_stat")
        s_std = sem("s_std")
        s_xn = sem("s_xn")
        s_xhi = sem("s_xhi")
        s_xl = sem("s_xl")
        s_xlo = sem("s_xlo")
        s_xt = sem("s_xt")
        s_xtc = sem("s_xtc")
        s_pm = sem("s_pm")
        s_vm = sem("s_vm")

        s_slot = sem("s_slot")
        s_tabs = sem("s_tabs")
        s_r3 = sem("s_r3")
        s_flag = sem("s_flag")
        s_fp = sem("s_fp")
        s_ends = sem("s_ends")
        s_of = [sem(f"s_of{i}") for i in range(2)]
        s_oi = [sem(f"s_oi{i}") for i in range(2)]
        s_oj = [sem(f"s_oj{i}") for i in range(2)]
        s_ox = [sem(f"s_ox{i}") for i in range(2)]
        s_oy = [sem(f"s_oy{i}") for i in range(2)]
        s_os = [sem(f"s_os{i}") for i in range(2)]
        s_ol = [sem(f"s_ol{i}") for i in range(2)]
        s_o1 = [sem(f"s_o1{i}") for i in range(2)]
        s_o2 = [sem(f"s_o2{i}") for i in range(2)]
        s_o3 = [sem(f"s_o3{i}") for i in range(2)]
        s_o4 = [sem(f"s_o4{i}") for i in range(2)]
        s_o5v = [sem(f"s_o5{i}") for i in range(2)]
        s_o6 = [sem(f"s_o6{i}") for i in range(2)]
        s_oo = [sem(f"s_oo{i}") for i in range(2)]
        s_bl = [sem(f"s_bl{i}") for i in range(2)]
        s_ab = [sem(f"s_ab{i}") for i in range(2)]
        s_ap = [sem(f"s_ap{i}") for i in range(2)]
        s_ag = [sem(f"s_ag{i}") for i in range(2)]
        s_an = [sem(f"s_an{i}") for i in range(2)]
        s_at = sem("s_at")
        s_ac = sem("s_ac")
        s_xr = sem("s_xr")
        s_xrf = sem("s_xrf")

        s_x4 = [sem(f"s_x4{i}") for i in range(2)]
        s_xT = sem("s_xT")
        s_xp = sem("s_xp")
        s_sq = sem("s_sq")
        s_sp = sem("s_sp")
        s_sr = sem("s_sr")
        s_sc2 = sem("s_sc2")
        s_hp = sem("s_hp")
        s_hr = sem("s_hr")
        s_yp = sem("s_yp")
        s_yh = sem("s_yh")
        s_zc = sem("s_zc")
        s_yl = sem("s_yl")

        s_we = [sem(f"s_we{e}") for e in range(EXPERTS)]
        s_wg = sem("s_wg")
        s_gv = sem("s_gv")
        s_gp = sem("s_gp")
        s_v2 = sem("s_v2")
        s_d2 = sem("s_d2")
        s_n2 = sem("s_n2")
        s_t2 = sem("s_t2")
        s_c2 = sem("s_c2")
        s_lp = sem("s_lp")
        s_lv = sem("s_lv")
        s_le = sem("s_le")
        s_cb = sem("s_cb")
        s_ct = sem("s_ct")
        s_cc = sem("s_cc")
        s_bp = sem("s_bp")
        s_ai = sem("s_ai")
        s_up = sem("s_up")
        s_ur = sem("s_ur")
        s_dp = sem("s_dp")
        s_da = sem("s_da")
        s_st = sem("s_st")
        s_o5 = sem("s_o5")
        s_gpc = sem("s_gpc")

        block = ctx.enter_context(nc.Block())

        @block.sync
        def _(sp):
            sp.wait_ge(s_blank, 1)
            for end, arr in (("src", eS), ("dst", eD)):
                v = io[end][0:(P - 1) * E].rearrange("(p c) -> p c", c=E)
                sp.dma_start(arr[0:112, 0:E], v[0:112, :]).then_inc(s_edges, 16)
                sp.dma_start(arr[112:127, 0:E], v[112:127, :]).then_inc(s_edges, 16)
                sp.dma_start(arr[127:128, 0:LASTE],
                             io[end][(P - 1) * E:EDGES].rearrange("(a n) -> a n", a=1)).then_inc(s_edges, 16)
            sp.wait_ge(s_zero, 1)
            sp.dma_start(slots_dram[0:TRASH, :].rearrange("(p c) a -> p (c a)", p=P),
                         slotZ[:, :]).then_inc(s_table, 16)
            for name, dst in (("L0_mix_Wq", Wq), ("L0_mix_Wk", Wk), ("L0_mix_Wv", Wv), ("L0_mix_Wfc", Wfc),
                              ("L0_gnn_W0_0", W0s[:, :, :]), ("L0_gnn_W1_0", W1s[:, :, :]),
                              ("L0_gnn_W1_1", Wc[:, :, 0:D]), ("L0_gnn_W0_1", Wc[:, :, D:2 * D])):
                sp.dma_start(dst, io[name].rearrange("(k p) n -> p k n", p=P)).then_inc(s_w, 16)
            for name, r in (("L0_mix_bk", BK), ("L0_mix_bv", BV), ("L0_mix_bfc", BFC),
                            ("L0_gnn_b0_1", B01), ("L0_gnn_b1_1", B11)):
                sp.dma_start(rows[0:1, r, :], io[name].rearrange("(a n) -> a n", a=1)).then_inc(s_w, 16)
            sp.dma_start(bqc, io["L0_mix_bq"].rearrange("(k p) -> p k", p=P)).then_inc(s_w, 16)
            sp.dma_start(bh[:, 0, :], io["L0_gnn_b0_0"].rearrange("(k p) -> p k", p=P)).then_inc(s_w, 16)
            sp.dma_start(bh[:, 1, :], io["L0_gnn_b1_0"].rearrange("(k p) -> p k", p=P)).then_inc(s_w, 16)
            xv = io["x"][0:(T - 1) * P, :].rearrange("(t p) c -> p t c", p=P)
            xiv = xin.rearrange("p (t c) -> p t c", c=D)
            sp.dma_start(rows[0:1, 8, 0:D], io["L0_mix_bk"].rearrange("(a n) -> a n", a=1)).then_inc(s_xT, 16)
            sp.dma_start(xiv, xv[:, 0:W, :]).then_inc(s_x, 16)
            with sp.Fori(1, T // W - 1) as b:
                sp.wait_ge(s_xn, b * W)
                sp.dma_start(xiv, io["x"][bass.ds(b * (W * P), W * P), :].rearrange("(t p) c -> p t c", p=P))\
                  .then_inc(s_x, 16)
                sp.wait_ge(s_xp, b)
                sp.dma_start(xT_dram[bass.ds(b - 1, 1), :, :].rearrange("a p c -> (a p) c"), xst).then_inc(s_xT, 16)
            sp.wait_ge(s_xn, T - W)
            sp.dma_start(xiv[:, 0:W - 1, :], xv[:, T - W:T - 1, :]).then_inc(s_x, 16)
            sp.dma_start(xiv[0:LAST, W - 1, :], io["x"][(T - 1) * P:N, :]).then_inc(s_x, 16)
            sp.dma_start(xiv[LAST:P, W - 1, :], zeros32[LAST:P, :]).then_inc(s_x, 16)
            for b in (T // W - 2, T // W - 1):
                sp.wait_ge(s_xp, b + 1)
                sp.dma_start(xT_dram[b, :, :], xst).then_inc(s_xT, 16)
            sp.wait_ge(s_sc[0], 16 * G * (GROUPS // 2))
            sp.wait_ge(s_sc[1], 16 * G * (GROUPS // 2))
            sp.wait_ge(s_vm, 12)
            sp.wait_ge(s_pm, 10)
            sp.wait_ge(s_sr, 1)
            sp.wait_ge(s_xT, 16 + 16 * (T // W))
            sp.dma_start(slotI, slots_dram[0:TRASH, :].rearrange("(p c) a -> p (c a)", p=P)).then_inc(s_slot, 16)
            def load4(g, par):
                sp.dma_start(xT4[par], xT_dram[bass.ds(g, 1), :, :].rearrange("a p c -> (a p) c")).then_inc(s_x4[par], 16)

            sp.wait_ge(s_ac, 1 + T)
            load4(0, 0)
            load4(1, 1)
            with sp.Fori(1, T // W // 2) as k:
                for par in range(2):
                    sp.wait_ge(s_yp, k * (2 * W) + par * W)
                    load4(2 * k + par, par)
            sp.wait_ge(s_yp, T - W)
            load4(T // W - 1, 0)
            sp.wait_ge(s_yp, W + T)
            with sp.Fori(0, T - 1) as t:
                sp.wait_ge(s_xrf, t + 1)
                sp.dma_start(xres, io["x"][bass.ds(t * P, P), :]).then_inc(s_xr, 16)
            sp.wait_ge(s_xrf, T)
            sp.dma_start(xres[0:LAST, :], io["x"][(T - 1) * P:N, :]).then_inc(s_xr, 16)
            sp.wait_ge(s_ap[1], Q + T * Q)
            sp.wait_ge(s_xrf, T + 1)
            sp.dma_start(Wgs, io["L0_ffn_Wg"].rearrange("(k p) n -> p k n", p=P)).then_inc(s_wg, 16)
            sp.dma_start(grows[0:1, 0, :], io["L0_ffn_bg"].rearrange("(a n) -> a n", a=1)).then_inc(s_wg, 16)
            sp.dma_start(grows[0:1, 1, :], io["L0_ffn_bias"].rearrange("(a n) -> a n", a=1)).then_inc(s_wg, 16)
            for e in range(EXPERTS):
                sp.dma_start(b1c[:, e, :], io["L0_ffn_b1"][e, :].rearrange("(f p) -> p f", p=P)).then_inc(s_wg, 16)
            sp.dma_start(b2s[0:EXPERTS, :], io["L0_ffn_b2"]).then_inc(s_st, 16)
            for e in range(EXPERTS):
                sp.dma_start(W1e[e], io["L0_ffn_W1"][e, :, :].rearrange("(k p) n -> p k n", p=P)).then_inc(s_we[e], 16)
                sp.dma_start(W2e[e], io["L0_ffn_W2"][e, :, :].rearrange("(k p) n -> p k n", p=P)).then_inc(s_we[e], 16)
            with sp.Fori(0, T // W - 1) as g:
                sp.wait_ge(s_da, 2 + 32 * (g + 1))
                sp.dma_start(io["out"][bass.ds(g * (W * P), W * P), :].rearrange("(t p) c -> p t c", p=P),
                             acc).then_inc(s_st, 16)
            sp.wait_ge(s_da, 2 + 32 * (T // W))
            sp.dma_start(io["out"][(T - W) * P:(T - 1) * P, :].rearrange("(t p) c -> p t c", p=P),
                         acc[:, 0:W - 1, :]).then_inc(s_o5, 16)
            sp.dma_start(io["out"][(T - 1) * P:N, :], acc[0:LAST, W - 1, :]).then_inc(s_o5, 16)
            sp.wait_ge(s_st, 16 * (T // W))
            sp.wait_ge(s_o5, 32)

        @block.gpsimd
        def _(pool):
            allow = dict(allow_small_or_imprecise_dtypes=True)
            nc.gpsimd.iota(iota128[:, :, :], [[1, P], [0, G]], base=0, channel_multiplier=0, **allow)
            nc.gpsimd.iota(iota49[:, :, :], [[1, T], [0, G]], base=0, channel_multiplier=0, **allow)
            nc.gpsimd.iota(iotaB[:, :, :], [[1, P], [0, QB]], base=1, channel_multiplier=0, **allow)
            nc.gpsimd.iota(trash[:, :], [[1, EP]], base=TRASH, channel_multiplier=EP)
            nc.gpsimd.iota(iota8[:, :], [[1, 8]], base=0, channel_multiplier=0, **allow)
            nc.gpsimd.iota(zrow[:, :], [[0, 1]], base=OVROW, channel_multiplier=1, **allow)
            nc.gpsimd.memset(zeros32[:, :], 0.0)
            nc.gpsimd.memset(zeros16[:, :], 0.0)
            nc.gpsimd.memset(ident[:, :], 0.0)
            nc.gpsimd.memset(ident16[:, :], 0.0)
            nc.gpsimd.memset(ones[:, :], 1.0)
            nc.gpsimd.memset(epsc[:, :], EPS)
            nc.gpsimd.memset(neg4[:, :, :], -1.0)
            nc.gpsimd.memset(hmask, 1.0)
            pool.drain()
            for m in (ident, ident16):
                nc.gpsimd.affine_select(out=m[:, :], in_=m[:, :], compare_op=ALU.not_equal, fill=1.0,
                                        base=0, pattern=[[-1, P]], channel_multiplier=1)
            nc.gpsimd.affine_select(out=neg4[:, :, :], in_=neg4[:, :, :], compare_op=ALU.is_ge, fill=0.0,
                                    base=0, pattern=[[0, 4], [-1, P]], channel_multiplier=1)
            hv = hmask.rearrange("p k (b c) -> p k b c", c=D // HEADS)
            nc.gpsimd.affine_select(out=hv, in_=hv, compare_op=ALU.is_ge, fill=0.0, base=0,
                                    pattern=[[P, 2], [-(D // HEADS), HEADS], [0, D // HEADS]], channel_multiplier=1)
            pool.drain()
            nc.gpsimd.affine_select(out=hv, in_=hv, compare_op=ALU.is_ge, fill=0.0, base=D // HEADS - 1,
                                    pattern=[[-P, 2], [D // HEADS, HEADS], [0, D // HEADS]],
                                    channel_multiplier=-1).then_inc(s_const, 1)
            pool.wait_ge(s_table, 16)

            def scatter(k, par, first):
                g = 2 * k + par
                pool.wait_ge(s_pos, g + 1)
                if not first:
                    pool.wait_ge(s_sc[par], 16 * G * k)
                nc.gpsimd.tensor_copy(stP[par][:, :], posI[:, bass.ds(g * G, G)])
                nc.gpsimd.tensor_copy(stR[par][:, :], rec[:, bass.ds(g * G, G)]).then_inc(s_stage, 1)
                pool.wait_ge(s_stage, g + 1)
                nc.gpsimd.tensor_tensor(pwait[:, 0:1], ones[:, 0:1], ones[:, 0:1], ALU.add)
                for c in range(G):
                    pool.indirect_dma_start(
                        out=slots_dram, out_offset=bass.IndirectOffsetOnAxis(ap=stP[par][:, c:c + 1], axis=0),
                        in_=stR[par][:, c:c + 1], in_offset=None).then_inc(s_sc[par], 16)

            scatter(0, 0, True)
            scatter(0, 1, True)
            with pool.Fori(1, GROUPS // 2) as k:
                scatter(k, 0, False)
                scatter(k, 1, False)
            pool.wait_ge(s_flag, 2)
            for i, ends in enumerate((eS, eD)):
                pool.dma_start(ends_dram[i, :, :], ends).then_inc(s_ends, 16)
            pool.wait_ge(s_ends, 32)
            nc.gpsimd.memset(R3[:, :], 0.0).then_inc(s_r3, 1)

            def wait(s, n):
                pool.drain()
                pool.wait_ge(s, n)
                nc.gpsimd.tensor_tensor(pwait[:, 0:1], ones[:, 0:1], ones[:, 0:1], ALU.add)

            def overflow(L):
                pool.dma_start(feat_dram[0:T * P, :].rearrange("(t p) c -> p t c", p=P),
                               R2[:, :].rearrange("p (t c) -> p t c", t=T)).then_inc(s_of[L], 16)
                pool.dma_start(feat_dram[T * P:(T + 1) * P, :], zeros32[:, :].bitcast(F16)).then_inc(s_of[L], 16)
                for i in range(2):
                    pool.dma_start(sum_dram[:, i * D:(i + 1) * D].rearrange("(t p) c -> p t c", p=P),
                                   zeros32[:, :].rearrange("p (a c) -> p a c", a=1).to_broadcast([P, T + 2, D]))\
                        .then_inc(s_of[L], 16)
                wait(s_of[L], 64)
                with pool.Fori(0, E) as c:
                    for i in range(2):
                        m = 2 * c + i
                        pool.dma_start(oa, ends_dram[i, :, bass.ds(c, 1)]).then_inc(s_oi[L], 16)
                        pool.dma_start(ob, ends_dram[1 - i, :, bass.ds(c, 1)]).then_inc(s_oj[L], 16)
                        wait(s_oi[L], m * 16 + 16)
                        wait(s_oj[L], m * 16 + 16)
                        pool.indirect_dma_start(out=oX, out_offset=None, in_=feat_dram,
                                                in_offset=bass.IndirectOffsetOnAxis(ap=oa, axis=0)).then_inc(s_ox[L], 16)
                        pool.indirect_dma_start(out=oA, out_offset=None, in_=sum_dram,
                                                in_offset=bass.IndirectOffsetOnAxis(ap=ob, axis=0)).then_inc(s_oy[L], 16)
                        wait(s_o5v[L], m + 1)
                        pool.indirect_dma_start(out=sum_dram, out_offset=bass.IndirectOffsetOnAxis(ap=ow, axis=0),
                                                in_=oN, in_offset=None).then_inc(s_os[L], 16)
                        wait(s_os[L], m * 16 + 16)
                with pool.Fori(0, T) as t:
                    pool.dma_start(oA, sum_dram[bass.ds(t * P, P), :]).then_inc(s_ol[L], 16)
                    wait(s_o6[L], t + 1)

            lacking = pool.value_load(flag[0:1, 0:1])
            pool.wait_ge(s_xlo, 1 + T)
            pool.wait_ge(s_tabs, 1)
            with pool.If(lacking > 0):
                overflow(0)
            pool.wait_ge(s_yl, 1 + T)
            pool.wait_ge(s_zc, 3 + T)
            with pool.If(lacking > 0):
                overflow(1)

        @block.vector
        def _(dve):
            v = nc.vector
            v.memset(R3i[:, 0:2 * EP], PADNODE)
            v.memset(Tsn[0], 0.0)
            v.memset(Tsn[1], 0.0).then_inc(s_blank, 1)
            v.memset(slotZ, 0).then_inc(s_zero, 1)
            v.memset(small[:, 0:1], 0.0).then_inc(s_t, 1)
            v.memset(small[:, 1:2], 0.0).then_inc(s_rk, 1)
            v.memset(small[:, 2:3], 0.0).then_inc(s_xtc, 1)
            v.memset(small[:, 3:4], 0.0).then_inc(s_ac, 1)
            v.memset(small[:, 4:5], 0.0).then_inc(s_an[0], 1)
            v.memset(small[:, 5:6], 0.0).then_inc(s_an[1], 1)
            v.memset(small[:, 6:7], 0.0).then_inc(s_zc, 3)
            v.memset(small[:, 7:8], 0.0).then_inc(s_xrf, 1)
            v.memset(small[:, 8:9], 0.0).then_inc(s_da, 2)
            dve.wait_ge(s_edges, 96)
            v.tensor_tensor(eHi, eS, eD, ALU.max)
            v.tensor_tensor(eLo, eS, eD, ALU.min)
            dve.drain()
            v.tensor_scalar(eTi, eHi, 7, None, ALU.logical_shift_right)
            v.tensor_scalar(eTj, eLo, 7, None, ALU.logical_shift_right)
            dve.drain()
            v.tensor_scalar(eHi, eHi, P - 1, None, ALU.bitwise_and)
            v.tensor_scalar(eLo, eLo, P - 1, None, ALU.bitwise_and)
            v.tensor_copy(fTi, eTi)
            v.tensor_copy(fTj, eTj)
            dve.drain()
            v.tensor_copy(fHi, eHi)
            v.tensor_copy(fLo, eLo)
            v.scalar_tensor_tensor(out=rec, in0=eHi, scalar=256.0, in1=eLo, op0=ALU.mult, op1=ALU.add)
            v.scalar_tensor_tensor(out=binb, in0=eTi, scalar=float(T), in1=eTj, op0=ALU.mult, op1=ALU.add)
            v.tensor_tensor(diag, eTi, eTj, ALU.is_equal)
            v.tensor_scalar(delta, eTi, -float(T), float(BINS), ALU.mult, ALU.add)
            v.tensor_scalar(inval, eTi, float(T), None, ALU.is_ge)
            dve.drain()
            v.tensor_scalar(rec, rec, 257.0, None, ALU.add)
            dve.drain()
            dve.wait_ge(s_const, 1)

            def onehots(par, g):
                dve.wait_ge(s_r, g + 1)
                for out, key, pat, m in ((OHi, fTi, iota49, T), (OHj, fTj, iota49, T),
                                         (LHi, fHi, iota128, P), (LLo, fLo, iota128, P)):
                    kb = key[:, bass.ds(g * G, G)].rearrange("p (a b) -> p a b", a=1).to_broadcast([P, m, G])
                    last = v.tensor_tensor(out[par], pat[:, :, :], kb, ALU.is_equal)
                last.then_inc(s_oh, 1)

            def counts(par, g):
                dve.wait_ge(s_h, g + 1)
                v.tensor_copy(Tsn[par][0:T, 0, :], Tsn[1 - par][0:T, G, :])
                t0 = Tsn[1 - par][0:T, G, :].rearrange("p (a j) -> p a j", a=1).to_broadcast([T, G, T])
                v.scalar_tensor_tensor(out=Tsn[par][0:T, 1:G + 1, :], in0=t0, scalar=1024.0,
                                       in1=banks[3][0:T, 0:G * T].rearrange("p (g j) -> p g j", j=T),
                                       op0=ALU.min, op1=ALU.add).then_inc(s_t, 1)

            def ranks(par, g):
                sl = bass.ds(g * G, G)
                dve.wait_ge(s_r, g + 3)
                v.tensor_tensor(prod, banks[4][:, 0:G * T].rearrange("p (g j) -> p g j", j=T),
                                OHj[par].rearrange("p j g -> p g j"), ALU.mult).then_inc(s_rk, 1)
                dve.drain()
                v.tensor_reduce(rank[:, sl], prod, AX.X, ALU.add)
                dve.drain()
                v.scalar_tensor_tensor(out=d1, in0=rank[:, sl], scalar=float(P), in1=diag[:, sl],
                                       op0=ALU.is_ge, op1=ALU.mult)
                dve.drain()
                v.scalar_tensor_tensor(out=rr, in0=d1, scalar=-float(P), in1=rank[:, sl],
                                       op0=ALU.mult, op1=ALU.add)
                v.tensor_tensor(ee, d1, delta[:, sl], ALU.mult)
                dve.drain()
                v.tensor_tensor(bb, ee, binb[:, sl], ALU.add)
                v.scalar_tensor_tensor(out=ov, in0=rr, scalar=float(P), in1=inval[:, sl],
                                       op0=ALU.is_ge, op1=ALU.max)
                dve.drain()
                v.tensor_copy(delta[:, sl], ov)
                v.scalar_tensor_tensor(out=pp, in0=rr, scalar=float(COLS), in1=bb, op0=ALU.mult, op1=ALU.add)
                dve.drain()
                v.scalar_tensor_tensor(out=tq, in0=pp, scalar=-1.0, in1=trash[:, sl], op0=ALU.mult, op1=ALU.add)
                dve.drain()
                v.tensor_tensor(tr, tq, ov, ALU.mult)
                dve.drain()
                v.tensor_tensor(posI[:, sl], tr, pp, ALU.add).then_inc(s_pos, 1)

            onehots(0, 0)
            with dve.Fori(0, GROUPS // 2) as k:
                for par in range(2):
                    g = 2 * k + par
                    onehots(1 - par, g + 1)
                    counts(par, g)
                    ranks(par, g)

            for i in range(W):
                v.memset(xs[i][:, D:D + 1], 1.0)

            def stats_of(b, need):
                dve.wait_ge(s_x, need)
                for i in range(W):
                    v.bn_stats(stats[:, i, :], xin[:, i * D:(i + 1) * D])
                dve.drain()
                for i in range(W):
                    v.bn_aggr(mv[:, i, :], stats[:, i, :])
                dve.drain()
                v.tensor_copy(rstd[:, 0:W], mv[:, 0:W, 1]).then_inc(s_stat, 1)
                dve.wait_ge(s_std, b + 1)
                v.reciprocal(rstd[:, 0:W], rstd[:, 0:W])
                dve.drain()
                dve.wait_ge(s_xT, 16 * b + 16)
                for i in range(W):
                    t = b * W + i
                    dve.wait_ge(s_xt, t + 1)
                    dve.wait_ge(s_xlo, t + 1)
                    v.tensor_scalar(xs[i][:, 0:D], xin[:, i * D:(i + 1) * D], mv[:, i, 0:1],
                                    rstd[:, i:i + 1], ALU.subtract, ALU.mult).then_inc(s_xn, 1)
                    dve.wait_ge(s_xhi, t + 1)
                    v.scalar_tensor_tensor(out=xlo[0], in0=xs[i][:, 0:D], scalar=S,
                                           in1=R2[:, bass.ds(t * 2 * D, D)],
                                           op0=ALU.mult, op1=ALU.subtract).then_inc(s_xl, 1)
                    dve.wait_ge(s_xt, t + 1 + W)
                    v.tensor_copy(xst[:, i * D:(i + 1) * D], banks[0][:, 0:D]).then_inc(s_xtc, 1)
                dve.drain()
                v.memset(small[:, 10:11], 0.0).then_inc(s_xp, 1)

            with dve.Fori(0, T // W - 1) as b:
                stats_of(b, 16 * b + 16)
            stats_of(T // W - 1, 16 * (T // W + 2))

            def copied(ins):
                ins.then_inc(s_vm, 1)

            def k2(ap):
                return ap.rearrange("p (k n) -> p k n", k=2)

            dve.wait_ge(s_pm, 1)
            v.tensor_copy(Gs[:, 0, :], banks[6][:, 0:D + 1])
            copied(v.tensor_copy(Gs[:, 1, :], banks[7][:, 0:D + 1]))
            for i, dst in enumerate((WkT, WvT, WfT)):
                dve.wait_ge(s_pm, 2 + i)
                copied(v.tensor_copy(dst, k2(banks[i][:, :])))
            dve.wait_ge(s_pm, 5)
            v.tensor_copy(B1s, k2(banks[3][:, :]))
            v.tensor_copy(rows[0:1, SV, :], banks[4][0:1, 0:D])
            copied(v.scalar_tensor_tensor(out=rows[0:1, SK, :], in0=rows[0:1, BK, :], scalar=float(N),
                                          in1=banks[4][0:1, D:2 * D], op0=ALU.mult, op1=ALU.add))
            dve.wait_ge(s_pm, 6)
            copied(v.scalar_tensor_tensor(out=PTs, in0=k2(banks[0][:, :]), scalar=1.0 / N, in1=hmask,
                                          op0=ALU.mult, op1=ALU.mult))
            dve.wait_ge(s_pm, 7)
            copied(v.tensor_copy(Rs, k2(banks[1][:, :])))
            dve.wait_ge(s_pm, 8)
            v.tensor_copy(Ms[:, :, :], k2(banks[2][:, :]))
            v.tensor_tensor(rows[0:1, ZB, :], banks[3][0:1, 0:D], rows[0:1, BFC, :], ALU.add)
            v.tensor_tensor(bhs[:, :], bh[:, 0, :], bh[:, 1, :], ALU.add)
            dve.drain()
            v.tensor_tensor(rows[0:1, SPARE, :], rows[0:1, ZB, :], rows[0:1, B01, :], ALU.add)
            dve.drain()
            copied(v.tensor_tensor(rows[0:1, ZB, :], rows[0:1, SPARE, :], rows[0:1, B11, :], ALU.add))
            dve.wait_ge(s_pm, 9)
            copied(v.tensor_copy(zb[:, :], banks[4][:, 0:D]))
            copied(v.tensor_copy(degT[0:T, :], banks[5][0:T, 0:P]))
            dve.wait_ge(s_pm, 10)
            v.tensor_scalar(deg[:, :], banks[1][:, 0:T], 1.0, None, ALU.max)
            dve.drain()
            copied(v.reciprocal(rdeg[:, :], deg[:, :]))
            dve.drain()
            copied(v.tensor_scalar(rd1[:, :], rdeg[:, :], 1.0 / S, None, ALU.mult))

            dve.wait_ge(s_sr, 1)
            v.tensor_tensor(small[:, 44:45], small[:, 40:41], small[:, 41:42], ALU.add)
            dve.drain()
            v.scalar_tensor_tensor(out=small[:, 45:46], in0=small[:, 44:45], scalar=float(D) ** 0.5,
                                   in1=small[:, 42:43], op0=ALU.mult, op1=ALU.add)
            dve.drain()
            v.tensor_tensor(small[:, 46:47], small[:, 45:46], small[:, 43:44], ALU.mult)
            dve.drain()
            v.tensor_scalar(small[:, 47:48], small[:, 46:47], 2.0 ** -100, 2.0 ** 120, ALU.max, ALU.min)
            dve.drain()
            v.tensor_scalar(smalli[:, 48:49], smalli[:, 47:48], 23, None, ALU.logical_shift_right)
            dve.drain()
            v.tensor_scalar(smalli[:, 49:50], smalli[:, 48:49], -1.0, 267.0, ALU.mult, ALU.add)
            v.tensor_scalar(smalli[:, 50:51], smalli[:, 48:49], -13.0, None, ALU.add)
            dve.drain()
            v.tensor_scalar(smalli[:, 51:53], smalli[:, 49:51], 23, None, ALU.logical_shift_left)
            dve.drain()
            v.tensor_scalar(Wc[:, :, 0:D], Wc[:, :, 0:D], small[:, 51:52], None, ALU.mult)
            v.tensor_scalar(rd2[:, :], rdeg[:, :], small[:, 52:53], None, ALU.mult).then_inc(s_sc2, 1)

            v.tensor_tensor(rank, delta, inval, ALU.subtract)
            dve.drain()
            v.tensor_reduce(small[:, 56:57], rank[:, 0:E], AX.X, ALU.add)
            v.memset(rank[:, E:EP], 0.0)
            for ends, t1, t2 in ((eS, binb, diag), (eD, delta, inval)):
                v.tensor_scalar(t1, ends, zrow[:, 0:1], None, ALU.subtract)
                dve.drain()
                v.tensor_tensor(t2, t1, rank, ALU.mult)
                dve.drain()
                v.tensor_scalar(ends, t2, zrow[:, 0:1], None, ALU.add)
            dve.drain()
            v.memset(small[:, 57:58], 0.0).then_inc(s_flag, 1)
            dve.wait_ge(s_fp, 1)
            v.tensor_copy(flag[:, :], banks[2][:, 0:1]).then_inc(s_flag, 1)

            dve.wait_ge(s_slot, 16)
            v.tensor_scalar(hiI, slotI, 8, None, ALU.logical_shift_right)
            dve.drain()
            v.tensor_copy(HI, hiI)
            v.tensor_scalar(slotI, slotI, 255, None, ALU.bitwise_and)
            dve.drain()
            v.tensor_copy(LO, slotI)
            v.memset(TT[:, T * TC:(T + 1) * TC], 0.0)
            v.memset(TU[:, T * TC:(T + 1) * TC], 0.0)
            dve.drain()
            tv, uv = (x[:, 0:T * TC].rearrange("p (t u) -> p t u", u=TC) for x in (TT, TU))
            hv, lv = (x[:, 0:BINS].rearrange("p (t u) -> p t u", u=T) for x in (HI, LO))
            v.tensor_tensor(tv[:, :, 0:T], hv, lv.rearrange("p t u -> p u t"), ALU.max)
            v.tensor_tensor(uv[:, :, 0:T], lv, hv.rearrange("p t u -> p u t"), ALU.max)
            dve.drain()
            hd, ld = (x[:, 0:BINS:T + 1] for x in (HI, LO))
            v.tensor_copy(TT[:, 0:T * TC:TC + 1], hd)
            v.tensor_copy(TU[:, 0:T * TC:TC + 1], ld)
            v.tensor_copy(tv[:, :, T], ld)
            v.tensor_copy(uv[:, :, T], hd)
            v.tensor_copy(tv[:, :, T + 1], HI[:, BINS:COLS])
            v.tensor_copy(uv[:, :, T + 1], LO[:, BINS:COLS])
            v.tensor_copy(tv[:, :, T + 2], LO[:, BINS:COLS])
            v.tensor_copy(uv[:, :, T + 2], HI[:, BINS:COLS])
            dve.drain()
            v.memset(small[:, 10:11], 0.0).then_inc(s_tabs, 1)

            def pairs(L, n, q, col):
                dve.wait_ge(s_bl[L], n + 1)
                for out, tab in ((OT, TT), (OU, TU)):
                    kb = tab[:, bass.ds(col, QB)].rearrange("p (a b) -> p a b", a=1).to_broadcast([P, P, QB])
                    last = v.tensor_tensor(out[q], iotaB[:, :, :], kb, ALU.is_equal)
                last.then_inc(s_oo[L], 1)

            def finish1(t):
                dve.wait_ge(s_ag[0], t + 2)
                v.scalar_tensor_tensor(out=aggc, in0=aggr[:, D:2 * D], scalar=1.0 / S, in1=aggr[:, 0:D],
                                       op0=ALU.mult, op1=ALU.add)
                dve.drain()
                v.scalar_tensor_tensor(out=aggn, in0=aggc, scalar=rd1[:, bass.ds(t, 1)],
                                       in1=R3[:, bass.ds(t * D, D)],
                                       op0=ALU.mult, op1=ALU.add).then_inc(s_an[0], 1)

            def place1(t):
                dve.wait_ge(s_at, t + 1)
                v.tensor_copy(R3[:, bass.ds(t * D, D)], banks[6][:, 0:D]).then_inc(s_ac, 1)

            def finish2(t):
                dve.wait_ge(s_ag[1], t + 2)
                v.scalar_tensor_tensor(out=aggc, in0=aggr[:, D:2 * D], scalar=1.0 / S, in1=aggr[:, 0:D],
                                       op0=ALU.mult, op1=ALU.add)
                dve.drain()
                v.scalar_tensor_tensor(out=aggn, in0=aggc, scalar=rd2[:, bass.ds(t, 1)],
                                       in1=R3[:, bass.ds(t * D, D)],
                                       op0=ALU.mult, op1=ALU.add).then_inc(s_an[1], 1)
                dve.drain()
                dve.wait_ge(s_xr, t * 16 + 16)
                v.tensor_tensor(aggc, aggn, xres, ALU.add).then_inc(s_xrf, 1)
                dve.drain()
                v.tensor_copy(R3[:, bass.ds(t * D, D)], aggc)
                v.bn_stats(stats[:, 0, :], aggc)
                dve.drain()
                v.bn_aggr(small[:, 16:18], stats[:, 0, :])
                dve.drain()
                v.tensor_copy(mv[:, bass.ds(t, 1), :], small[:, 16:18].rearrange("p (t c) -> p t c", c=2))

            def overflow(L, rd):
                with dve.Fori(0, E) as c:
                    for i in range(2):
                        m = 2 * c + i
                        dve.wait_ge(s_oj[L], m * 16 + 16)
                        v.tensor_copy(obf, ob)
                        dve.drain()
                        v.tensor_copy(oB, obf.to_broadcast([P, P])).then_inc(s_o1[L], 1)
                        dve.wait_ge(s_o2[L], m + 1)
                        v.tensor_scalar(oSel, banks[0][:, 0:P], obf, None, ALU.is_equal).then_inc(s_o3[L], 1)
                        dve.drain()
                        v.tensor_tensor(oM, oSel, neg4[:, 0, :], ALU.mult)
                        dve.drain()
                        v.tensor_reduce(oc, oM, AX.X, ALU.add)
                        v.scalar_tensor_tensor(out=od, in0=zrow[:, 0:1], scalar=float(P), in1=obf,
                                               op0=ALU.add, op1=ALU.subtract)
                        dve.drain()
                        v.scalar_tensor_tensor(out=oe, in0=oc, scalar=-1.5, in1=od, op0=ALU.is_lt, op1=ALU.mult)
                        dve.drain()
                        v.tensor_tensor(ow, oe, obf, ALU.add)
                        dve.wait_ge(s_oy[L], m * 16 + 16)
                        dve.wait_ge(s_o4[L], m + 1)
                        v.tensor_tensor(oN, banks[1][:, :], oA, ALU.add).then_inc(s_o5v[L], 1)
                with dve.Fori(0, T) as t:
                    dve.wait_ge(s_ol[L], t * 16 + 16)
                    v.scalar_tensor_tensor(out=oN[:, 0:D], in0=oA[:, D:2 * D], scalar=1.0 / S, in1=oA[:, 0:D],
                                           op0=ALU.mult, op1=ALU.add)
                    dve.drain()
                    v.scalar_tensor_tensor(out=oN[:, D:2 * D], in0=oN[:, 0:D], scalar=rd[:, bass.ds(t, 1)],
                                           in1=R3[:, bass.ds(t * D, D)], op0=ALU.mult, op1=ALU.add)
                    dve.drain()
                    v.tensor_copy(R3[:, bass.ds(t * D, D)], oN[:, D:2 * D]).then_inc(s_o6[L], 1)
                dve.drain()

            dve.wait_ge(s_r3, 1)
            dve.drain()
            lacking = dve.value_load(flag[0:1, 0:1])
            with dve.If(lacking > 0):
                overflow(0, rd1)

            for q in range(Q):
                pairs(0, q, q, q * QB)
            for q in range(Q):
                pairs(0, Q + q, q, TC + q * QB)
            finish1(0)
            with dve.Fori(1, T) as t:
                for q in range(Q):
                    pairs(0, (t + 1) * Q + q, q, (t + 1) * TC + q * QB)
                place1(t - 1)
                finish1(t)
            place1(T - 1)

            def tile4(n, i):
                dve.wait_ge(s_yh, n + 1)
                bank = banks[Y4(i)]
                v.tensor_tensor(R3[:, bass.ds(n * D, D)], bank[:, D:2 * D], zb[:, :], ALU.add)
                dve.wait_ge(s_yl, n + 1)
                v.tensor_tensor(ylo[0], bank[:, 0:D], R2[:, bass.ds(n * 2 * D, D)],
                                ALU.subtract).then_inc(s_zc, 1)

            with dve.Fori(0, T // W) as g:
                for i in range(W):
                    tile4(g * W + i, i)

            dve.wait_ge(s_yp, W + T)
            dve.wait_ge(s_yl, 1 + T)
            dve.drain()
            with dve.If(lacking > 0):
                overflow(1, rd2)
            for q in range(Q):
                pairs(1, q, q, q * QB)
            with dve.Fori(0, T) as t:
                for q in range(Q):
                    pairs(1, (t + 1) * Q + q, q, (t + 1) * TC + q * QB)
                finish2(t)

            dve.drain()
            v.tensor_copy(rstd[:, :], mv[:, :, 1]).then_inc(s_v2, 1)
            dve.wait_ge(s_d2, 1)
            v.reciprocal(rstd[:, :], rstd[:, :])
            dve.wait_ge(s_wg, 16 * (3 + EXPERTS))
            v.tensor_tensor(grows[0:1, 2, :], grows[0:1, 0, :], grows[0:1, 1, :], ALU.add).then_inc(s_gv, 1)
            dve.wait_ge(s_gp, 1)
            v.tensor_copy(gb, banks[6][:, 0:8]).then_inc(s_gpc, 1)
            dve.drain()
            with dve.Fori(0, T // W) as g:
                for i in range(W):
                    n = g * W + i
                    dve.wait_ge(s_t2, n + 1)
                    v.tensor_scalar(x2n[BUF5[i]], R3[:, bass.ds(n * D, D)], mv[:, bass.ds(n, 1), 0],
                                    rstd[:, bass.ds(n, 1)], ALU.subtract, ALU.mult).then_inc(s_n2, 1)
                dve.wait_ge(s_lp, g + 1)
                gbb = gb.rearrange("p (a n) -> p a n", a=1).to_broadcast([P, W, 8])
                v.tensor_tensor(lg, banks[7][:, 0:W * 8].rearrange("p (t n) -> p t n", n=8), gbb, ALU.add)
                dve.drain()
                for i in range(W):
                    v.max(mx[:, i, :], lg[:, i, :])
                dve.drain()
                for i in range(W):
                    v.max_index(mi[:, i, :], mx[:, i, :], lg[:, i, :])
                v.tensor_tensor(gw[:, :, 0:1], mx[:, :, 1:2], mx[:, :, 0:1], ALU.subtract).then_inc(s_lv, 1)
                dve.drain()
                v.tensor_copy(mif, mi[:, :, 0:2])
                dve.wait_ge(s_le, g + 1)
                v.tensor_scalar(gw[:, :, 2:3], gw[:, :, 1:2], 1.0, None, ALU.add)
                dve.drain()
                v.reciprocal(gw[:, :, 3:4], gw[:, :, 2:3])
                dve.drain()
                v.tensor_tensor(gw[:, :, 2:3], gw[:, :, 3:4], gw[:, :, 1:2], ALU.mult)
                i8 = iota8.rearrange("p (a n) -> p a n", a=1).to_broadcast([P, W, 8])
                v.tensor_tensor(c0, i8, mif[:, :, 0:1].to_broadcast([P, W, 8]), ALU.is_equal)
                v.tensor_tensor(c1, i8, mif[:, :, 1:2].to_broadcast([P, W, 8]), ALU.is_equal)
                dve.drain()
                v.tensor_tensor(lg, c0, gw[:, :, 3:4].to_broadcast([P, W, 8]), ALU.mult)
                v.tensor_tensor(mx, c1, gw[:, :, 2:3].to_broadcast([P, W, 8]), ALU.mult)
                dve.drain()
                v.tensor_tensor(comb, lg, mx, ALU.add).then_inc(s_cb, 1)
                for j in range(4):
                    w = 2 if j < 3 else 1
                    dve.wait_ge(s_bp, 4 * g + j + 1)
                    if j == 0:
                        dve.wait_ge(s_st, 16 * g + 16)
                    v.tensor_tensor(acc[:, 2 * j:2 * j + w, :],
                                    banks[j][:, 0:w * D].rearrange("p (t n) -> p t n", n=D),
                                    R3[:, bass.ds(g * (W * D) + 2 * j * D, w * D)].rearrange("p (t n) -> p t n", n=D),
                                    ALU.add).then_inc(s_ai, 1)
                dve.drain()
                for e in range(EXPERTS):
                    for j in range(4):
                        dve.wait_ge(s_dp, 32 * g + 4 * e + j + 9)
                        for i in range(2 * j, min(2 * j + 2, W)):
                            last = v.scalar_tensor_tensor(
                                out=acc[:, i, :], in0=banks[4 + j % 2][:, (i % 2) * D:(i % 2 + 1) * D],
                                scalar=comb[:, i, e:e + 1], in1=acc[:, i, :], op0=ALU.mult, op1=ALU.add)
                        last.then_inc(s_da, 1)
                    dve.drain()

        @block.scalar
        def _(act):
            a = nc.scalar
            act.wait_ge(s_const, 1)
            for n, c in ((1, s_ot), (1, s_m), (1, s_xlo), (4, s_ab[0]), (4, s_ab[1]), (1, s_ag[0]), (1, s_ag[1]),
                         (4, s_hr), (1, s_yl), (1, s_c2), (4, s_ur), (1, s_cc)):
                a.activation(cred[:, 0:1], ones[:, 0:1], ACT.Copy).then_inc(c, n)
                act.drain()

            def group1(par, g):
                act.wait_ge(s_tp, g + 1)
                act.wait_ge(s_r, g + 1)
                a.activation(OHiT[par][0:T, :], bank0h[0:T, :], ACT.Copy).then_inc(s_ot, 1)
                act.wait_ge(s_eq, g + 1)
                for h in range(2):
                    last = a.activation(Mm[par][:, 4 * h:4 * h + 4, :],
                                        banks[1 + h][:, :].rearrange("p (g e) -> p g e", e=P), ACT.Relu)
                last.then_inc(s_m, 1)

            with act.Fori(0, GROUPS // 2) as k:
                group1(0, 2 * k)
                group1(1, 2 * k + 1)
            group1(0, GROUPS)

            act.wait_ge(s_table, 16)
            with act.Fori(0, T // W) as b:
                act.wait_ge(s_stat, b + 1)
                a.activation(rstd[:, 0:W], rstd[:, 0:W], ACT.Sqrt, bias=epsc[:, :]).then_inc(s_std, 1)
                for i in range(W):
                    t = b * W + i
                    act.wait_ge(s_xn, t + 1)
                    a.activation(R2[:, bass.ds(t * 2 * D, D)], xs[i][:, 0:D], ACT.Copy, scale=S).then_inc(s_xhi, 1)
                    act.wait_ge(s_xl, t + 1)
                    a.activation(R2[:, bass.ds(t * 2 * D + D, D)], xlo[0], ACT.Copy, scale=S).then_inc(s_xlo, 1)
            act.wait_ge(s_w, 16 * 16)
            act.wait_ge(s_vm, 8)
            for j, src in enumerate((W0s[:, :, :], W1s[:, :, :], bhs[:, :], Wc[:, :, 0:D])):
                dst = sqs[:, 0:4] if j == 2 else sqs.rearrange("p (k n) -> p k n", k=2 if j < 2 else 4)
                last = a.activation(dst, src, ACT.Square, accum_out=small[:, 32 + j:33 + j])
                act.drain()
            a.activation(cred[:, 1:2], ones[:, 0:1], ACT.Copy).then_inc(s_sq, 1)
            act.wait_ge(s_sp, 1)
            a.activation(small[:, 40:44], banks[3][:, 0:4], ACT.Sqrt).then_inc(s_sr, 1)

            def evac(L, n, q):
                act.wait_ge(s_bl[L], n + 1 + Q)
                act.wait_ge(s_ap[L], n + 1)
                a.activation(Ab[q], banks[BB(q)][:, :], ACT.Copy).then_inc(s_ab[L], 1)

            def aggregate(L):
                for q in range(LEAD):
                    evac(L, q, q)
                with act.Fori(0, T) as t:
                    for q in range(Q):
                        evac(L, t * Q + q + LEAD, (q + LEAD) % Q)
                    act.wait_ge(s_ap[L], (t + 1) * Q + Q)
                    act.wait_ge(s_an[L], t + 1)
                    a.activation(aggr, banks[5][:, :], ACT.Copy).then_inc(s_ag[L], 1)

            aggregate(0)
            with act.Fori(0, T // W) as g:
                for h, (t0, tn) in enumerate(HALF):
                    for f in range(4):
                        j = 4 * h + f
                        act.wait_ge(s_hp, g * 8 + j + 1)
                        if j == 0:
                            act.wait_ge(s_yp, g * W + W)
                        a.activation(hT[:, f, t0 * P:(t0 + tn) * P], banks[f][:, 0:tn * P], ACT.Relu,
                                     bias=bhs[:, f:f + 1]).then_inc(s_hr, 1)
                for i in range(W):
                    n = g * W + i
                    act.wait_ge(s_yp, n + 1 + W)
                    a.activation(R2[:, bass.ds(n * 2 * D, D)],
                                 banks[Y4(i)][:, 0:D], ACT.Copy).then_inc(s_yh, 1)
                    act.wait_ge(s_zc, n + 4)
                    a.activation(R2[:, bass.ds(n * 2 * D + D, D)], ylo[0], ACT.Copy, scale=S).then_inc(s_yl, 1)
            act.wait_ge(s_yp, W + T)
            aggregate(1)

            act.wait_ge(s_v2, 1)
            a.activation(rstd[:, :], rstd[:, :], ACT.Sqrt, bias=epsc[:, :]).then_inc(s_d2, 1)
            act.wait_ge(s_wg, 16 * (3 + EXPERTS))
            with act.Fori(0, T // W) as g:
                for i in range(W):
                    n = g * W + i
                    act.wait_ge(s_t2, n + 1 + 2)
                    if i == 0:
                        act.wait_ge(s_up, g * 64 + 1)
                    a.activation(x2T[:, i, :, :], banks[6][:, 0:D].rearrange("p (k n) -> p k n", k=2),
                                 ACT.Copy).then_inc(s_c2, 1)
                act.wait_ge(s_lv, g + 1)
                a.activation(gw[:, :, 1:2], gw[:, :, 0:1], ACT.Exp).then_inc(s_le, 1)
                act.wait_ge(s_ct, 2 * g + 1)
                a.activation(combT[0:8, 0:4, :], banks[6][0:8, :].rearrange("p (t n) -> p t n", n=P), ACT.Copy)
                act.wait_ge(s_ct, 2 * g + 2)
                a.activation(combT[0:8, 4:7, :], banks[7][0:8, 0:3 * P].rearrange("p (t n) -> p t n", n=P),
                             ACT.Copy).then_inc(s_cc, 1)
                for e in range(EXPERTS):
                    for h, (t0, tn) in enumerate(HALF):
                        for f in range(4):
                            j = 4 * h + f
                            act.wait_ge(s_up, g * 64 + 8 * e + j + 2)
                            if j == 0:
                                act.wait_ge(s_dp, g * 32 + 4 * e - 4 + 8)
                            a.activation(h5[e % 2][:, f, t0 * P:(t0 + tn) * P], banks[j % 4][:, 0:tn * P],
                                         ACT.Relu, bias=b1c[:, e, f:f + 1]).then_inc(s_ur, 1)

        @block.tensor
        def _(pe):
            mm = nc.tensor.matmul
            pe.wait_ge(s_const, 1)
            for n, c in ((2, s_r), (W, s_xt), (Q, s_bl[0]), (Q, s_bl[1]), (Q, s_ap[0]), (Q, s_ap[1]),
                         (W, s_yp), (2, s_t2), (1, s_up), (8, s_dp)):
                mm(banks[6][:, 0:P], zeros16[:, :], zeros16[:, :], start=True, stop=True).then_inc(c, n)
            mm(banks[5][0:T, 0:P], zeros16[:, 0:T], zeros16[:, :], start=True, stop=False)

            def groupA(par, g):
                pe.wait_ge(s_ot, g + 1)
                pe.wait_ge(s_oh, g + 1)
                pe.wait_ge(s_t, g + 1)
                for c in range(G):
                    mm(banks[3][0:T, c * T:G * T], OHi[par][:, :, c],
                       OHj[par][:, :, c].rearrange("p (a j) -> p a j", a=1).to_broadcast([P, G - c, T]),
                       start=(c == 0), stop=(c == G - 1))
                for c in range(G):
                    last = nc.tensor.transpose(bank0h[0:T, c * P:(c + 1) * P], OHi[par][:, :, c], ident16[:, :])
                last.then_inc(s_tp, 1)
                for c in range(G):
                    mm(banks[5][0:T, 0:P], OHi[par][:, :, c], LHi[par][:, :, c], start=False, stop=False)
                    last = mm(banks[5][0:T, 0:P], OHj[par][:, :, c], LLo[par][:, :, c], start=False, stop=False)
                last.then_inc(s_h, 1)
                pe.wait_ge(s_m, g + 1)
                for h in range(2):
                    mm(banks[1 + h][:, :], ident16[:, :], neg4[:, :, :].rearrange("p c e -> p (c e)"),
                       start=True, stop=False)
                pe.wait_ge(s_ot, g + 2)
                for c in range(G):
                    ot = OHiT[par][0:T, c * P:(c + 1) * P]
                    last = mm(banks[1 + c // 4][:, (c % 4) * P:(c % 4 + 1) * P], ot, ot, start=False, stop=(c % 4 == 3))
                last.then_inc(s_eq, 1)

            def groupF(par, g):
                pe.wait_ge(s_m, g + 2)
                pe.wait_ge(s_t, g + 2)
                pe.wait_ge(s_rk, g + 1)
                for c in range(G):
                    o = banks[4][:, c * T:(c + 1) * T]
                    mm(o, Mm[par][:, c, :], OHj[par][:, :, c], start=True, stop=False)
                    last = mm(o, OHiT[par][0:T, c * P:(c + 1) * P], Tsn[par][0:T, c, :], start=False, stop=True)
                last.then_inc(s_r, 1)

            groupA(0, 0)
            with pe.Fori(0, GROUPS // 2) as k:
                for par in range(2):
                    g = 2 * k + par
                    groupF(par, g)
                    groupA(1 - par, g + 1)

            pe.wait_ge(s_ot, GROUPS + 2)
            pe.wait_ge(s_rk, GROUPS + 1)
            for h in range(2):
                mm(banks[6 + h][:, :], zeros16[:, :], zeros16[:, 0:1].to_broadcast([P, 512]), start=True, stop=False)
            with pe.Fori(0, T // W) as b:
                for i in range(W):
                    t = b * W + i
                    pe.wait_ge(s_xn, t + 1)
                    pe.wait_ge(s_xtc, t + 1)
                    for h in range(2):
                        nc.tensor.transpose(banks[0][:, h * P:(h + 1) * P], xs[i][:, h * P:(h + 1) * P], ident[:, :])
                    for h in range(2):
                        last = mm(banks[6 + h][:, 0:D + 1], xs[i][:, h * P:(h + 1) * P], xs[i][:, 0:D + 1],
                                  start=False, stop=False)
                    last.then_inc(s_xt, 1)

            pe.wait_ge(s_w, 16 * 16)
            mm(banks[5][0:T, 0:P], zeros16[:, 0:T], zeros16[:, :], start=False, stop=True)
            mm(banks[6][:, 0:P], zeros16[:, :], zeros16[:, :], start=False, stop=True)
            mm(banks[7][:, 0:P], zeros16[:, :], zeros16[:, :], start=False, stop=True).then_inc(s_pm, 1)
            for i, wgt in enumerate((Wk, Wv, Wfc)):
                if i == 0:
                    pe.wait_ge(s_xtc, T + 1)
                for kt in range(2):
                    for dt in range(2):
                        last = nc.tensor.transpose(banks[i][:, dt * D + kt * P:dt * D + (kt + 1) * P],
                                                   wgt[:, kt, dt * P:(dt + 1) * P], ident[:, :])
                last.then_inc(s_pm, 1)
            pe.wait_ge(s_vm, 3)
            for gt in range(2):
                for dt in range(2):
                    mm(banks[3][:, gt * D:(gt + 1) * D], Gs[:, dt, gt * P:(gt + 1) * P], WvT[:, dt, :],
                       start=(dt == 0), stop=(dt == 1))
            for r, wt in ((0, WvT), (1, WkT)):
                for dt in range(2):
                    last = mm(banks[4][0:1, r * D:(r + 1) * D], Gs[:, dt, D:D + 1], wt[:, dt, :],
                              start=(dt == 0), stop=(dt == 1))
            last.then_inc(s_pm, 1)
            pe.wait_ge(s_vm, 5)
            for vt in range(2):
                o = banks[0][:, vt * D:(vt + 1) * D]
                for gt in range(2):
                    mm(o, B1s[:, gt, vt * P:(vt + 1) * P], WkT[:, gt, :], start=(gt == 0), stop=False)
                mm(o, rows[0:1, SV, vt * P:(vt + 1) * P], rows[0:1, BK, :], start=False, stop=False)
                last = mm(o, rows[0:1, BV, vt * P:(vt + 1) * P], rows[0:1, SK, :], start=False, stop=True)
            last.then_inc(s_pm, 1)
            pe.wait_ge(s_vm, 6)
            for dt in range(2):
                for et in range(2):
                    last = mm(banks[1][:, dt * D:(dt + 1) * D], PTs[:, et, dt * P:(dt + 1) * P], WfT[:, et, :],
                              start=(et == 0), stop=(et == 1))
            last.then_inc(s_pm, 1)
            pe.wait_ge(s_vm, 7)
            for xt in range(2):
                for dt in range(2):
                    mm(banks[2][:, xt * D:(xt + 1) * D], Wq[:, dt, xt * P:(xt + 1) * P], Rs[:, dt, :],
                       start=(dt == 0), stop=(dt == 1))
            for dt in range(2):
                last = mm(banks[3][0:1, 0:D], bqc[:, dt:dt + 1], Rs[:, dt, :], start=(dt == 0), stop=(dt == 1))
            last.then_inc(s_pm, 1)
            pe.wait_ge(s_vm, 8)
            mm(banks[4][:, 0:D], ones[0:1, :], rows[0:1, ZB, :], start=True, stop=True).then_inc(s_pm, 1)
            pe.wait_ge(s_vm, 10)
            nc.tensor.transpose(banks[1][:, 0:T], degT[0:T, :], ident[0:T, 0:T]).then_inc(s_pm, 1)
            pe.wait_ge(s_sq, 1)
            mm(banks[3][:, 0:4], ones[:, :], small[:, 32:36], start=True, stop=True).then_inc(s_sp, 1)
            pe.wait_ge(s_vm, 12)
            pe.wait_ge(s_sr, 1)
            pe.wait_ge(s_flag, 1)
            mm(banks[2][:, 0:1], ones[:, :], small[:, 56:57], start=True, stop=True).then_inc(s_fp, 1)
            pe.wait_ge(s_flag, 2)
            lacking = pe.value_load(flag[0:1, 0:1])

            def overflow(L):
                with pe.Fori(0, E) as c:
                    for i in range(2):
                        m = 2 * c + i
                        pe.wait_ge(s_o1[L], m + 1)
                        nc.tensor.transpose(banks[0][:, 0:P], oB, ident[:, :]).then_inc(s_o2[L], 1)
                        pe.wait_ge(s_ox[L], m * 16 + 16)
                        pe.wait_ge(s_o3[L], m + 1)
                        mm(banks[1][:, :], oSel, oX, start=True, stop=True).then_inc(s_o4[L], 1)

            def build(L, n, q):
                pe.wait_ge(s_oo[L], n + 1)
                pe.wait_ge(s_ab[L], n + 1)
                for c in range(QB):
                    last = mm(banks[BB(q)][:, c * P:(c + 1) * P], OU[q][:, :, c], OT[q][:, :, c],
                              start=True, stop=True)
                last.then_inc(s_bl[L], 1)

            def apply(L, t, q):
                if q == 0:
                    pe.wait_ge(s_ag[L], t + 1)
                pe.wait_ge(s_ab[L], t * Q + q + 5)
                for c in range(QB):
                    u = q * QB + c
                    src = R2[:, u * 2 * D:(u + 1) * 2 * D] if u < T else R2[:, bass.ds(t * (2 * D), 2 * D)]
                    last = mm(banks[5][:, :], Ab[q][:, c * P:(c + 1) * P], src,
                              start=(u == 0), stop=(u == TC - 1))
                last.then_inc(s_ap[L], 1)

            def transposed(t):
                pe.wait_ge(s_an[0], t + 2)
                pe.wait_ge(s_ac, t + 1)
                for h in range(2):
                    last = nc.tensor.transpose(banks[6][:, h * P:(h + 1) * P], aggn[:, h * P:(h + 1) * P], ident[:, :])
                last.then_inc(s_at, 1)

            def tile3(L, t, before):
                for q in range(Q):
                    build(L, t * Q + q + LEAD, (q + LEAD) % Q)
                    apply(L, t, q)
                    if q == 6 and before:
                        transposed(t - 1)

            pe.wait_ge(s_xhi, T)
            pe.wait_ge(s_xlo, 1 + T)
            with pe.If(lacking > 0):
                overflow(0)
            for q in range(LEAD):
                build(0, q, q)
            tile3(0, 0, False)
            with pe.Fori(1, T) as t:
                tile3(0, t, True)
            transposed(T - 1)

            pe.wait_ge(s_ac, 1 + T)
            pe.wait_ge(s_sc2, 1)
            pe.wait_ge(s_ab[0], T * Q + LEAD + 4)
            pe.wait_ge(s_ag[0], 1 + T)
            def hidden(g, par, need):
                pe.wait_ge(s_x4[par], need)
                for h, (t0, tn) in enumerate(HALF):
                    xv = xT4[par][:, t0 * D:(t0 + tn) * D].rearrange("p (t k n) -> p t k n", t=tn, k=2)
                    av = R3[:, bass.ds(g * (W * D) + t0 * D, tn * D)].rearrange("p (t k n) -> p t k n", t=tn, k=2)
                    for f in range(4):
                        j = 4 * h + f
                        pe.wait_ge(s_hr, g * 8 + j + 1)
                        o = banks[f][:, 0:tn * P].rearrange("p (t n) -> p t n", n=P)
                        for k in range(2):
                            mm(o, W0s[:, k, f * P:(f + 1) * P], xv[:, :, k, :], start=(k == 0), stop=False)
                        for k in range(2):
                            last = mm(o, W1s[:, k, f * P:(f + 1) * P], av[:, :, k, :], start=False, stop=(k == 1))
                        last.then_inc(s_hp, 1)
                pe.wait_ge(s_hr, g * 8 + 12)
                for i in range(W):
                    n = g * W + i
                    pe.wait_ge(s_zc, n + 1)
                    o = banks[Y4(i)]
                    for f in range(4):
                        mm(o[:, :], hT[:, f, i * P:(i + 1) * P], Wc[:, f, :], start=(f == 0), stop=False)
                    for k in range(2):
                        last = mm(o[:, D:2 * D], xT4[par][:, i * D + k * P:i * D + (k + 1) * P], Ms[:, k, :],
                                  start=False, stop=(k == 1))
                    last.then_inc(s_yp, 1)

            with pe.Fori(0, T // W // 2) as k2:
                for par in range(2):
                    hidden(2 * k2 + par, par, 16 * k2 + 16)
            hidden(T // W - 1, 0, 16 * (T // W // 2 + 1))

            pe.wait_ge(s_yl, 1 + T)
            pe.wait_ge(s_zc, 3 + T)
            with pe.If(lacking > 0):
                overflow(1)
            for q in range(LEAD):
                build(1, q, q)
            with pe.Fori(0, T) as t:
                tile3(1, t, False)

            pe.wait_ge(s_ab[1], T * Q + LEAD + 4)
            pe.wait_ge(s_ag[1], 1 + T)
            pe.wait_ge(s_gv, 1)
            mm(banks[6][:, 0:8], ones[0:1, :], grows[0:1, 2, :], start=True, stop=True).then_inc(s_gp, 1)
            pe.wait_ge(s_gpc, 1)
            pe.wait_ge(s_wg, 16 * (3 + EXPERTS))
            pe.wait_ge(s_st, 16)
            with pe.Fori(0, T // W) as g:
                for i in range(W):
                    n = g * W + i
                    pe.wait_ge(s_n2, n + 1)
                    pe.wait_ge(s_c2, n + 1)
                    if i == 0:
                        pe.wait_ge(s_cc, g + 1)
                    for k in range(2):
                        last = nc.tensor.transpose(banks[6][:, k * P:(k + 1) * P],
                                                   x2n[BUF5[i]][:, k * P:(k + 1) * P], ident[:, :])
                    last.then_inc(s_t2, 1)
                pe.wait_ge(s_c2, (g + 1) * W + 1)
                for i in range(W):
                    for k in range(2):
                        last = mm(banks[7][:, i * 8:(i + 1) * 8], x2T[:, i, k, :], Wgs[:, k, :],
                                  start=(k == 0), stop=(k == 1))
                last.then_inc(s_lp, 1)

                def up(e):
                    pe.wait_ge(s_we[e], 32)
                    for h, (t0, tn) in enumerate(HALF):
                        for f in range(4):
                            j = 4 * h + f
                            pe.wait_ge(s_ur, g * 64 + 8 * e + j + 1)
                            o = banks[j % 4][:, 0:tn * P].rearrange("p (t n) -> p t n", n=P)
                            for k in range(2):
                                last = mm(o, W1e[e][:, k, f * P:(f + 1) * P], x2T[:, t0:t0 + tn, k, :],
                                          start=(k == 0), stop=(k == 1))
                            last.then_inc(s_up, 1)

                def down(e):
                    pe.wait_ge(s_ur, g * 64 + 8 * e + 12)
                    for j in range(4):
                        pe.wait_ge(s_da, g * 32 + 4 * e + j + 1)
                        for i in range(2 * j, min(2 * j + 2, W)):
                            o = banks[4 + j % 2][:, (i % 2) * D:(i % 2 + 1) * D]
                            for f in range(4):
                                last = mm(o, h5[e % 2][:, f, i * P:(i + 1) * P], W2e[e][:, f, :],
                                          start=(f == 0), stop=(f == 3))
                        last.then_inc(s_dp, 1)

                pe.wait_ge(s_cb, g + 1)
                for i in range(W):
                    last = nc.tensor.transpose(banks[6 + i // 4][0:8, (i % 4) * P:(i % 4 + 1) * P],
                                               comb[:, i, :], ident[:, :])
                    if i in (3, 6):
                        last.then_inc(s_ct, 1)
                pe.wait_ge(s_cc, g + 2)
                pe.wait_ge(s_ur, g * 64 + 4)
                for j in range(4):
                    for i in range(2 * j, min(2 * j + 2, W)):
                        last = mm(banks[j][:, (i % 2) * D:(i % 2 + 1) * D], combT[0:8, i, :], b2s[0:8, :],
                                  start=True, stop=True)
                    last.then_inc(s_bp, 1)
                pe.wait_ge(s_ai, 4 * g + 4)
                up(0)
                for e in range(EXPERTS):
                    if e + 1 < EXPERTS:
                        up(e + 1)
                    down(e)


_INS = ["x", "src", "dst", "L0_gnn_W0_0", "L0_gnn_b0_0", "L0_gnn_W1_0", "L0_gnn_b1_0", "L0_gnn_W0_1",
        "L0_gnn_b0_1", "L0_gnn_W1_1", "L0_gnn_b1_1", "L0_mix_Wq", "L0_mix_bq", "L0_mix_Wk", "L0_mix_bk",
        "L0_mix_Wv", "L0_mix_bv", "L0_mix_Wfc", "L0_mix_bfc", "L0_ffn_Wg", "L0_ffn_bg", "L0_ffn_bias",
        "L0_ffn_W1", "L0_ffn_b1", "L0_ffn_W2", "L0_ffn_b2"]


def kernel(**inputs):
    import numpy as _np
    import concourse.bacc as _bacc
    from concourse import mybir as _mybir
    from concourse.bass_utils import run_bass_kernel_spmd as _run

    nc = _bacc.Bacc("TRN2", target_bir_lowering=False, num_devices=1)
    arrays, io = {}, {}
    for name in _INS:
        a = _np.ascontiguousarray(inputs[name])
        arrays[f"in_{name}_dram"] = a
        io[name] = nc.dram_tensor(f"in_{name}_dram", a.shape, _mybir.dt.from_np(a.dtype), kind="ExternalInput").ap()
    io["out"] = nc.dram_tensor("out_dram", (N, D), _mybir.dt.float32, kind="ExternalOutput").ap()
    gps_layer(nc, io)
    r = _run(nc, [arrays], core_ids=[0])
    return r.results[0]["out_dram"]
```

```python
import concourse.bass as bass
from concourse import mybir
from contextlib import ExitStack

F32, F16, I32 = mybir.dt.float32, mybir.dt.float16, mybir.dt.int32
U32, BF16 = mybir.dt.uint32, mybir.dt.bfloat16
ALU, ACT, AX = mybir.AluOpType, mybir.ActivationFunctionType, mybir.AxisListType
RADD = bass.bass_isa.ReduceOp.add

P = 128
N, D, F, EXPERTS, HEADS = 6250, 256, 512, 8, 8
EDGES = 106250
T = -(-N // P)
LAST = N - (T - 1) * P
E = 832
EP = E + 8
G = 8
GROUPS = E // G
LASTE = EDGES - (P - 1) * E
PADNODE = 8191
BINS = T * T
COLS = BINS + T
TRASH = P * COLS
SLOTS = TRASH + P * EP
TC = T + 3
QB = 4
Q = TC // QB
LEAD = 3
S = 2048.0
W = 7
HALF = ((0, 4), (4, 3))
OVROW = T * P
EPS = 1e-5


def gps_layer(nc, io):
    ctx = ExitStack()
    with ctx:
        ctx.enter_context(nc.allow_non_contiguous_dma(reason="bias columns"))

        def sb(name, shape, dt=F32):
            return ctx.enter_context(nc.sbuf_tensor(name, shape, dt))

        def sem(name):
            return ctx.enter_context(nc.semaphore(name))

        slots_dram = nc.dram_tensor("slots_dram", [SLOTS, 1], I32).ap()
        feat_dram = nc.dram_tensor("feat_dram", [(T + 1) * P, 2 * D], F16).ap()
        sum_dram = nc.dram_tensor("sum_dram", [(T + 2) * P, 2 * D], F32).ap()
        ends_dram = nc.dram_tensor("ends_dram", [2, P, EP], I32).ap()
        w_dram = nc.dram_tensor("w_dram", [EXPERTS, P, 8 * F], F16).ap()
        x2_dram = nc.dram_tensor("x2_dram", [T * P, D], F32).ap()
        xT_dram = nc.dram_tensor("xT_dram", [T // W, P, W * D], F32).ap()

        R2 = sb("R2", [P, T * 2 * D], F16)
        R3 = sb("R3", [P, T * D])
        R2f = R2[:, :].bitcast(F32)
        R3i = R3[:, :].bitcast(I32)
        R3h = R3[:, :].bitcast(F16)

        def words(i):
            return slice(i * EP, (i + 1) * EP)

        eS, eD = R3i[:, words(0)], R3i[:, words(1)]
        eHi, eLo = R3i[:, words(2)], R3i[:, words(3)]
        eTi, eTj = R3i[:, words(4)], R3i[:, words(5)]
        rank, posI = R3[:, words(4)], R3i[:, words(5)]
        rec = R3i[:, words(6)]
        binb, diag = R3[:, words(7)], R3[:, words(8)]
        delta = R3[:, words(9)]
        inval = R3[:, words(10)]
        half0 = 11 * EP * 2
        fTi, fTj, fHi, fLo = (R3h[:, half0 + i * EP:half0 + (i + 1) * EP] for i in range(4))
        assert half0 + 4 * EP <= 2 * T * D

        trash = sb("trash", [P, EP], I32)
        TT = sb("TT", [P, (T + 1) * TC], F16)
        TU = sb("TU", [P, (T + 1) * TC], F16)
        iota128 = sb("iota128", [P, P, G], F16)
        iota49 = sb("iota49", [P, T, G], F16)
        iotaB = sb("iotaB", [P, P, QB], F16)
        ident16 = sb("ident16", [P, P], F16)
        ident = sb("ident", [P, P])
        zeros16 = sb("zeros16", [P, P], F16)
        neg4 = sb("neg4", [P, 4, P], F16)
        ones = sb("ones", [P, P])
        epsc = sb("epsc", [P, 1])
        W01 = sb("W01", [P, 4, F])
        W0s, W1s = W01[:, 0:2, :], W01[:, 2:4, :]
        Wc = sb("Wc", [P, 4, 2 * D])
        bh = sb("bh", [P, 2, 4])
        bhs = sb("bhs", [P, 4])
        zb = sb("zb", [P, D])
        Ms = sb("Ms", [P, 2, D])
        deg = sb("deg", [P, T])
        rdeg = sb("rdeg", [P, T])
        rd1 = sb("rd1", [P, T])
        rd2 = sb("rd2", [P, T])
        stats = sb("stats", [P, W, 6])
        iota8 = sb("iota8", [P, 8])
        zeros32 = sb("zeros32", [P, D])
        cred = sb("cred", [P, 2])
        iscA = sb("iscA", [P, EXPERTS])
        csA = sb("csA", [P, EXPERTS])
        b1A = sb("b1A", [P, EXPERTS * 4])
        zrow = sb("zrow", [P, 1])
        flag = sb("flag", [P, 1], I32)
        pwait = sb("pwait", [P, 1])
        mv = sb("mv", [P, W, 2])
        rstd = sb("rstd", [P, W])
        small = sb("small", [P, 64])
        smalli = small[:, :].bitcast(I32)
        BIG = 17330
        big = sb("big", [P, BIG])
        bigh = big[:, :].bitcast(F16)
        bigi = big[:, :].bitcast(I32)

        def BB(q):
            return q % 4 if q < 12 else 4

        def blocks(q):
            return QB if q < Q - 1 else 2

        def Y4(i):
            return 4 + (i % 3 if i < 6 else 3)

        banks = [ctx.enter_context(nc.psum_tensor(f"bank{i}", [P, 512], F32)) for i in range(8)]

        bank0h = banks[0][:, :].bitcast(F16)

        class Space:
            def __init__(self, at=0):
                self.at = at

            def f32(self, *shape):
                n = 1
                for s in shape:
                    n *= s
                ap = big[:, self.at:self.at + n]
                self.at += n
                assert self.at <= BIG, self.at
                return ap

            def f16(self, *shape):
                n = 1
                for s in shape:
                    n *= s
                ap = bigh[:, 2 * self.at:2 * self.at + n]
                self.at += -(-n // 2)
                assert self.at <= BIG, self.at
                return ap

            def i32(self, *shape):
                n = 1
                for s in shape:
                    n *= s
                ap = bigi[:, self.at:self.at + n]
                self.at += n
                assert self.at <= BIG, self.at
                return ap

        sp1 = Space()
        OHi = [sp1.f16(T * G).rearrange("p (m g) -> p m g", g=G) for _ in range(2)]
        OHj = [sp1.f16(T * G).rearrange("p (m g) -> p m g", g=G) for _ in range(2)]
        at_L = sp1.at
        LHi = [sp1.f16(P * G).rearrange("p (m g) -> p m g", g=G) for _ in range(2)]
        LLo = [sp1.f16(P * G).rearrange("p (m g) -> p m g", g=G) for _ in range(2)]
        at_T = sp1.at
        OHiT = [sp1.f16(G * P) for _ in range(2)]
        sqs = big[:, at_T:at_T + 1024]
        Mm = [sp1.f16(G * P).rearrange("p (g e) -> p g e", g=G) for _ in range(2)]
        Tsn = [sp1.f16((G + 1) * T).rearrange("p (g j) -> p g j", j=T) for _ in range(2)]
        prod = sp1.f32(G * T).rearrange("p (g j) -> p g j", j=T)
        d1 = sp1.f32(G)
        rr = sp1.f32(G)
        ee = sp1.f32(G)
        bb = sp1.f32(G)
        pp = sp1.f32(G)
        ov = sp1.f32(G)
        tq = sp1.f32(G)
        tr = sp1.f32(G)
        stP = [sb(f"stP{i}", [P, G], I32) for i in range(2)]
        stR = [sb(f"stR{i}", [P, G], I32) for i in range(2)]
        xs = [sp1.f32(D + 1) for _ in range(W)]
        xlo = [sp1.f32(D) for _ in range(2)]
        Gs = sp1.f32(2 * (D + 1)).rearrange("p (k n) -> p k n", k=2)
        Wq, Wk, Wv, Wfc = (sp1.f32(2 * D).rearrange("p (k n) -> p k n", k=2) for _ in range(4))
        hmask = sp1.f32(2 * D).rearrange("p (k n) -> p k n", k=2)
        xin = sp1.f32(W * D)
        xst = sp1.f32(W * D)
        sp2 = Space(at_L)
        WkT, WvT, B1s, PTs = (sp2.f32(2 * D).rearrange("p (k n) -> p k n", k=2) for _ in range(4))
        assert sp2.at <= at_T
        sp2 = Space(at_T + 1024)
        WfT, Rs = (sp2.f32(2 * D).rearrange("p (k n) -> p k n", k=2) for _ in range(2))
        bqc = sp1.f32(2)
        rows = sp1.f32(9 * D).rearrange("p (r n) -> p r n", r=9)
        BK, BV, BFC, B01, B11, SV, SK, ZB, SPARE = range(9)
        degT = sp1.f32(P)

        sp3 = Space()
        slotI = sp3.i32(COLS)
        hiI = sp3.i32(COLS)
        HI = sp3.f16(COLS)
        LO = sp3.f16(COLS)
        sp3b = Space()
        OT = [sp3b.f16(P * QB).rearrange("p (m b) -> p m b", b=QB) for _ in range(Q)]
        OU = [sp3b.f16(P * QB).rearrange("p (m b) -> p m b", b=QB) for _ in range(Q)]
        Ab = [sp3b.f16(QB * P) for _ in range(Q)]
        aggr = sp3b.f32(2 * D)
        aggc = sp3b.f32(D)
        aggn = sp3b.f32(D)
        xres = sp3b.f32(D)
        x2b, x2n = sp3b.f32(D), sp3b.f32(D)
        x2s, x2m, x2r = sp3b.f32(6), sp3b.f32(2), sp3b.f32(1)
        graw = sp3b.f32(2 * 8).rearrange("p (k n) -> p k n", k=2)
        gres = sp3b.f32(2 * 8).rearrange("p (k n) -> p k n", k=2)
        gres2 = sp3b.f32(2 * 8).rearrange("p (k n) -> p k n", k=2)
        gpart = sp3b.f16(2 * 24).bitcast(BF16).rearrange("p (k g n) -> p k g n", k=2, g=3)
        spo = Space(sp3b.at)
        oX = spo.f16(2 * D)
        oA = spo.f32(2 * D)
        oN = spo.f32(2 * D)
        oSel = spo.f16(P)
        oB = spo.f32(P)
        oM = spo.f32(P)
        oa, ob, ow = (spo.i32(1) for _ in range(3))
        obf, oc, od, oe = (spo.f32(1) for _ in range(4))
        sp4 = Space()
        hT = sp4.f32(4 * W * P).rearrange("p (f n) -> p f n", f=4)
        xT4 = [sp4.f32(W * D) for _ in range(2)]
        ylo = [sp4.f32(D) for _ in range(2)]
        wraw = sp4.f32(4 * F)
        wsq = sp4.f32(2 * F)
        wout = sp4.f16(8 * F)
        braw = sp4.f32(4)
        sq3, nr3, nv3 = sp4.f32(3), sp4.f32(3), sp4.f32(3)
        ex3, cl3 = sp4.i32(3), sp4.f32(3)
        ab6, sc6 = sp4.i32(6), sp4.i32(6)
        sp5 = Space()
        h32 = [sp5.f32(4 * P) for _ in range(4)]
        hhi = [sp5.f16(4 * W * P).rearrange("p (f n) -> p f n", f=4) for _ in range(2)]
        hlo = [sp5.f16(4 * W * P).rearrange("p (f n) -> p f n", f=4) for _ in range(2)]
        acc = sp5.f32(W * D).rearrange("p (t n) -> p t n", t=W)
        xr5 = sp5.f32(W * D).rearrange("p (t n) -> p t n", t=W)
        gb = sp5.f32(8)
        combg = sp5.f32(W * 8)
        grows = sp5.f32(3 * 8).rearrange("p (r n) -> p r n", r=3)
        b2s = sp5.f32(D)

        def tiles8():
            return sp5.f32(T * 8).rearrange("p (t n) -> p t n", t=T)

        lg, mx, comb, combs, c0 = (tiles8() for _ in range(5))
        mi = sp5.i32(T * 8).bitcast(U32).rearrange("p (t n) -> p t n", t=T)
        mif = sp5.f32(T * 2).rearrange("p (t n) -> p t n", t=T)
        gw = sp5.f32(T * 4).rearrange("p (t n) -> p t n", t=T)
        combT = sp5.f32(W * P).rearrange("p (t n) -> p t n", t=W)
        wslot = [R2[:, 8 * F * e:8 * F * (e + 1)] for e in range(6)]
        wslot += [x[:, :, :].rearrange("p k n -> p (k n)").bitcast(F16) for x in (W01, Wc)]
        LG = big[:, BIG - T * 8:BIG].rearrange("p (t n) -> p t n", t=T)
        assert sp5.at <= BIG - T * 8 and spo.at <= BIG - T * 8 and sp4.at <= BIG - T * 8

        def R3t(t, part):
            return R3h[:, t * 2 * D + part * D:t * 2 * D + (part + 1) * D] if isinstance(t, int) else \
                R3h[:, bass.ds(t * (2 * D) + part * D, D)]

        def w1(e, part, k):
            return wslot[e][:, part * 2 * F + k * F:part * 2 * F + (k + 1) * F]

        def w2(e, part, k):
            return wslot[e][:, (2 + part) * 2 * F + k * D:(2 + part) * 2 * F + (k + 1) * D]

        slotZ = R2[:, 0:2 * COLS].bitcast(I32)

        s_const = sem("s_const")
        s_blank = sem("s_blank")
        s_edges = sem("s_edges")
        s_zero = sem("s_zero")
        s_table = sem("s_table")
        s_x = sem("s_x")
        s_w = sem("s_w")
        s_keys = sem("s_keys")
        s_oh = sem("s_oh")
        s_tp = sem("s_tp")
        s_ot = sem("s_ot")
        s_eq = sem("s_eq")
        s_h = sem("s_h")
        s_m = sem("s_m")
        s_t = sem("s_t")
        s_r = sem("s_r")
        s_rk = sem("s_rk")
        s_pos = sem("s_pos")
        s_stage = sem("s_stage")
        s_sc = [sem("s_sc0"), sem("s_sc1")]

        s_stat = sem("s_stat")
        s_std = sem("s_std")
        s_xn = sem("s_xn")
        s_xhi = sem("s_xhi")
        s_xl = sem("s_xl")
        s_xlo = sem("s_xlo")
        s_xt = sem("s_xt")
        s_xtc = sem("s_xtc")
        s_pm = sem("s_pm")
        s_vm = sem("s_vm")

        s_slot = sem("s_slot")
        s_tabs = sem("s_tabs")
        s_r3 = sem("s_r3")
        s_flag = sem("s_flag")
        s_fp = sem("s_fp")
        s_ends = sem("s_ends")
        s_of = [sem(f"s_of{i}") for i in range(2)]
        s_oi = [sem(f"s_oi{i}") for i in range(2)]
        s_oj = [sem(f"s_oj{i}") for i in range(2)]
        s_ox = [sem(f"s_ox{i}") for i in range(2)]
        s_oy = [sem(f"s_oy{i}") for i in range(2)]
        s_os = [sem(f"s_os{i}") for i in range(2)]
        s_ol = [sem(f"s_ol{i}") for i in range(2)]
        s_o1 = [sem(f"s_o1{i}") for i in range(2)]
        s_o2 = [sem(f"s_o2{i}") for i in range(2)]
        s_o3 = [sem(f"s_o3{i}") for i in range(2)]
        s_o4 = [sem(f"s_o4{i}") for i in range(2)]
        s_o5v = [sem(f"s_o5{i}") for i in range(2)]
        s_o6 = [sem(f"s_o6{i}") for i in range(2)]
        s_oo = [sem(f"s_oo{i}") for i in range(2)]
        s_bl = [sem(f"s_bl{i}") for i in range(2)]
        s_ab = [sem(f"s_ab{i}") for i in range(2)]
        s_ap = [sem(f"s_ap{i}") for i in range(2)]
        s_ag = [sem(f"s_ag{i}") for i in range(2)]
        s_an = [sem(f"s_an{i}") for i in range(2)]
        s_at = sem("s_at")
        s_ac = sem("s_ac")
        s_xr = sem("s_xr")
        s_xrf = sem("s_xrf")

        s_x4 = [sem(f"s_x4{i}") for i in range(2)]
        s_xT = sem("s_xT")
        s_xp = sem("s_xp")
        s_sq = sem("s_sq")
        s_sp = sem("s_sp")
        s_sr = sem("s_sr")
        s_sc2 = sem("s_sc2")
        s_hp = sem("s_hp")
        s_hr = sem("s_hr")
        s_yp = sem("s_yp")
        s_yh = sem("s_yh")
        s_zc = sem("s_zc")
        s_yl = sem("s_yl")

        s_wl = sem("s_wl")
        s_wq = sem("s_wq")
        s_wr = sem("s_wr")
        s_wt = sem("s_wt")
        s_wc = sem("s_wc")
        s_wh = sem("s_wh")
        s_wo = sem("s_wo")
        s_wst = sem("s_wst")
        s_gl = sem("s_gl")
        s_gs = sem("s_gs")
        s_v2 = sem("s_v2")
        s_x2 = sem("s_x2")
        s_d2 = sem("s_d2")
        s_n2 = sem("s_n2")
        s_t2 = sem("s_t2")
        s_h2 = sem("s_h2")
        s_l2 = sem("s_l2")
        s_lp = sem("s_lp")
        s_lr = sem("s_lr")
        s_we = [sem(f"s_we{e}") for e in range(EXPERTS)]
        s_wg = sem("s_wg")
        s_gv = sem("s_gv")
        s_gp = sem("s_gp")
        s_lv = sem("s_lv")
        s_le = sem("s_le")
        s_cb = sem("s_cb")
        s_ct = sem("s_ct")
        s_cc = sem("s_cc")
        s_bp = sem("s_bp")
        s_ai = sem("s_ai")
        s_xr5 = sem("s_xr5")
        s_up = sem("s_up")
        s_ua = sem("s_ua")
        s_us = sem("s_us")
        s_dp = sem("s_dp")
        s_da = sem("s_da")
        s_st = sem("s_st")
        s_o5 = sem("s_o5")

        block = ctx.enter_context(nc.Block())

        @block.sync
        def _(sp):
            sp.wait_ge(s_blank, 1)
            for end, arr in (("src", eS), ("dst", eD)):
                v = io[end][0:(P - 1) * E].rearrange("(p c) -> p c", c=E)
                sp.dma_start(arr[0:112, 0:E], v[0:112, :]).then_inc(s_edges, 16)
                sp.dma_start(arr[112:127, 0:E], v[112:127, :]).then_inc(s_edges, 16)
                sp.dma_start(arr[127:128, 0:LASTE],
                             io[end][(P - 1) * E:EDGES].rearrange("(a n) -> a n", a=1)).then_inc(s_edges, 16)
            sp.wait_ge(s_zero, 1)
            sp.dma_start(slots_dram[0:TRASH, :].rearrange("(p c) a -> p (c a)", p=P),
                         slotZ[:, :]).then_inc(s_table, 16)
            for name, dst in (("L0_mix_Wq", Wq), ("L0_mix_Wk", Wk), ("L0_mix_Wv", Wv), ("L0_mix_Wfc", Wfc),
                              ("L0_gnn_W0_0", W0s), ("L0_gnn_W1_0", W1s),
                              ("L0_gnn_W1_1", Wc[:, :, 0:D]), ("L0_gnn_W0_1", Wc[:, :, D:2 * D])):
                sp.dma_start(dst, io[name].rearrange("(k p) n -> p k n", p=P)).then_inc(s_w, 16)
            for name, r in (("L0_mix_bk", BK), ("L0_mix_bv", BV), ("L0_mix_bfc", BFC),
                            ("L0_gnn_b0_1", B01), ("L0_gnn_b1_1", B11)):
                sp.dma_start(rows[0:1, r, :], io[name].rearrange("(a n) -> a n", a=1)).then_inc(s_w, 16)
            sp.dma_start(bqc, io["L0_mix_bq"].rearrange("(k p) -> p k", p=P)).then_inc(s_w, 16)
            sp.dma_start(bh[:, 0, :], io["L0_gnn_b0_0"].rearrange("(k p) -> p k", p=P)).then_inc(s_w, 16)
            sp.dma_start(bh[:, 1, :], io["L0_gnn_b1_0"].rearrange("(k p) -> p k", p=P)).then_inc(s_w, 16)
            xv = io["x"][0:(T - 1) * P, :].rearrange("(t p) c -> p t c", p=P)
            xiv = xin.rearrange("p (t c) -> p t c", c=D)
            sp.dma_start(rows[0:1, 8, 0:D], io["L0_mix_bk"].rearrange("(a n) -> a n", a=1)).then_inc(s_xT, 16)
            sp.dma_start(xiv, xv[:, 0:W, :]).then_inc(s_x, 16)
            with sp.Fori(1, T // W - 1) as b:
                sp.wait_ge(s_xn, b * W)
                sp.dma_start(xiv, io["x"][bass.ds(b * (W * P), W * P), :].rearrange("(t p) c -> p t c", p=P))\
                  .then_inc(s_x, 16)
                sp.wait_ge(s_xp, b)
                sp.dma_start(xT_dram[bass.ds(b - 1, 1), :, :].rearrange("a p c -> (a p) c"), xst).then_inc(s_xT, 16)
            sp.wait_ge(s_xn, T - W)
            sp.dma_start(xiv[:, 0:W - 1, :], xv[:, T - W:T - 1, :]).then_inc(s_x, 16)
            sp.dma_start(xiv[0:LAST, W - 1, :], io["x"][(T - 1) * P:N, :]).then_inc(s_x, 16)
            sp.dma_start(xiv[LAST:P, W - 1, :], zeros32[LAST:P, :]).then_inc(s_x, 16)
            for b in (T // W - 2, T // W - 1):
                sp.wait_ge(s_xp, b + 1)
                sp.dma_start(xT_dram[b, :, :], xst).then_inc(s_xT, 16)
            sp.wait_ge(s_sc[0], 16 * G * (GROUPS // 2))
            sp.wait_ge(s_sc[1], 16 * G * (GROUPS // 2))
            sp.wait_ge(s_vm, 12)
            sp.wait_ge(s_pm, 10)
            sp.wait_ge(s_sr, 1)
            sp.wait_ge(s_xT, 16 + 16 * (T // W))
            sp.dma_start(slotI, slots_dram[0:TRASH, :].rearrange("(p c) a -> p (c a)", p=P)).then_inc(s_slot, 16)
            def load4(g, par):
                sp.dma_start(xT4[par], xT_dram[bass.ds(g, 1), :, :].rearrange("a p c -> (a p) c")).then_inc(s_x4[par], 16)

            sp.wait_ge(s_ac, 1 + T)
            load4(0, 0)
            load4(1, 1)
            with sp.Fori(1, T // W // 2) as k:
                for par in range(2):
                    sp.wait_ge(s_yp, k * (2 * W) + par * W)
                    load4(2 * k + par, par)
            sp.wait_ge(s_yp, T - W)
            load4(T // W - 1, 0)
            sp.wait_ge(s_yp, W + T)
            sp.wait_ge(s_wst, 16 * EXPERTS)
            for e in range(6, EXPERTS):
                sp.dma_start(wslot[e], w_dram[e, :, :]).then_inc(s_we[e], 16)
            sp.dma_start(graw, io["L0_ffn_Wg"].rearrange("(k p) n -> p k n", p=P)).then_inc(s_gl, 16)
            sp.dma_start(xres, io["x"][0:P, :]).then_inc(s_xr, 16)
            with sp.Fori(1, T - 1) as t:
                sp.wait_ge(s_xrf, t + 1)
                sp.dma_start(xres, io["x"][bass.ds(t * P, P), :]).then_inc(s_xr, 16)
                sp.dma_start(x2_dram[bass.ds(t * P - P, P), :], x2b).then_inc(s_x2, 16)
            sp.wait_ge(s_xrf, T)
            sp.dma_start(xres[0:LAST, :], io["x"][(T - 1) * P:N, :]).then_inc(s_xr, 16)
            sp.dma_start(x2_dram[(T - 2) * P:(T - 1) * P, :], x2b).then_inc(s_x2, 16)
            sp.wait_ge(s_xrf, T + 1)
            sp.dma_start(x2_dram[(T - 1) * P:T * P, :], x2b).then_inc(s_x2, 16)
            sp.wait_ge(s_ap[1], Q + T * Q)
            for e in range(6):
                sp.dma_start(wslot[e], w_dram[e, :, :]).then_inc(s_we[e], 16)
            sp.wait_ge(s_lp, T)
            sp.wait_ge(s_lr, 1 + T)
            sp.wait_ge(s_x2, 16 * T)
            for r, name in enumerate(("L0_ffn_bg", "L0_ffn_bias")):
                sp.dma_start(grows[0:1, r, :], io[name].rearrange("(a n) -> a n", a=1)).then_inc(s_wg, 16)
            sp.dma_start(b2s[0:EXPERTS, :], io["L0_ffn_b2"]).then_inc(s_st, 16)
            sp.dma_start(xr5, x2_dram[0:W * P, :].rearrange("(t p) c -> p t c", p=P)).then_inc(s_xr5, 16)
            with sp.Fori(1, T // W) as g:
                sp.wait_ge(s_ai, 4 * g)
                sp.dma_start(xr5, x2_dram[bass.ds(g * (W * P), W * P), :].rearrange("(t p) c -> p t c", p=P))\
                  .then_inc(s_xr5, 16)
                sp.wait_ge(s_da, g * 32 + 4)
                sp.dma_start(io["out"][bass.ds(g * (W * P) - W * P, W * P), :].rearrange("(t p) c -> p t c", p=P),
                             acc).then_inc(s_st, 16)
            sp.wait_ge(s_da, 4 + 32 * (T // W))
            sp.dma_start(io["out"][(T - W) * P:(T - 1) * P, :].rearrange("(t p) c -> p t c", p=P),
                         acc[:, 0:W - 1, :]).then_inc(s_o5, 16)
            sp.dma_start(io["out"][(T - 1) * P:N, :], acc[0:LAST, W - 1, :]).then_inc(s_o5, 16)
            sp.wait_ge(s_st, 16 * (T // W))
            sp.wait_ge(s_o5, 32)

        @block.gpsimd
        def _(pool):
            allow = dict(allow_small_or_imprecise_dtypes=True)
            nc.gpsimd.iota(iota128[:, :, :], [[1, P], [0, G]], base=0, channel_multiplier=0, **allow)
            nc.gpsimd.iota(iota49[:, :, :], [[1, T], [0, G]], base=0, channel_multiplier=0, **allow)
            nc.gpsimd.iota(iotaB[:, :, :], [[1, P], [0, QB]], base=1, channel_multiplier=0, **allow)
            nc.gpsimd.iota(trash[:, :], [[1, EP]], base=TRASH, channel_multiplier=EP)
            nc.gpsimd.iota(iota8[:, :], [[1, 8]], base=0, channel_multiplier=0, **allow)
            nc.gpsimd.iota(zrow[:, :], [[0, 1]], base=OVROW, channel_multiplier=1, **allow)
            nc.gpsimd.memset(zeros32[:, :], 0.0)
            nc.gpsimd.memset(zeros16[:, :], 0.0)
            nc.gpsimd.memset(ident[:, :], 0.0)
            nc.gpsimd.memset(ident16[:, :], 0.0)
            nc.gpsimd.memset(ones[:, :], 1.0)
            nc.gpsimd.memset(epsc[:, :], EPS)
            nc.gpsimd.memset(neg4[:, :, :], -1.0)
            nc.gpsimd.memset(hmask, 1.0)
            pool.drain()
            for m in (ident, ident16):
                nc.gpsimd.affine_select(out=m[:, :], in_=m[:, :], compare_op=ALU.not_equal, fill=1.0,
                                        base=0, pattern=[[-1, P]], channel_multiplier=1)
            nc.gpsimd.affine_select(out=neg4[:, :, :], in_=neg4[:, :, :], compare_op=ALU.is_ge, fill=0.0,
                                    base=0, pattern=[[0, 4], [-1, P]], channel_multiplier=1)
            hv = hmask.rearrange("p k (b c) -> p k b c", c=D // HEADS)
            nc.gpsimd.affine_select(out=hv, in_=hv, compare_op=ALU.is_ge, fill=0.0, base=0,
                                    pattern=[[P, 2], [-(D // HEADS), HEADS], [0, D // HEADS]], channel_multiplier=1)
            pool.drain()
            nc.gpsimd.affine_select(out=hv, in_=hv, compare_op=ALU.is_ge, fill=0.0, base=D // HEADS - 1,
                                    pattern=[[-P, 2], [D // HEADS, HEADS], [0, D // HEADS]],
                                    channel_multiplier=-1).then_inc(s_const, 1)
            pool.wait_ge(s_table, 16)

            def scatter(k, par, first):
                g = 2 * k + par
                pool.wait_ge(s_pos, g + 1)
                if not first:
                    pool.wait_ge(s_sc[par], 16 * G * k)
                nc.gpsimd.tensor_copy(stP[par][:, :], posI[:, bass.ds(g * G, G)])
                nc.gpsimd.tensor_copy(stR[par][:, :], rec[:, bass.ds(g * G, G)]).then_inc(s_stage, 1)
                pool.wait_ge(s_stage, g + 1)
                nc.gpsimd.tensor_tensor(pwait[:, 0:1], ones[:, 0:1], ones[:, 0:1], ALU.add)
                for c in range(G):
                    pool.indirect_dma_start(
                        out=slots_dram, out_offset=bass.IndirectOffsetOnAxis(ap=stP[par][:, c:c + 1], axis=0),
                        in_=stR[par][:, c:c + 1], in_offset=None).then_inc(s_sc[par], 16)

            scatter(0, 0, True)
            scatter(0, 1, True)
            with pool.Fori(1, GROUPS // 2) as k:
                scatter(k, 0, False)
                scatter(k, 1, False)
            pool.wait_ge(s_flag, 2)
            for i, ends in enumerate((eS, eD)):
                pool.dma_start(ends_dram[i, :, :], ends).then_inc(s_ends, 16)
            pool.wait_ge(s_ends, 32)
            nc.gpsimd.memset(R3[:, :], 0.0).then_inc(s_r3, 1)

            def wait(s, n):
                pool.drain()
                pool.wait_ge(s, n)
                nc.gpsimd.tensor_tensor(pwait[:, 0:1], ones[:, 0:1], ones[:, 0:1], ALU.add)

            def overflow(L):
                pool.dma_start(feat_dram[0:T * P, :].rearrange("(t p) c -> p t c", p=P),
                               R2[:, :].rearrange("p (t c) -> p t c", t=T)).then_inc(s_of[L], 16)
                pool.dma_start(feat_dram[T * P:(T + 1) * P, :], zeros32[:, :].bitcast(F16)).then_inc(s_of[L], 16)
                for i in range(2):
                    pool.dma_start(sum_dram[:, i * D:(i + 1) * D].rearrange("(t p) c -> p t c", p=P),
                                   zeros32[:, :].rearrange("p (a c) -> p a c", a=1).to_broadcast([P, T + 2, D]))\
                        .then_inc(s_of[L], 16)
                wait(s_of[L], 64)
                with pool.Fori(0, E) as c:
                    for i in range(2):
                        m = 2 * c + i
                        pool.dma_start(oa, ends_dram[i, :, bass.ds(c, 1)]).then_inc(s_oi[L], 16)
                        pool.dma_start(ob, ends_dram[1 - i, :, bass.ds(c, 1)]).then_inc(s_oj[L], 16)
                        wait(s_oi[L], m * 16 + 16)
                        wait(s_oj[L], m * 16 + 16)
                        pool.indirect_dma_start(out=oX, out_offset=None, in_=feat_dram,
                                                in_offset=bass.IndirectOffsetOnAxis(ap=oa, axis=0)).then_inc(s_ox[L], 16)
                        pool.indirect_dma_start(out=oA, out_offset=None, in_=sum_dram,
                                                in_offset=bass.IndirectOffsetOnAxis(ap=ob, axis=0)).then_inc(s_oy[L], 16)
                        wait(s_o5v[L], m + 1)
                        pool.indirect_dma_start(out=sum_dram, out_offset=bass.IndirectOffsetOnAxis(ap=ow, axis=0),
                                                in_=oN, in_offset=None).then_inc(s_os[L], 16)
                        wait(s_os[L], m * 16 + 16)
                with pool.Fori(0, T) as t:
                    pool.dma_start(oA, sum_dram[bass.ds(t * P, P), :]).then_inc(s_ol[L], 16)
                    wait(s_o6[L], t + 1)

            lacking = pool.value_load(flag[0:1, 0:1])
            pool.wait_ge(s_xlo, 1 + T)
            pool.wait_ge(s_tabs, 1)
            with pool.If(lacking > 0):
                overflow(0)
            pool.wait_ge(s_ac, 1 + T)

            def expert(e, first):
                if not first:
                    wait(s_wst, e * 16)
                if first:
                    w1s, w2s, b1s = (io[f"L0_ffn_{n}"][0:1] for n in ("W1", "W2", "b1"))
                else:
                    w1s, w2s, b1s = (io[f"L0_ffn_{n}"][bass.ds(e, 1)] for n in ("W1", "W2", "b1"))
                pool.dma_start(wraw[:, 0:2 * F].rearrange("p (k n) -> p k n", k=2),
                               w1s.rearrange("a (k p) n -> p (a k) n", p=P)).then_inc(s_wl, 16)
                pool.dma_start(wraw[:, 2 * F:4 * F].rearrange("p (k n) -> p k n", k=4),
                               w2s.rearrange("a (k p) n -> p (a k) n", p=P)).then_inc(s_wl, 16)
                pool.dma_start(braw, b1s.rearrange("a (f p) -> p (a f)", p=P)).then_inc(s_wl, 16)
                wait(s_wq, e + 1)
                nc.gpsimd.partition_all_reduce(nr3, sq3, P, RADD).then_inc(s_wr, 1)
                wait(s_wh, e + 1)
                wait(s_wo, e + 1)
                dst = w_dram[0, :, :] if first else w_dram[bass.ds(e, 1), :, :].rearrange("a p c -> (a p) c")
                pool.dma_start(dst, wout).then_inc(s_wst, 16)

            expert(0, True)
            with pool.Fori(1, EXPERTS) as e:
                expert(e, False)
            pool.wait_ge(s_yl, 1 + T)
            pool.wait_ge(s_zc, 3 + T)
            with pool.If(lacking > 0):
                overflow(1)

        @block.vector
        def _(dve):
            v = nc.vector
            v.memset(R3i[:, 0:2 * EP], PADNODE)
            v.memset(Tsn[0], 0.0)
            v.memset(Tsn[1], 0.0).then_inc(s_blank, 1)
            v.memset(slotZ, 0).then_inc(s_zero, 1)
            v.memset(small[:, 0:1], 0.0).then_inc(s_t, 1)
            v.memset(small[:, 1:2], 0.0).then_inc(s_rk, 1)
            v.memset(small[:, 2:3], 0.0).then_inc(s_xtc, 1)
            v.memset(small[:, 3:4], 0.0).then_inc(s_ac, 1)
            v.memset(small[:, 4:5], 0.0).then_inc(s_an[0], 1)
            v.memset(small[:, 5:6], 0.0).then_inc(s_an[1], 1)
            v.memset(small[:, 6:7], 0.0).then_inc(s_zc, 3)
            v.memset(small[:, 7:8], 0.0).then_inc(s_xrf, 1)
            v.memset(small[:, 8:9], 0.0).then_inc(s_da, 4)
            v.memset(small[:, 9:10], 0.0).then_inc(s_us, 4)
            v.memset(small[:, 11:12], 0.0).then_inc(s_lr, 1)
            dve.wait_ge(s_edges, 96)
            v.tensor_tensor(eHi, eS, eD, ALU.max)
            v.tensor_tensor(eLo, eS, eD, ALU.min)
            dve.drain()
            v.tensor_scalar(eTi, eHi, 7, None, ALU.logical_shift_right)
            v.tensor_scalar(eTj, eLo, 7, None, ALU.logical_shift_right)
            dve.drain()
            v.tensor_scalar(eHi, eHi, P - 1, None, ALU.bitwise_and)
            v.tensor_scalar(eLo, eLo, P - 1, None, ALU.bitwise_and)
            v.tensor_copy(fTi, eTi)
            v.tensor_copy(fTj, eTj)
            dve.drain()
            v.tensor_copy(fHi, eHi)
            v.tensor_copy(fLo, eLo)
            v.scalar_tensor_tensor(out=rec, in0=eHi, scalar=256.0, in1=eLo, op0=ALU.mult, op1=ALU.add)
            v.scalar_tensor_tensor(out=binb, in0=eTi, scalar=float(T), in1=eTj, op0=ALU.mult, op1=ALU.add)
            v.tensor_tensor(diag, eTi, eTj, ALU.is_equal)
            v.tensor_scalar(delta, eTi, -float(T), float(BINS), ALU.mult, ALU.add)
            v.tensor_scalar(inval, eTi, float(T), None, ALU.is_ge)
            dve.drain()
            v.tensor_scalar(rec, rec, 257.0, None, ALU.add)
            dve.drain()
            dve.wait_ge(s_const, 1)

            def onehots(par, g):
                dve.wait_ge(s_r, g + 1)
                for out, key, pat, m in ((OHi, fTi, iota49, T), (OHj, fTj, iota49, T),
                                         (LHi, fHi, iota128, P), (LLo, fLo, iota128, P)):
                    kb = key[:, bass.ds(g * G, G)].rearrange("p (a b) -> p a b", a=1).to_broadcast([P, m, G])
                    last = v.tensor_tensor(out[par], pat[:, :, :], kb, ALU.is_equal)
                last.then_inc(s_oh, 1)

            def counts(par, g):
                dve.wait_ge(s_h, g + 1)
                v.tensor_copy(Tsn[par][0:T, 0, :], Tsn[1 - par][0:T, G, :])
                t0 = Tsn[1 - par][0:T, G, :].rearrange("p (a j) -> p a j", a=1).to_broadcast([T, G, T])
                v.scalar_tensor_tensor(out=Tsn[par][0:T, 1:G + 1, :], in0=t0, scalar=1024.0,
                                       in1=banks[3][0:T, 0:G * T].rearrange("p (g j) -> p g j", j=T),
                                       op0=ALU.min, op1=ALU.add).then_inc(s_t, 1)

            def ranks(par, g):
                sl = bass.ds(g * G, G)
                dve.wait_ge(s_r, g + 3)
                v.tensor_tensor(prod, banks[4][:, 0:G * T].rearrange("p (g j) -> p g j", j=T),
                                OHj[par].rearrange("p j g -> p g j"), ALU.mult).then_inc(s_rk, 1)
                dve.drain()
                v.tensor_reduce(rank[:, sl], prod, AX.X, ALU.add)
                dve.drain()
                v.scalar_tensor_tensor(out=d1, in0=rank[:, sl], scalar=float(P), in1=diag[:, sl],
                                       op0=ALU.is_ge, op1=ALU.mult)
                dve.drain()
                v.scalar_tensor_tensor(out=rr, in0=d1, scalar=-float(P), in1=rank[:, sl],
                                       op0=ALU.mult, op1=ALU.add)
                v.tensor_tensor(ee, d1, delta[:, sl], ALU.mult)
                dve.drain()
                v.tensor_tensor(bb, ee, binb[:, sl], ALU.add)
                v.scalar_tensor_tensor(out=ov, in0=rr, scalar=float(P), in1=inval[:, sl],
                                       op0=ALU.is_ge, op1=ALU.max)
                dve.drain()
                v.tensor_copy(delta[:, sl], ov)
                v.scalar_tensor_tensor(out=pp, in0=rr, scalar=float(COLS), in1=bb, op0=ALU.mult, op1=ALU.add)
                dve.drain()
                v.scalar_tensor_tensor(out=tq, in0=pp, scalar=-1.0, in1=trash[:, sl], op0=ALU.mult, op1=ALU.add)
                dve.drain()
                v.tensor_tensor(tr, tq, ov, ALU.mult)
                dve.drain()
                v.tensor_tensor(posI[:, sl], tr, pp, ALU.add).then_inc(s_pos, 1)

            onehots(0, 0)
            with dve.Fori(0, GROUPS // 2) as k:
                for par in range(2):
                    g = 2 * k + par
                    onehots(1 - par, g + 1)
                    counts(par, g)
                    ranks(par, g)

            for i in range(W):
                v.memset(xs[i][:, D:D + 1], 1.0)

            def stats_of(b, need):
                dve.wait_ge(s_x, need)
                for i in range(W):
                    v.bn_stats(stats[:, i, :], xin[:, i * D:(i + 1) * D])
                dve.drain()
                for i in range(W):
                    v.bn_aggr(mv[:, i, :], stats[:, i, :])
                dve.drain()
                v.tensor_copy(rstd[:, 0:W], mv[:, 0:W, 1]).then_inc(s_stat, 1)
                dve.wait_ge(s_std, b + 1)
                v.reciprocal(rstd[:, 0:W], rstd[:, 0:W])
                dve.drain()
                dve.wait_ge(s_xT, 16 * b + 16)
                for i in range(W):
                    t = b * W + i
                    dve.wait_ge(s_xt, t + 1)
                    dve.wait_ge(s_xlo, t + 1)
                    v.tensor_scalar(xs[i][:, 0:D], xin[:, i * D:(i + 1) * D], mv[:, i, 0:1],
                                    rstd[:, i:i + 1], ALU.subtract, ALU.mult).then_inc(s_xn, 1)
                    dve.wait_ge(s_xhi, t + 1)
                    v.scalar_tensor_tensor(out=xlo[0], in0=xs[i][:, 0:D], scalar=S,
                                           in1=R2[:, bass.ds(t * 2 * D, D)],
                                           op0=ALU.mult, op1=ALU.subtract).then_inc(s_xl, 1)
                    dve.wait_ge(s_xt, t + 1 + W)
                    v.tensor_copy(xst[:, i * D:(i + 1) * D], banks[0][:, 0:D]).then_inc(s_xtc, 1)
                dve.drain()
                v.memset(small[:, 10:11], 0.0).then_inc(s_xp, 1)

            with dve.Fori(0, T // W - 1) as b:
                stats_of(b, 16 * b + 16)
            stats_of(T // W - 1, 16 * (T // W + 2))

            def copied(ins):
                ins.then_inc(s_vm, 1)

            def k2(ap):
                return ap.rearrange("p (k n) -> p k n", k=2)

            dve.wait_ge(s_pm, 1)
            v.tensor_copy(Gs[:, 0, :], banks[6][:, 0:D + 1])
            copied(v.tensor_copy(Gs[:, 1, :], banks[7][:, 0:D + 1]))
            for i, dst in enumerate((WkT, WvT, WfT)):
                dve.wait_ge(s_pm, 2 + i)
                copied(v.tensor_copy(dst, k2(banks[i][:, :])))
            dve.wait_ge(s_pm, 5)
            v.tensor_copy(B1s, k2(banks[3][:, :]))
            v.tensor_copy(rows[0:1, SV, :], banks[4][0:1, 0:D])
            copied(v.scalar_tensor_tensor(out=rows[0:1, SK, :], in0=rows[0:1, BK, :], scalar=float(N),
                                          in1=banks[4][0:1, D:2 * D], op0=ALU.mult, op1=ALU.add))
            dve.wait_ge(s_pm, 6)
            copied(v.scalar_tensor_tensor(out=PTs, in0=k2(banks[0][:, :]), scalar=1.0 / N, in1=hmask,
                                          op0=ALU.mult, op1=ALU.mult))
            dve.wait_ge(s_pm, 7)
            copied(v.tensor_copy(Rs, k2(banks[1][:, :])))
            dve.wait_ge(s_pm, 8)
            v.tensor_copy(Ms[:, :, :], k2(banks[2][:, :]))
            v.tensor_tensor(rows[0:1, ZB, :], banks[3][0:1, 0:D], rows[0:1, BFC, :], ALU.add)
            v.tensor_tensor(bhs[:, :], bh[:, 0, :], bh[:, 1, :], ALU.add)
            dve.drain()
            v.tensor_tensor(rows[0:1, SPARE, :], rows[0:1, ZB, :], rows[0:1, B01, :], ALU.add)
            dve.drain()
            copied(v.tensor_tensor(rows[0:1, ZB, :], rows[0:1, SPARE, :], rows[0:1, B11, :], ALU.add))
            dve.wait_ge(s_pm, 9)
            copied(v.tensor_copy(zb[:, :], banks[4][:, 0:D]))
            copied(v.tensor_copy(degT[0:T, :], banks[5][0:T, 0:P]))
            dve.wait_ge(s_pm, 10)
            v.tensor_scalar(deg[:, :], banks[1][:, 0:T], 1.0, None, ALU.max)
            dve.drain()
            copied(v.reciprocal(rdeg[:, :], deg[:, :]))
            dve.drain()
            copied(v.tensor_scalar(rd1[:, :], rdeg[:, :], 1.0 / S, None, ALU.mult))

            dve.wait_ge(s_sr, 1)
            v.tensor_tensor(small[:, 44:45], small[:, 40:41], small[:, 41:42], ALU.add)
            dve.drain()
            v.scalar_tensor_tensor(out=small[:, 45:46], in0=small[:, 44:45], scalar=float(D) ** 0.5,
                                   in1=small[:, 42:43], op0=ALU.mult, op1=ALU.add)
            dve.drain()
            v.tensor_tensor(small[:, 46:47], small[:, 45:46], small[:, 43:44], ALU.mult)
            dve.drain()
            v.tensor_scalar(small[:, 47:48], small[:, 46:47], 2.0 ** -100, 2.0 ** 120, ALU.max, ALU.min)
            dve.drain()
            v.tensor_scalar(smalli[:, 48:49], smalli[:, 47:48], 23, None, ALU.logical_shift_right)
            dve.drain()
            v.tensor_scalar(smalli[:, 49:50], smalli[:, 48:49], -1.0, 267.0, ALU.mult, ALU.add)
            v.tensor_scalar(smalli[:, 50:51], smalli[:, 48:49], -13.0, None, ALU.add)
            dve.drain()
            v.tensor_scalar(smalli[:, 51:53], smalli[:, 49:51], 23, None, ALU.logical_shift_left)
            dve.drain()
            v.tensor_scalar(Wc[:, :, 0:D], Wc[:, :, 0:D], small[:, 51:52], None, ALU.mult)
            v.tensor_scalar(rd2[:, :], rdeg[:, :], small[:, 52:53], None, ALU.mult).then_inc(s_sc2, 1)

            v.tensor_tensor(rank, delta, inval, ALU.subtract)
            dve.drain()
            v.tensor_reduce(small[:, 56:57], rank[:, 0:E], AX.X, ALU.add)
            v.memset(rank[:, E:EP], 0.0)
            for ends, t1, t2 in ((eS, binb, diag), (eD, delta, inval)):
                v.tensor_scalar(t1, ends, zrow[:, 0:1], None, ALU.subtract)
                dve.drain()
                v.tensor_tensor(t2, t1, rank, ALU.mult)
                dve.drain()
                v.tensor_scalar(ends, t2, zrow[:, 0:1], None, ALU.add)
            dve.drain()
            v.memset(small[:, 57:58], 0.0).then_inc(s_flag, 1)
            dve.wait_ge(s_fp, 1)
            v.tensor_copy(flag[:, :], banks[2][:, 0:1]).then_inc(s_flag, 1)

            dve.wait_ge(s_slot, 16)
            v.tensor_scalar(hiI, slotI, 8, None, ALU.logical_shift_right)
            dve.drain()
            v.tensor_copy(HI, hiI)
            v.tensor_scalar(slotI, slotI, 255, None, ALU.bitwise_and)
            dve.drain()
            v.tensor_copy(LO, slotI)
            v.memset(TT[:, T * TC:(T + 1) * TC], 0.0)
            v.memset(TU[:, T * TC:(T + 1) * TC], 0.0)
            dve.drain()
            tv, uv = (x[:, 0:T * TC].rearrange("p (t u) -> p t u", u=TC) for x in (TT, TU))
            hv, lv = (x[:, 0:BINS].rearrange("p (t u) -> p t u", u=T) for x in (HI, LO))
            v.tensor_tensor(tv[:, :, 0:T], hv, lv.rearrange("p t u -> p u t"), ALU.max)
            v.tensor_tensor(uv[:, :, 0:T], lv, hv.rearrange("p t u -> p u t"), ALU.max)
            dve.drain()
            hd, ld = (x[:, 0:BINS:T + 1] for x in (HI, LO))
            v.tensor_copy(TT[:, 0:T * TC:TC + 1], hd)
            v.tensor_copy(TU[:, 0:T * TC:TC + 1], ld)
            v.tensor_copy(tv[:, :, T], ld)
            v.tensor_copy(uv[:, :, T], hd)
            v.tensor_copy(tv[:, :, T + 1], HI[:, BINS:COLS])
            v.tensor_copy(uv[:, :, T + 1], LO[:, BINS:COLS])
            v.tensor_copy(tv[:, :, T + 2], LO[:, BINS:COLS])
            v.tensor_copy(uv[:, :, T + 2], HI[:, BINS:COLS])
            dve.drain()
            v.memset(small[:, 10:11], 0.0).then_inc(s_tabs, 1)

            def pairs(L, n, q, col):
                dve.wait_ge(s_bl[L], n + 1)
                for out, tab in ((OT, TT), (OU, TU)):
                    kb = tab[:, bass.ds(col, QB)].rearrange("p (a b) -> p a b", a=1).to_broadcast([P, P, QB])
                    last = v.tensor_tensor(out[q], iotaB[:, :, :], kb, ALU.is_equal)
                last.then_inc(s_oo[L], 1)

            def finish1(t):
                dve.wait_ge(s_ag[0], t + 3)
                v.scalar_tensor_tensor(out=aggc, in0=aggr[:, D:2 * D], scalar=1.0 / S, in1=aggr[:, 0:D],
                                       op0=ALU.mult, op1=ALU.add)
                dve.drain()
                v.scalar_tensor_tensor(out=aggn, in0=aggc, scalar=rd1[:, bass.ds(t, 1)],
                                       in1=R3[:, bass.ds(t * D, D)],
                                       op0=ALU.mult, op1=ALU.add).then_inc(s_an[0], 1)

            def place1(t):
                dve.wait_ge(s_at, t + 1)
                v.tensor_copy(R3[:, bass.ds(t * D, D)], banks[6][:, 0:D]).then_inc(s_ac, 1)

            def finish2(t):
                dve.wait_ge(s_ag[1], t + 3)
                v.scalar_tensor_tensor(out=aggc, in0=aggr[:, D:2 * D], scalar=1.0 / S, in1=aggr[:, 0:D],
                                       op0=ALU.mult, op1=ALU.add)
                dve.drain()
                v.scalar_tensor_tensor(out=aggn, in0=aggc, scalar=rd2[:, bass.ds(t, 1)],
                                       in1=R3[:, bass.ds(t * D, D)],
                                       op0=ALU.mult, op1=ALU.add).then_inc(s_an[1], 1)
                dve.drain()
                dve.wait_ge(s_xr, t * 16 + 16)
                v.tensor_tensor(x2b, aggn, xres, ALU.add).then_inc(s_xrf, 1)
                dve.drain()
                v.bn_stats(x2s, x2b)
                dve.drain()
                v.bn_aggr(x2m, x2s).then_inc(s_v2, 1)

            def normal2(t):
                dve.wait_ge(s_d2, t + 1)
                v.reciprocal(x2r, x2r)
                dve.drain()
                v.tensor_scalar(x2n, x2b, x2m[:, 0:1], x2r, ALU.subtract, ALU.mult).then_inc(s_n2, 1)

            def low2(t):
                dve.wait_ge(s_h2, t + 1)
                v.scalar_tensor_tensor(out=R3t(t, 1), in0=banks[6][:, 0:D], scalar=S, in1=R3t(t, 0),
                                       op0=ALU.mult, op1=ALU.subtract).then_inc(s_l2, 1)

            def logits2(t):
                dve.wait_ge(s_lp, t + 1)
                v.tensor_reduce(LG[:, bass.ds(t, 1), :], banks[6][:, D:D + 24].rearrange("p (g a n) -> p a n g", g=3, a=1),
                                AX.X, ALU.add).then_inc(s_lr, 1)

            def overflow(L, rd):
                with dve.Fori(0, E) as c:
                    for i in range(2):
                        m = 2 * c + i
                        dve.wait_ge(s_oj[L], m * 16 + 16)
                        v.tensor_copy(obf, ob)
                        dve.drain()
                        v.tensor_copy(oB, obf.to_broadcast([P, P])).then_inc(s_o1[L], 1)
                        dve.wait_ge(s_o2[L], m + 1)
                        v.tensor_scalar(oSel, banks[0][:, 0:P], obf, None, ALU.is_equal).then_inc(s_o3[L], 1)
                        dve.drain()
                        v.tensor_tensor(oM, oSel, neg4[:, 0, :], ALU.mult)
                        dve.drain()
                        v.tensor_reduce(oc, oM, AX.X, ALU.add)
                        v.scalar_tensor_tensor(out=od, in0=zrow[:, 0:1], scalar=float(P), in1=obf,
                                               op0=ALU.add, op1=ALU.subtract)
                        dve.drain()
                        v.scalar_tensor_tensor(out=oe, in0=oc, scalar=-1.5, in1=od, op0=ALU.is_lt, op1=ALU.mult)
                        dve.drain()
                        v.tensor_tensor(ow, oe, obf, ALU.add)
                        dve.wait_ge(s_oy[L], m * 16 + 16)
                        dve.wait_ge(s_o4[L], m + 1)
                        v.tensor_tensor(oN, banks[1][:, :], oA, ALU.add).then_inc(s_o5v[L], 1)
                with dve.Fori(0, T) as t:
                    dve.wait_ge(s_ol[L], t * 16 + 16)
                    v.scalar_tensor_tensor(out=oN[:, 0:D], in0=oA[:, D:2 * D], scalar=1.0 / S, in1=oA[:, 0:D],
                                           op0=ALU.mult, op1=ALU.add)
                    dve.drain()
                    v.scalar_tensor_tensor(out=oN[:, D:2 * D], in0=oN[:, 0:D], scalar=rd[:, bass.ds(t, 1)],
                                           in1=R3[:, bass.ds(t * D, D)], op0=ALU.mult, op1=ALU.add)
                    dve.drain()
                    v.tensor_copy(R3[:, bass.ds(t * D, D)], oN[:, D:2 * D]).then_inc(s_o6[L], 1)
                dve.drain()

            dve.wait_ge(s_r3, 1)
            dve.drain()
            lacking = dve.value_load(flag[0:1, 0:1])
            with dve.If(lacking > 0):
                overflow(0, rd1)

            for q in range(Q):
                pairs(0, q, q, q * QB)
            for q in range(Q):
                pairs(0, Q + q, q, TC + q * QB)
            finish1(0)
            with dve.Fori(1, T) as t:
                for q in range(Q):
                    pairs(0, (t + 1) * Q + q, q, (t + 1) * TC + q * QB)
                place1(t - 1)
                finish1(t)
            place1(T - 1)

            def tile4(n, i):
                dve.wait_ge(s_yh, n + 1)
                bank = banks[Y4(i)]
                v.tensor_tensor(R3[:, bass.ds(n * D, D)], bank[:, D:2 * D], zb[:, :], ALU.add)
                dve.wait_ge(s_yl, n + 1)
                v.tensor_tensor(ylo[0], bank[:, 0:D], R2[:, bass.ds(n * 2 * D, D)],
                                ALU.subtract).then_inc(s_zc, 1)

            def scales(e):
                dve.wait_ge(s_wt, e + 1)
                v.tensor_copy(nv3[:, 0:2], nr3[:, 0:2])
                v.scalar_tensor_tensor(out=nv3[:, 2:3], in0=nr3[:, 0:1], scalar=float(D) ** 0.5, in1=nr3[:, 2:3],
                                       op0=ALU.mult, op1=ALU.add)
                dve.drain()
                v.tensor_scalar(cl3, nv3, 2.0 ** -60, None, ALU.max)
                dve.drain()
                v.tensor_scalar(ex3, cl3.bitcast(I32), 23, None, ALU.logical_shift_right)
                dve.drain()
                v.tensor_scalar(ab6[:, 0:3], ex3, -1.0, 267.0, ALU.mult, ALU.add)
                v.tensor_scalar(ab6[:, 3:6], ex3, -13.0, None, ALU.add)
                dve.drain()
                v.tensor_scalar(sc6, ab6, 23, None, ALU.logical_shift_left)
                dve.drain()
                sf = sc6.bitcast(F32)
                v.scalar_tensor_tensor(out=iscA[:, bass.ds(e, 1)], in0=sf[:, 2:3], scalar=1.0 / S, in1=sf[:, 3:4],
                                       op0=ALU.mult, op1=ALU.mult)
                v.scalar_tensor_tensor(out=csA[:, bass.ds(e, 1)], in0=sf[:, 5:6], scalar=1.0, in1=sf[:, 4:5],
                                       op0=ALU.mult, op1=ALU.mult)
                v.tensor_scalar(b1A[:, bass.ds(e * 4, 4)], braw, sf[:, 2:3], None, ALU.mult).then_inc(s_wc, 1)

            def lows(e):
                dve.wait_ge(s_wh, e + 1)
                sf = sc6.bitcast(F32)
                for j in range(2):
                    last = v.scalar_tensor_tensor(
                        out=wout[:, (2 * j + 1) * 2 * F:(2 * j + 2) * 2 * F], in0=wraw[:, j * 2 * F:(j + 1) * 2 * F],
                        scalar=sf[:, j:j + 1], in1=wout[:, 2 * j * 2 * F:(2 * j + 1) * 2 * F],
                        op0=ALU.mult, op1=ALU.subtract)
                last.then_inc(s_wo, 1)

            scales(0)
            lows(0)
            with dve.Fori(0, T // W) as g:
                for i in range(W):
                    tile4(g * W + i, i)
                    if i == 2:
                        scales(g + 1)
                    if i == 4:
                        lows(g + 1)

            dve.wait_ge(s_gl, 16)
            v.tensor_copy(gpart[:, :, 0, :], graw)
            dve.drain()
            v.tensor_tensor(gres, graw, gpart[:, :, 0, :], ALU.subtract)
            dve.drain()
            v.tensor_copy(gpart[:, :, 1, :], gres)
            dve.drain()
            v.tensor_tensor(gres2, gres, gpart[:, :, 1, :], ALU.subtract)
            dve.drain()
            v.tensor_copy(gpart[:, :, 2, :], gres2).then_inc(s_gs, 1)

            dve.wait_ge(s_yp, W + T)
            dve.wait_ge(s_yl, 1 + T)
            dve.drain()
            with dve.If(lacking > 0):
                overflow(1, rd2)
            for q in range(Q):
                pairs(1, q, q, q * QB)
            def iterate2(t, before):
                for q in range(Q):
                    pairs(1, (t + 1) * Q + q, q, (t + 1) * TC + q * QB)
                    if before and q == 2:
                        normal2(t - 1)
                    if before and q == 8:
                        low2(t - 1)
                if before:
                    logits2(t - 1)
                    dve.wait_ge(s_x2, t * 16)
                finish2(t)

            iterate2(0, False)
            with dve.Fori(1, T) as t:
                iterate2(t, True)
            normal2(T - 1)
            low2(T - 1)
            logits2(T - 1)

            dve.wait_ge(s_wg, 32)
            v.tensor_tensor(grows[0:1, 2, :], grows[0:1, 0, :], grows[0:1, 1, :], ALU.add).then_inc(s_gv, 1)
            dve.wait_ge(s_gp, 1)
            v.tensor_copy(gb, banks[7][:, 0:8])
            dve.drain()
            gbb = gb.rearrange("p (a n) -> p a n", a=1).to_broadcast([P, T, 8])
            v.scalar_tensor_tensor(out=lg, in0=LG, scalar=1.0 / S, in1=gbb, op0=ALU.mult, op1=ALU.add)
            dve.drain()
            for i in range(T):
                v.max(mx[:, i, :], lg[:, i, :])
            dve.drain()
            for i in range(T):
                v.max_index(mi[:, i, :], mx[:, i, :], lg[:, i, :])
            v.tensor_tensor(gw[:, :, 0:1], mx[:, :, 1:2], mx[:, :, 0:1], ALU.subtract).then_inc(s_lv, 1)
            dve.drain()
            v.tensor_copy(mif, mi[:, :, 0:2])
            dve.wait_ge(s_le, 1)
            v.tensor_scalar(gw[:, :, 2:3], gw[:, :, 1:2], 1.0, None, ALU.add)
            dve.drain()
            v.reciprocal(gw[:, :, 3:4], gw[:, :, 2:3])
            dve.drain()
            v.tensor_tensor(gw[:, :, 2:3], gw[:, :, 3:4], gw[:, :, 1:2], ALU.mult)
            i8 = iota8[:, :].rearrange("p (a n) -> p a n", a=1).to_broadcast([P, T, 8])
            v.tensor_tensor(c0, i8, mif[:, :, 0:1].to_broadcast([P, T, 8]), ALU.is_equal)
            v.tensor_tensor(mx, i8, mif[:, :, 1:2].to_broadcast([P, T, 8]), ALU.is_equal)
            dve.drain()
            v.tensor_tensor(lg, c0, gw[:, :, 3:4].to_broadcast([P, T, 8]), ALU.mult)
            v.tensor_tensor(combs, mx, gw[:, :, 2:3].to_broadcast([P, T, 8]), ALU.mult)
            dve.drain()
            v.tensor_tensor(comb, lg, combs, ALU.add)
            dve.drain()
            csb = csA[:, :].rearrange("p (a n) -> p a n", a=1).to_broadcast([P, T, 8])
            v.tensor_tensor(combs, comb, csb, ALU.mult)
            dve.drain()

            def lowh(g, e):
                for h, (t0, tn) in enumerate(HALF):
                    for f in range(4):
                        j = 4 * h + f
                        dve.wait_ge(s_ua, g * 64 + 8 * e + j + 5)
                        v.tensor_tensor(hlo[e % 2][:, f, t0 * P:(t0 + tn) * P], h32[j % 4][:, 0:tn * P],
                                        hhi[e % 2][:, f, t0 * P:(t0 + tn) * P], ALU.subtract).then_inc(s_us, 1)

            def add(g, e):
                for j in range(4):
                    dve.wait_ge(s_dp, g * 32 + 4 * e + j + 9)
                    for i in range(2 * j, min(2 * j + 2, W)):
                        last = v.scalar_tensor_tensor(
                            out=acc[:, i, :], in0=banks[4 + j][:, (i % 2) * D:(i % 2 + 1) * D],
                            scalar=combs[:, bass.ds(g * W + i, 1), e], in1=acc[:, i, :], op0=ALU.mult, op1=ALU.add)
                    last.then_inc(s_da, 1)
                dve.drain()

            with dve.Fori(0, T // W) as g:
                dve.wait_ge(s_cc, g + 1)
                v.tensor_copy(combg.rearrange("p (t n) -> p t n", n=8), comb[:, bass.ds(g * W, W), :]).then_inc(s_cb, 1)
                lowh(g, 0)
                dve.wait_ge(s_xr5, g * 16 + 16)
                dve.wait_ge(s_st, g * 16 + 16)
                for j in range(4):
                    w = min(2, W - 2 * j)
                    dve.wait_ge(s_bp, 4 * g + j + 1)
                    v.tensor_tensor(acc[:, 2 * j:2 * j + w, :],
                                    banks[4 + (j + 2) % 4][:, 0:w * D].rearrange("p (t n) -> p t n", n=D),
                                    xr5[:, 2 * j:2 * j + w, :], ALU.add).then_inc(s_ai, 1)
                dve.drain()
                for e in range(EXPERTS):
                    if e + 1 < EXPERTS:
                        lowh(g, e + 1)
                    add(g, e)

        @block.scalar
        def _(act):
            a = nc.scalar
            act.wait_ge(s_const, 1)
            for n, c in ((1, s_ot), (1, s_m), (1, s_xlo), (4, s_ab[0]), (4, s_ab[1]), (2, s_ag[0]), (2, s_ag[1]),
                         (4, s_hr), (1, s_yl), (4, s_ua), (1, s_cc)):
                a.activation(cred[:, 0:1], ones[:, 0:1], ACT.Copy).then_inc(c, n)
                act.drain()

            def group1(par, g):
                act.wait_ge(s_tp, g + 1)
                act.wait_ge(s_r, g + 1)
                a.activation(OHiT[par][0:T, :], bank0h[0:T, :], ACT.Copy).then_inc(s_ot, 1)
                act.wait_ge(s_eq, g + 1)
                for h in range(2):
                    last = a.activation(Mm[par][:, 4 * h:4 * h + 4, :],
                                        banks[1 + h][:, :].rearrange("p (g e) -> p g e", e=P), ACT.Relu)
                last.then_inc(s_m, 1)

            with act.Fori(0, GROUPS // 2) as k:
                group1(0, 2 * k)
                group1(1, 2 * k + 1)
            group1(0, GROUPS)

            act.wait_ge(s_table, 16)
            with act.Fori(0, T // W) as b:
                act.wait_ge(s_stat, b + 1)
                a.activation(rstd[:, 0:W], rstd[:, 0:W], ACT.Sqrt, bias=epsc[:, :]).then_inc(s_std, 1)
                for i in range(W):
                    t = b * W + i
                    act.wait_ge(s_xn, t + 1)
                    a.activation(R2[:, bass.ds(t * 2 * D, D)], xs[i][:, 0:D], ACT.Copy, scale=S).then_inc(s_xhi, 1)
                    act.wait_ge(s_xl, t + 1)
                    a.activation(R2[:, bass.ds(t * 2 * D + D, D)], xlo[0], ACT.Copy, scale=S).then_inc(s_xlo, 1)
            act.wait_ge(s_w, 16 * 16)
            act.wait_ge(s_vm, 8)
            for j, src in enumerate((W0s, W1s, bhs[:, :], Wc[:, :, 0:D])):
                dst = sqs[:, 0:4] if j == 2 else sqs.rearrange("p (k n) -> p k n", k=2 if j < 2 else 4)
                last = a.activation(dst, src, ACT.Square, accum_out=small[:, 32 + j:33 + j])
                act.drain()
            a.activation(cred[:, 1:2], ones[:, 0:1], ACT.Copy).then_inc(s_sq, 1)
            act.wait_ge(s_sp, 1)
            a.activation(small[:, 40:44], banks[3][:, 0:4], ACT.Sqrt).then_inc(s_sr, 1)

            def evac(L, n, q):
                act.wait_ge(s_bl[L], n + 1 + Q)
                act.wait_ge(s_ap[L], n + 1)
                n = blocks(q) * P
                a.activation(Ab[q][:, 0:n], banks[BB(q)][:, 0:n], ACT.Copy).then_inc(s_ab[L], 1)

            def copy(L, t, bank):
                act.wait_ge(s_ap[L], (t + 1) * Q + Q)
                act.wait_ge(s_an[L], t + 1)
                a.activation(aggr, bank[:, :], ACT.Copy).then_inc(s_ag[L], 1)

            def deviation(t):
                act.wait_ge(s_v2, t + 1)
                a.activation(x2r, x2m[:, 1:2], ACT.Sqrt, bias=epsc[:, :]).then_inc(s_d2, 1)

            def high2(t):
                act.wait_ge(s_t2, t + 1)
                a.activation(R3t(t, 0), banks[6][:, 0:D], ACT.Copy, scale=S).then_inc(s_h2, 1)

            def iterate(L, t, before, bank):
                for q in range(Q):
                    evac(L, t * Q + q + LEAD, (q + LEAD) % Q)
                    if before and q == 0:
                        deviation(t - 1)
                    if before and q == 7:
                        high2(t - 1)
                copy(L, t, bank)

            def aggregate(L):
                for q in range(LEAD):
                    evac(L, q, q)
                iterate(L, 0, False, banks[5])
                with act.Fori(0, T // 2) as k:
                    iterate(L, 2 * k + 1, L == 1, banks[7])
                    iterate(L, 2 * k + 2, L == 1, banks[5])
                if L == 1:
                    deviation(T - 1)
                    high2(T - 1)

            aggregate(0)

            def squares(e):
                act.wait_ge(s_wl, 48 * e + 48)
                a.activation(wsq, wraw[:, 0:2 * F], ACT.Square, accum_out=sq3[:, 0:1])
                act.drain()
                a.activation(wsq, wraw[:, 2 * F:4 * F], ACT.Square, accum_out=sq3[:, 1:2])
                act.drain()
                a.activation(wsq[:, 0:4], braw, ACT.Square, accum_out=sq3[:, 2:3])
                act.drain()
                a.activation(cred[:, 1:2], ones[:, 0:1], ACT.Copy).then_inc(s_wq, 1)
                act.drain()

            def norms(e):
                act.wait_ge(s_wr, e + 1)
                a.activation(nr3, nr3, ACT.Sqrt).then_inc(s_wt, 1)

            def highs(e):
                act.wait_ge(s_wc, e + 1)
                sf = sc6.bitcast(F32)
                for j in range(2):
                    last = a.activation(wout[:, 2 * j * 2 * F:(2 * j + 1) * 2 * F], wraw[:, j * 2 * F:(j + 1) * 2 * F],
                                        ACT.Copy, scale=sf[:, j:j + 1])
                last.then_inc(s_wh, 1)

            act.wait_ge(s_ac, 1 + T)
            squares(0)
            norms(0)
            highs(0)
            with act.Fori(0, T // W) as g:
                for h, (t0, tn) in enumerate(HALF):
                    for f in range(4):
                        j = 4 * h + f
                        act.wait_ge(s_hp, g * 8 + j + 1)
                        if j == 0:
                            act.wait_ge(s_yp, g * W + W)
                        a.activation(hT[:, f, t0 * P:(t0 + tn) * P], banks[f][:, 0:tn * P], ACT.Relu,
                                     bias=bhs[:, f:f + 1]).then_inc(s_hr, 1)
                for i in range(W):
                    n = g * W + i
                    act.wait_ge(s_yp, n + 1 + W)
                    a.activation(R2[:, bass.ds(n * 2 * D, D)],
                                 banks[Y4(i)][:, 0:D], ACT.Copy).then_inc(s_yh, 1)
                    act.wait_ge(s_zc, n + 4)
                    a.activation(R2[:, bass.ds(n * 2 * D + D, D)], ylo[0], ACT.Copy, scale=S).then_inc(s_yl, 1)
                    if i == 0:
                        squares(g + 1)
                    if i == 2:
                        norms(g + 1)
                    if i == 4:
                        highs(g + 1)
            act.wait_ge(s_yp, W + T)
            aggregate(1)

            act.wait_ge(s_lv, 1)
            a.activation(gw[:, :, 1:2], gw[:, :, 0:1], ACT.Exp).then_inc(s_le, 1)
            with act.Fori(0, T // W) as g:
                for e in range(EXPERTS):
                    for h, (t0, tn) in enumerate(HALF):
                        for f in range(4):
                            j = 4 * h + f
                            act.wait_ge(s_up, g * 64 + 8 * e + j + 1)
                            if j == 0:
                                act.wait_ge(s_dp, g * 32 + 4 * e + 4)
                            act.wait_ge(s_us, g * 64 + 8 * e + j + 1)
                            sc, bi = iscA[:, e:e + 1], b1A[:, 4 * e + f:4 * e + f + 1]
                            a.activation(hhi[e % 2][:, f, t0 * P:(t0 + tn) * P], banks[j % 4][:, 0:tn * P],
                                         ACT.Relu, bias=bi, scale=sc)
                            a.activation(h32[j % 4][:, 0:tn * P], banks[j % 4][:, 0:tn * P],
                                         ACT.Relu, bias=bi, scale=sc).then_inc(s_ua, 1)
                    if e == 0:
                        for j in range(2):
                            act.wait_ge(s_ct, 2 * g + j + 1)
                            n = 4 if j == 0 else 3
                            last = a.activation(combT[0:8, 4 * j:4 * j + n, :],
                                                banks[4 + j][0:8, 0:n * P].rearrange("p (t n) -> p t n", n=P), ACT.Copy)
                        last.then_inc(s_cc, 1)

        @block.tensor
        def _(pe):
            mm = nc.tensor.matmul
            pe.wait_ge(s_const, 1)
            for n, c in ((2, s_r), (W, s_xt), (Q, s_bl[0]), (Q, s_bl[1]), (Q, s_ap[0]), (Q, s_ap[1]),
                         (W, s_yp), (8, s_dp)):
                mm(banks[6][:, 0:P], zeros16[:, :], zeros16[:, :], start=True, stop=True).then_inc(c, n)
            mm(banks[5][0:T, 0:P], zeros16[:, 0:T], zeros16[:, :], start=True, stop=False)

            def groupA(par, g):
                pe.wait_ge(s_ot, g + 1)
                pe.wait_ge(s_oh, g + 1)
                pe.wait_ge(s_t, g + 1)
                for c in range(G):
                    mm(banks[3][0:T, c * T:G * T], OHi[par][:, :, c],
                       OHj[par][:, :, c].rearrange("p (a j) -> p a j", a=1).to_broadcast([P, G - c, T]),
                       start=(c == 0), stop=(c == G - 1))
                for c in range(G):
                    last = nc.tensor.transpose(bank0h[0:T, c * P:(c + 1) * P], OHi[par][:, :, c], ident16[:, :])
                last.then_inc(s_tp, 1)
                for c in range(G):
                    mm(banks[5][0:T, 0:P], OHi[par][:, :, c], LHi[par][:, :, c], start=False, stop=False)
                    last = mm(banks[5][0:T, 0:P], OHj[par][:, :, c], LLo[par][:, :, c], start=False, stop=False)
                last.then_inc(s_h, 1)
                pe.wait_ge(s_m, g + 1)
                for h in range(2):
                    mm(banks[1 + h][:, :], ident16[:, :], neg4[:, :, :].rearrange("p c e -> p (c e)"),
                       start=True, stop=False)
                pe.wait_ge(s_ot, g + 2)
                for c in range(G):
                    ot = OHiT[par][0:T, c * P:(c + 1) * P]
                    last = mm(banks[1 + c // 4][:, (c % 4) * P:(c % 4 + 1) * P], ot, ot, start=False, stop=(c % 4 == 3))
                last.then_inc(s_eq, 1)

            def groupF(par, g):
                pe.wait_ge(s_m, g + 2)
                pe.wait_ge(s_t, g + 2)
                pe.wait_ge(s_rk, g + 1)
                for c in range(G):
                    o = banks[4][:, c * T:(c + 1) * T]
                    mm(o, Mm[par][:, c, :], OHj[par][:, :, c], start=True, stop=False)
                    last = mm(o, OHiT[par][0:T, c * P:(c + 1) * P], Tsn[par][0:T, c, :], start=False, stop=True)
                last.then_inc(s_r, 1)

            groupA(0, 0)
            with pe.Fori(0, GROUPS // 2) as k:
                for par in range(2):
                    g = 2 * k + par
                    groupF(par, g)
                    groupA(1 - par, g + 1)

            pe.wait_ge(s_ot, GROUPS + 2)
            pe.wait_ge(s_rk, GROUPS + 1)
            for h in range(2):
                mm(banks[6 + h][:, :], zeros16[:, :], zeros16[:, 0:1].to_broadcast([P, 512]), start=True, stop=False)
            with pe.Fori(0, T // W) as b:
                for i in range(W):
                    t = b * W + i
                    pe.wait_ge(s_xn, t + 1)
                    pe.wait_ge(s_xtc, t + 1)
                    for h in range(2):
                        nc.tensor.transpose(banks[0][:, h * P:(h + 1) * P], xs[i][:, h * P:(h + 1) * P], ident[:, :])
                    for h in range(2):
                        last = mm(banks[6 + h][:, 0:D + 1], xs[i][:, h * P:(h + 1) * P], xs[i][:, 0:D + 1],
                                  start=False, stop=False)
                    last.then_inc(s_xt, 1)

            pe.wait_ge(s_w, 16 * 16)
            mm(banks[5][0:T, 0:P], zeros16[:, 0:T], zeros16[:, :], start=False, stop=True)
            mm(banks[6][:, 0:P], zeros16[:, :], zeros16[:, :], start=False, stop=True)
            mm(banks[7][:, 0:P], zeros16[:, :], zeros16[:, :], start=False, stop=True).then_inc(s_pm, 1)
            for i, wgt in enumerate((Wk, Wv, Wfc)):
                if i == 0:
                    pe.wait_ge(s_xtc, T + 1)
                for kt in range(2):
                    for dt in range(2):
                        last = nc.tensor.transpose(banks[i][:, dt * D + kt * P:dt * D + (kt + 1) * P],
                                                   wgt[:, kt, dt * P:(dt + 1) * P], ident[:, :])
                last.then_inc(s_pm, 1)
            pe.wait_ge(s_vm, 3)
            for gt in range(2):
                for dt in range(2):
                    mm(banks[3][:, gt * D:(gt + 1) * D], Gs[:, dt, gt * P:(gt + 1) * P], WvT[:, dt, :],
                       start=(dt == 0), stop=(dt == 1))
            for r, wt in ((0, WvT), (1, WkT)):
                for dt in range(2):
                    last = mm(banks[4][0:1, r * D:(r + 1) * D], Gs[:, dt, D:D + 1], wt[:, dt, :],
                              start=(dt == 0), stop=(dt == 1))
            last.then_inc(s_pm, 1)
            pe.wait_ge(s_vm, 5)
            for vt in range(2):
                o = banks[0][:, vt * D:(vt + 1) * D]
                for gt in range(2):
                    mm(o, B1s[:, gt, vt * P:(vt + 1) * P], WkT[:, gt, :], start=(gt == 0), stop=False)
                mm(o, rows[0:1, SV, vt * P:(vt + 1) * P], rows[0:1, BK, :], start=False, stop=False)
                last = mm(o, rows[0:1, BV, vt * P:(vt + 1) * P], rows[0:1, SK, :], start=False, stop=True)
            last.then_inc(s_pm, 1)
            pe.wait_ge(s_vm, 6)
            for dt in range(2):
                for et in range(2):
                    last = mm(banks[1][:, dt * D:(dt + 1) * D], PTs[:, et, dt * P:(dt + 1) * P], WfT[:, et, :],
                              start=(et == 0), stop=(et == 1))
            last.then_inc(s_pm, 1)
            pe.wait_ge(s_vm, 7)
            for xt in range(2):
                for dt in range(2):
                    mm(banks[2][:, xt * D:(xt + 1) * D], Wq[:, dt, xt * P:(xt + 1) * P], Rs[:, dt, :],
                       start=(dt == 0), stop=(dt == 1))
            for dt in range(2):
                last = mm(banks[3][0:1, 0:D], bqc[:, dt:dt + 1], Rs[:, dt, :], start=(dt == 0), stop=(dt == 1))
            last.then_inc(s_pm, 1)
            pe.wait_ge(s_vm, 8)
            mm(banks[4][:, 0:D], ones[0:1, :], rows[0:1, ZB, :], start=True, stop=True).then_inc(s_pm, 1)
            pe.wait_ge(s_vm, 10)
            nc.tensor.transpose(banks[1][:, 0:T], degT[0:T, :], ident[0:T, 0:T]).then_inc(s_pm, 1)
            pe.wait_ge(s_sq, 1)
            mm(banks[3][:, 0:4], ones[:, :], small[:, 32:36], start=True, stop=True).then_inc(s_sp, 1)
            pe.wait_ge(s_vm, 12)
            pe.wait_ge(s_sr, 1)
            pe.wait_ge(s_flag, 1)
            mm(banks[2][:, 0:1], ones[:, :], small[:, 56:57], start=True, stop=True).then_inc(s_fp, 1)
            pe.wait_ge(s_flag, 2)
            lacking = pe.value_load(flag[0:1, 0:1])

            def overflow(L):
                with pe.Fori(0, E) as c:
                    for i in range(2):
                        m = 2 * c + i
                        pe.wait_ge(s_o1[L], m + 1)
                        nc.tensor.transpose(banks[0][:, 0:P], oB, ident[:, :]).then_inc(s_o2[L], 1)
                        pe.wait_ge(s_ox[L], m * 16 + 16)
                        pe.wait_ge(s_o3[L], m + 1)
                        mm(banks[1][:, :], oSel, oX, start=True, stop=True).then_inc(s_o4[L], 1)

            def build(L, n, q):
                pe.wait_ge(s_oo[L], n + 1)
                pe.wait_ge(s_ab[L], n + 1)
                for c in range(QB):
                    own = q == Q - 1 and c >= 1
                    o = 1 if own else c
                    last = mm(banks[BB(q)][:, o * P:(o + 1) * P], OU[q][:, :, c], OT[q][:, :, c],
                              start=(not own or c == 1), stop=(not own or c == QB - 1))
                last.then_inc(s_bl[L], 1)

            def apply(L, t, q, bank):
                if q == 0:
                    pe.wait_ge(s_ag[L], t + 1)
                pe.wait_ge(s_ab[L], t * Q + q + 5)
                for c in range(blocks(q)):
                    u = q * QB + c
                    src = R2[:, u * 2 * D:(u + 1) * 2 * D] if u < T else R2[:, bass.ds(t * (2 * D), 2 * D)]
                    last = mm(bank[:, :], Ab[q][:, c * P:(c + 1) * P], src, start=(u == 0), stop=(u == T))
                last.then_inc(s_ap[L], 1)

            def transposed(t):
                pe.wait_ge(s_an[0], t + 2)
                pe.wait_ge(s_ac, t + 1)
                for h in range(2):
                    last = nc.tensor.transpose(banks[6][:, h * P:(h + 1) * P], aggn[:, h * P:(h + 1) * P], ident[:, :])
                last.then_inc(s_at, 1)

            def transposed2(t):
                pe.wait_ge(s_n2, t + 1)
                pe.wait_ge(s_lr, t + 1)
                for k in range(2):
                    last = nc.tensor.transpose(banks[6][:, k * P:(k + 1) * P], x2n[:, k * P:(k + 1) * P], ident[:, :])
                last.then_inc(s_t2, 1)

            def gate(t):
                pe.wait_ge(s_l2, t + 1)
                for part in range(2):
                    for k in range(2):
                        last = mm(banks[6][:, D:D + 24], R3t(t, part)[:, k * P:(k + 1) * P],
                                  gpart[:, k, :, :].rearrange("p g n -> p (g n)"),
                                  start=(part + k == 0), stop=(part + k == 2))
                last.then_inc(s_lp, 1)

            def tile3(L, t, before, bank):
                for q in range(Q):
                    build(L, t * Q + q + LEAD, (q + LEAD) % Q)
                    apply(L, t, q, bank)
                    if q == 6 and before and L == 0:
                        transposed(t - 1)
                    if q == 5 and before and L == 1:
                        transposed2(t - 1)
                    if q == 11 and before and L == 1:
                        gate(t - 1)

            def tiles3(L):
                tile3(L, 0, False, banks[5])
                with pe.Fori(0, T // 2) as k:
                    tile3(L, 2 * k + 1, True, banks[7])
                    tile3(L, 2 * k + 2, True, banks[5])

            pe.wait_ge(s_xhi, T)
            pe.wait_ge(s_xlo, 1 + T)
            with pe.If(lacking > 0):
                overflow(0)
            for q in range(LEAD):
                build(0, q, q)
            tiles3(0)
            transposed(T - 1)

            pe.wait_ge(s_ac, 1 + T)
            pe.wait_ge(s_sc2, 1)
            pe.wait_ge(s_ab[0], T * Q + LEAD + 4)
            pe.wait_ge(s_ag[0], 2 + T)
            def hidden(g, par, need):
                pe.wait_ge(s_x4[par], need)
                for h, (t0, tn) in enumerate(HALF):
                    xv = xT4[par][:, t0 * D:(t0 + tn) * D].rearrange("p (t k n) -> p t k n", t=tn, k=2)
                    av = R3[:, bass.ds(g * (W * D) + t0 * D, tn * D)].rearrange("p (t k n) -> p t k n", t=tn, k=2)
                    for f in range(4):
                        j = 4 * h + f
                        pe.wait_ge(s_hr, g * 8 + j + 1)
                        o = banks[f][:, 0:tn * P].rearrange("p (t n) -> p t n", n=P)
                        for k in range(2):
                            mm(o, W0s[:, k, f * P:(f + 1) * P], xv[:, :, k, :], start=(k == 0), stop=False)
                        for k in range(2):
                            last = mm(o, W1s[:, k, f * P:(f + 1) * P], av[:, :, k, :], start=False, stop=(k == 1))
                        last.then_inc(s_hp, 1)
                pe.wait_ge(s_hr, g * 8 + 12)
                for i in range(W):
                    n = g * W + i
                    pe.wait_ge(s_zc, n + 1)
                    o = banks[Y4(i)]
                    for f in range(4):
                        mm(o[:, :], hT[:, f, i * P:(i + 1) * P], Wc[:, f, :], start=(f == 0), stop=False)
                    for k in range(2):
                        last = mm(o[:, D:2 * D], xT4[par][:, i * D + k * P:i * D + (k + 1) * P], Ms[:, k, :],
                                  start=False, stop=(k == 1))
                    last.then_inc(s_yp, 1)

            with pe.Fori(0, T // W // 2) as k2:
                for par in range(2):
                    hidden(2 * k2 + par, par, 16 * k2 + 16)
            hidden(T // W - 1, 0, 16 * (T // W // 2 + 1))

            pe.wait_ge(s_yl, 1 + T)
            pe.wait_ge(s_zc, 3 + T)
            with pe.If(lacking > 0):
                overflow(1)
            for q in range(LEAD):
                build(1, q, q)
            pe.wait_ge(s_gs, 1)
            tiles3(1)
            transposed2(T - 1)
            gate(T - 1)

            pe.wait_ge(s_ab[1], T * Q + LEAD + 4)
            pe.wait_ge(s_ag[1], 2 + T)
            pe.wait_ge(s_lr, 1 + T)
            pe.wait_ge(s_gv, 1)
            mm(banks[7][:, 0:8], ones[0:1, :], grows[0:1, 2, :], start=True, stop=True).then_inc(s_gp, 1)
            pe.wait_ge(s_st, 16)
            with pe.Fori(0, T // W) as g:
                def up(e):
                    pe.wait_ge(s_we[e], 16)
                    for h, (t0, tn) in enumerate(HALF):
                        xv = R3h[:, bass.ds(g * (W * 2 * D) + t0 * 2 * D, tn * 2 * D)]\
                            .rearrange("p (t s k n) -> p t s k n", t=tn, s=2, k=2)
                        for f in range(4):
                            j = 4 * h + f
                            pe.wait_ge(s_ua, g * 64 + 8 * e + j + 1)
                            o = banks[j % 4][:, 0:tn * P].rearrange("p (t n) -> p t n", n=P)
                            n = 0
                            for k in range(2):
                                for wp, xp in ((0, 0), (0, 1), (1, 0)):
                                    last = mm(o, w1(e, wp, k)[:, f * P:(f + 1) * P], xv[:, :, xp, k, :],
                                              start=(n == 0), stop=(n == 5))
                                    n += 1
                            last.then_inc(s_up, 1)

                def down(e):
                    pe.wait_ge(s_us, g * 64 + 8 * e + 8 + 4)
                    for j in range(4):
                        pe.wait_ge(s_da, g * 32 + 4 * e + j + 1)
                        for i in range(2 * j, min(2 * j + 2, W)):
                            o = banks[4 + j][:, (i % 2) * D:(i % 2 + 1) * D]
                            n = 0
                            for f in range(4):
                                for hp, wp in ((hhi, 0), (hhi, 1), (hlo, 0)):
                                    last = mm(o, hp[e % 2][:, f, i * P:(i + 1) * P], w2(e, wp, f),
                                              start=(n == 0), stop=(n == 11))
                                    n += 1
                        last.then_inc(s_dp, 1)

                up(0)
                pe.wait_ge(s_cb, g + 1)
                pe.wait_ge(s_da, g * 32 + 4)
                for i in range(W):
                    last = nc.tensor.transpose(banks[4 + i // 4][0:8, (i % 4) * P:(i % 4 + 1) * P],
                                               combg[:, i * 8:(i + 1) * 8], ident[:, :])
                    if i in (3, 6):
                        last.then_inc(s_ct, 1)
                up(1)
                pe.wait_ge(s_cc, g + 2)
                for j in range(4):
                    for i in range(2 * j, min(2 * j + 2, W)):
                        last = mm(banks[4 + (j + 2) % 4][:, (i % 2) * D:(i % 2 + 1) * D], combT[0:8, i, :], b2s[0:8, :],
                                  start=True, stop=True)
                    last.then_inc(s_bp, 1)
                pe.wait_ge(s_ai, 4 * g + 4)
                for e in range(EXPERTS):
                    if e >= 1 and e + 1 < EXPERTS:
                        up(e + 1)
                    down(e)


_INS = ["x", "src", "dst", "L0_gnn_W0_0", "L0_gnn_b0_0", "L0_gnn_W1_0", "L0_gnn_b1_0", "L0_gnn_W0_1",
        "L0_gnn_b0_1", "L0_gnn_W1_1", "L0_gnn_b1_1", "L0_mix_Wq", "L0_mix_bq", "L0_mix_Wk", "L0_mix_bk",
        "L0_mix_Wv", "L0_mix_bv", "L0_mix_Wfc", "L0_mix_bfc", "L0_ffn_Wg", "L0_ffn_bg", "L0_ffn_bias",
        "L0_ffn_W1", "L0_ffn_b1", "L0_ffn_W2", "L0_ffn_b2"]


def kernel(**inputs):
    import numpy as _np
    import concourse.bacc as _bacc
    from concourse import mybir as _mybir
    from concourse.bass_utils import run_bass_kernel_spmd as _run

    nc = _bacc.Bacc("TRN2", target_bir_lowering=False, num_devices=1)
    arrays, io = {}, {}
    for name in _INS:
        a = _np.ascontiguousarray(inputs[name])
        arrays[f"in_{name}_dram"] = a
        io[name] = nc.dram_tensor(f"in_{name}_dram", a.shape, _mybir.dt.from_np(a.dtype), kind="ExternalInput").ap()
    io["out"] = nc.dram_tensor("out_dram", (N, D), _mybir.dt.float32, kind="ExternalOutput").ap()
    gps_layer(nc, io)
    r = _run(nc, [arrays], core_ids=[0])
    return r.results[0]["out_dram"]
```

```python
import concourse.bass as bass
from concourse import mybir
from contextlib import ExitStack

F32, F16, I32 = mybir.dt.float32, mybir.dt.float16, mybir.dt.int32
U32, BF16 = mybir.dt.uint32, mybir.dt.bfloat16
ALU, ACT, AX = mybir.AluOpType, mybir.ActivationFunctionType, mybir.AxisListType
RADD = bass.bass_isa.ReduceOp.add

P = 128
N, D, F, EXPERTS, HEADS = 6250, 256, 512, 8, 8
EDGES = 106250
T = -(-N // P)
LAST = N - (T - 1) * P
E = 832
EP = E + 8
G = 8
GROUPS = E // G
LASTE = EDGES - (P - 1) * E
PADNODE = 8191
BINS = T * T
COLS = BINS + T
TRASH = P * COLS
SLOTS = TRASH + P * EP
TC = T + 3
QB = 4
Q = TC // QB
LEAD = 3
S = 2048.0
W = 7
HALF = ((0, 4), (4, 3))
OVROW = T * P
EPS = 1e-5


def gps_layer(nc, io):
    ctx = ExitStack()
    with ctx:
        ctx.enter_context(nc.allow_non_contiguous_dma(reason="bias columns"))

        def sb(name, shape, dt=F32):
            return ctx.enter_context(nc.sbuf_tensor(name, shape, dt))

        def sem(name):
            return ctx.enter_context(nc.semaphore(name))

        slots_dram = nc.dram_tensor("slots_dram", [SLOTS, 1], I32).ap()
        feat_dram = nc.dram_tensor("feat_dram", [(T + 1) * P, 2 * D], F16).ap()
        sum_dram = nc.dram_tensor("sum_dram", [(T + 2) * P, 2 * D], F32).ap()
        ends_dram = nc.dram_tensor("ends_dram", [2, P, EP], I32).ap()
        w_dram = nc.dram_tensor("w_dram", [EXPERTS, P, 8 * F], F16).ap()
        x2_dram = nc.dram_tensor("x2_dram", [T * P, D], F32).ap()
        xT_dram = nc.dram_tensor("xT_dram", [T * P, D], F32).ap()

        R2 = sb("R2", [P, T * 2 * D], F16)
        R3 = sb("R3", [P, T * D])
        R3i = R3[:, :].bitcast(I32)
        R3h = R3[:, :].bitcast(F16)

        def words(i):
            return slice(i * EP, (i + 1) * EP)

        eS, eD = R3i[:, words(0)], R3i[:, words(1)]
        eHi, eLo = R3i[:, words(2)], R3i[:, words(3)]
        eTi, eTj = R3i[:, words(4)], R3i[:, words(5)]
        rank = R3[:, words(4)]
        rec = R3i[:, words(6)]
        binb, diag = R3[:, words(7)], R3[:, words(8)]
        delta = R3[:, words(9)]
        inval = R3[:, words(10)]
        half0 = 11 * EP * 2
        fTi, fTj, fHi, fLo = (R3h[:, half0 + i * EP:half0 + (i + 1) * EP] for i in range(4))
        assert half0 + 4 * EP <= 2 * T * D

        trash = sb("trash", [P, EP], I32)
        TT = sb("TT", [P, (T + 1) * TC], F16)
        TU = sb("TU", [P, (T + 1) * TC], F16)
        iota128 = sb("iota128", [P, P, G], F16)
        iota49 = sb("iota49", [P, T, G], F16)
        iotaB = sb("iotaB", [P, P, QB], F16)
        ident16 = sb("ident16", [P, P], F16)
        ident = sb("ident", [P, P])
        zeros16 = sb("zeros16", [P, P], F16)
        neg4 = sb("neg4", [P, 4, P], F16)
        ones = sb("ones", [P, P])
        epsc = sb("epsc", [P, 1])
        W01 = sb("W01", [P, 4, F])
        W0s, W1s = W01[:, 0:2, :], W01[:, 2:4, :]
        Wc = sb("Wc", [P, 4, 2 * D])
        bh = sb("bh", [P, 2, 4])
        bhs = sb("bhs", [P, 4])
        zb = sb("zb", [P, D])
        Ms = sb("Ms", [P, 2, D])
        deg = sb("deg", [P, T])
        rdeg = sb("rdeg", [P, T])
        rd1 = sb("rd1", [P, T])
        rd2 = sb("rd2", [P, T])
        stats = sb("stats", [P, 6])
        iota8 = sb("iota8", [P, 8])
        zeros32 = sb("zeros32", [P, D])
        cred = sb("cred", [P, 2])
        iscA = sb("iscA", [P, EXPERTS])
        csA = sb("csA", [P, EXPERTS])
        b1A = sb("b1A", [P, EXPERTS * 4])
        zrow = sb("zrow", [P, 1])
        flag = sb("flag", [P, 1], I32)
        pwait = sb("pwait", [P, 1])
        mv = sb("mv", [P, 2])
        rstd = sb("rstd", [P, 1])
        small = sb("small", [P, 64])
        smalli = small[:, :].bitcast(I32)
        vals = small[:, 16:19]
        hsc, csc = small[:, 48:49], small[:, 49:50]
        unsc, ysc = small[:, 54:55], small[:, 55:56]
        sbh = small[:, 60:64]
        BIG = 17330
        big = sb("big", [P, BIG])
        bigh = big[:, :].bitcast(F16)
        bigi = big[:, :].bitcast(I32)

        def BB(q):
            return q % 4 if q < 12 else 4

        def blocks(q):
            return QB if q < Q - 1 else 2

        def Y4(i):
            return 4 + (i % 3 if i < 6 else 3)

        banks = [ctx.enter_context(nc.psum_tensor(f"bank{i}", [P, 512], F32)) for i in range(8)]

        bank0h = banks[0][:, :].bitcast(F16)

        class Space:
            def __init__(self, at=0):
                self.at = at

            def f32(self, *shape):
                n = 1
                for s in shape:
                    n *= s
                ap = big[:, self.at:self.at + n]
                self.at += n
                assert self.at <= BIG, self.at
                return ap

            def f16(self, *shape):
                n = 1
                for s in shape:
                    n *= s
                ap = bigh[:, 2 * self.at:2 * self.at + n]
                self.at += -(-n // 2)
                assert self.at <= BIG, self.at
                return ap

            def i32(self, *shape):
                n = 1
                for s in shape:
                    n *= s
                ap = bigi[:, self.at:self.at + n]
                self.at += n
                assert self.at <= BIG, self.at
                return ap

        sp1 = Space()
        OHi = [sp1.f16(T * G).rearrange("p (m g) -> p m g", g=G) for _ in range(2)]
        OHj = [sp1.f16(T * G).rearrange("p (m g) -> p m g", g=G) for _ in range(2)]
        at_L = sp1.at
        LHi = [sp1.f16(P * G).rearrange("p (m g) -> p m g", g=G) for _ in range(2)]
        LLo = [sp1.f16(P * G).rearrange("p (m g) -> p m g", g=G) for _ in range(2)]
        at_T = sp1.at
        OHiT = [sp1.f16(G * P) for _ in range(2)]
        sqs = big[:, at_T:at_T + 1024]
        Mm = [sp1.f16(G * P).rearrange("p (g e) -> p g e", g=G) for _ in range(2)]
        Tsn = [sp1.f16((G + 1) * T).rearrange("p (g j) -> p g j", j=T) for _ in range(2)]
        prod = sp1.f32(G * T).rearrange("p (g j) -> p g j", j=T)
        d1 = sp1.f32(G)
        rr = sp1.f32(G)
        ee = sp1.f32(G)
        bb = sp1.f32(G)
        pp = sp1.f32(G)
        ov = sp1.f32(G)
        tq = sp1.f32(G)
        tr = sp1.f32(G)
        stP = [sb(f"stP{i}", [P, G], I32) for i in range(2)]
        stR = [sb(f"stR{i}", [P, G], I32) for i in range(2)]
        xs = sp1.f32(D + 1)
        xlo = sp1.f32(D)
        Gs = sp1.f32(2 * (D + 1)).rearrange("p (k n) -> p k n", k=2)
        Wq, Wk, Wv, Wfc = (sp1.f32(2 * D).rearrange("p (k n) -> p k n", k=2) for _ in range(4))
        hmask = sp1.f32(2 * D).rearrange("p (k n) -> p k n", k=2)
        xin = sp1.f32(D)
        xst = sp1.f32(D)
        sp2 = Space(at_L)
        WkT, WvT, B1s, PTs = (sp2.f32(2 * D).rearrange("p (k n) -> p k n", k=2) for _ in range(4))
        assert sp2.at <= at_T
        sp2 = Space(at_T + 1024)
        WfT, Rs = (sp2.f32(2 * D).rearrange("p (k n) -> p k n", k=2) for _ in range(2))
        bqc = sp1.f32(2)
        rows = sp1.f32(9 * D).rearrange("p (r n) -> p r n", r=9)
        BK, BV, BFC, B01, B11, SV, SK, ZB, SPARE = range(9)
        degT = sp1.f32(P)

        sp3 = Space()
        slotI = sp3.i32(COLS)
        hiI = sp3.i32(COLS)
        HI = sp3.f16(COLS)
        LO = sp3.f16(COLS)
        sp3b = Space()
        OT = [sp3b.f16(P * QB).rearrange("p (m b) -> p m b", b=QB) for _ in range(Q)]
        OU = [sp3b.f16(P * QB).rearrange("p (m b) -> p m b", b=QB) for _ in range(Q)]
        Ab = [sp3b.f16(QB * P) for _ in range(Q)]
        aggr = sp3b.f32(2 * D)
        aggc = sp3b.f32(D)
        aggn = sp3b.f32(D)
        xres = sp3b.f32(D)
        x2b, x2n = sp3b.f32(D), sp3b.f32(D)
        x2s, x2m, x2r = sp3b.f32(6), sp3b.f32(2), sp3b.f32(1)
        graw = sp3b.f32(2 * 8).rearrange("p (k n) -> p k n", k=2)
        gres = sp3b.f32(2 * 8).rearrange("p (k n) -> p k n", k=2)
        gres2 = sp3b.f32(2 * 8).rearrange("p (k n) -> p k n", k=2)
        gpart = sp3b.f16(2 * 24).bitcast(BF16).rearrange("p (k g n) -> p k g n", k=2, g=3)
        spo = Space(sp3b.at)
        oX = spo.f16(2 * D)
        oA = spo.f32(2 * D)
        oN = spo.f32(2 * D)
        oSel = spo.f16(P)
        oB = spo.f32(P)
        oM = spo.f32(P)
        oa, ob, ow = (spo.i32(1) for _ in range(3))
        obf, oc, od, oe = (spo.f32(1) for _ in range(4))
        sp4 = Space()
        hhi4, hlo4 = (sp4.f16(4 * W * P).rearrange("p (f n) -> p f n", f=4) for _ in range(2))
        h4 = [sp4.f32(4 * P) for _ in range(4)]
        WcP = [sp4.f16(4 * 2 * D).rearrange("p (f n) -> p f n", f=4) for _ in range(2)]
        xT4 = [sp4.f32(W * D) for _ in range(2)]
        ylo = sp4.f32(D)
        wraw = sp4.f32(4 * F)
        wsq = sp4.f32(2 * F)
        wout = sp4.f16(8 * F)
        braw = sp4.f32(4)
        sq3, nr3, nv3 = sp4.f32(3), sp4.f32(3), sp4.f32(3)
        ex3, cl3 = sp4.i32(3), sp4.f32(3)
        ab6, sc6 = sp4.i32(6), sp4.i32(6)
        sp5 = Space()
        h32 = [sp5.f32(4 * P) for _ in range(4)]
        hhi = [sp5.f16(4 * W * P).rearrange("p (f n) -> p f n", f=4) for _ in range(2)]
        hlo = [sp5.f16(4 * W * P).rearrange("p (f n) -> p f n", f=4) for _ in range(2)]
        acc = sp5.f32(W * D).rearrange("p (t n) -> p t n", t=W)
        xr5 = sp5.f32(W * D).rearrange("p (t n) -> p t n", t=W)
        combg = sp5.f32(W * 8)
        comb, combs, c0, c1 = (sp5.f32(T * 8).rearrange("p (t n) -> p t n", t=T) for _ in range(4))
        gw = sp5.f32(T * 4).rearrange("p (t n) -> p t n", t=T)
        combT = sp5.f32(W * P).rearrange("p (t n) -> p t n", t=W)
        wslot = [x[:, :, :].rearrange("p k n -> p (k n)").bitcast(F16) for x in (W01, Wc)]
        wslot += [R2[:, 8 * F * e:8 * F * (e + 1)] for e in range(EXPERTS - 2)]
        TOP = BIG - (2 * T * 2 + 8 * 8 + D)
        spt = Space(TOP)
        lgt, mxt, mit = spt.f32(8), spt.f32(8), spt.i32(8).bitcast(U32)
        mx, mif = (spt.f32(T * 2).rearrange("p (t n) -> p t n", t=T) for _ in range(2))
        lraw = spt.f32(8)
        gb = spt.f32(8)
        low_top = spt.at
        grows = spt.f32(3 * 8).rearrange("p (r n) -> p r n", r=3)
        b2s = spt.f32(D)
        assert sp5.at <= TOP and sp3b.at <= TOP and spo.at <= low_top, (sp5.at, sp3b.at, spo.at, TOP)

        def R3t(t, part):
            return R3h[:, t * 2 * D + part * D:t * 2 * D + (part + 1) * D] if isinstance(t, int) else \
                R3h[:, bass.ds(t * (2 * D) + part * D, D)]

        def w1(e, part, k):
            return wslot[e][:, part * 2 * F + k * F:part * 2 * F + (k + 1) * F]

        def w2(e, part, k):
            return wslot[e][:, (2 + part) * 2 * F + k * D:(2 + part) * 2 * F + (k + 1) * D]

        slotZ = R2[:, 0:2 * COLS].bitcast(I32)

        DEG = 3 * P

        s_const = sem("s_const")
        s_blank = sem("s_blank")
        s_edges = sem("s_edges")
        s_zero = sem("s_zero")
        s_table = sem("s_table")
        s_x = sem("s_x")
        s_xz = sem("s_xz")
        s_w = sem("s_w")
        s_oh = sem("s_oh")
        s_tp = sem("s_tp")
        s_ot = sem("s_ot")
        s_eq = sem("s_eq")
        s_h = sem("s_h")
        s_m = sem("s_m")
        s_t = sem("s_t")
        s_r = sem("s_r")
        s_rk = sem("s_rk")
        s_pos = sem("s_pos")
        s_stage = sem("s_stage")
        s_sc = [sem("s_sc0"), sem("s_sc1")]

        s_stat = sem("s_stat")
        s_std = sem("s_std")
        s_xn = sem("s_xn")
        s_xhi = sem("s_xhi")
        s_xl = sem("s_xl")
        s_xlo = sem("s_xlo")
        s_xt = sem("s_xt")
        s_xtc = sem("s_xtc")
        s_pm = sem("s_pm")
        s_vm = sem("s_vm")

        s_slot = sem("s_slot")
        s_tabs = sem("s_tabs")
        s_r3 = sem("s_r3")
        s_flag = sem("s_flag")
        s_fp = sem("s_fp")
        s_ends = sem("s_ends")
        s_of = [sem(f"s_of{i}") for i in range(2)]
        s_oi = [sem(f"s_oi{i}") for i in range(2)]
        s_oj = [sem(f"s_oj{i}") for i in range(2)]
        s_ox = [sem(f"s_ox{i}") for i in range(2)]
        s_oy = [sem(f"s_oy{i}") for i in range(2)]
        s_os = [sem(f"s_os{i}") for i in range(2)]
        s_ol = [sem(f"s_ol{i}") for i in range(2)]
        s_o1 = [sem(f"s_o1{i}") for i in range(2)]
        s_o2 = [sem(f"s_o2{i}") for i in range(2)]
        s_o3 = [sem(f"s_o3{i}") for i in range(2)]
        s_o4 = [sem(f"s_o4{i}") for i in range(2)]
        s_o5v = [sem(f"s_o5{i}") for i in range(2)]
        s_o6 = [sem(f"s_o6{i}") for i in range(2)]
        s_oo = [sem(f"s_oo{i}") for i in range(2)]
        s_bl = [sem(f"s_bl{i}") for i in range(2)]
        s_ab = [sem(f"s_ab{i}") for i in range(2)]
        s_ap = [sem(f"s_ap{i}") for i in range(2)]
        s_ag = [sem(f"s_ag{i}") for i in range(2)]
        s_an = [sem(f"s_an{i}") for i in range(2)]
        s_at = sem("s_at")
        s_ac = sem("s_ac")
        s_xr = sem("s_xr")
        s_xrf = sem("s_xrf")

        s_x4 = [sem(f"s_x4{i}") for i in range(2)]
        s_xT = sem("s_xT")
        s_sq = sem("s_sq")
        s_sp = sem("s_sp")
        s_sr = sem("s_sr")
        s_sc2 = sem("s_sc2")
        s_ch = sem("s_ch")
        s_cl = sem("s_cl")
        s_hp = sem("s_hp")
        s_hr = sem("s_hr")
        s_hl = sem("s_hl")
        s_yp = sem("s_yp")
        s_yh = sem("s_yh")
        s_zc = sem("s_zc")
        s_yl = sem("s_yl")

        s_wl = sem("s_wl")
        s_wq = sem("s_wq")
        s_wr = sem("s_wr")
        s_wt = sem("s_wt")
        s_wc = sem("s_wc")
        s_wh = sem("s_wh")
        s_wo = sem("s_wo")
        s_wst = sem("s_wst")
        s_gl = sem("s_gl")
        s_gs = sem("s_gs")
        s_v2 = sem("s_v2")
        s_x2 = sem("s_x2")
        s_d2 = sem("s_d2")
        s_n2 = sem("s_n2")
        s_t2 = sem("s_t2")
        s_h2 = sem("s_h2")
        s_l2 = sem("s_l2")
        s_lp = sem("s_lp")
        s_lr = sem("s_lr")
        s_we = [sem(f"s_we{e}") for e in range(EXPERTS)]
        s_wg = sem("s_wg")
        s_gv = sem("s_gv")
        s_gp = sem("s_gp")
        s_lv = sem("s_lv")
        s_le = sem("s_le")
        s_cb = sem("s_cb")
        s_ct = sem("s_ct")
        s_cc = sem("s_cc")
        s_bp = sem("s_bp")
        s_ai = sem("s_ai")
        s_xr5 = sem("s_xr5")
        s_up = sem("s_up")
        s_ua = sem("s_ua")
        s_us = sem("s_us")
        s_dp = sem("s_dp")
        s_da = sem("s_da")
        s_st = sem("s_st")
        s_o5 = sem("s_o5")

        block = ctx.enter_context(nc.Block())

        @block.sync
        def _(sp):
            sp.wait_ge(s_blank, 1)
            for end, arr in (("src", eS), ("dst", eD)):
                v = io[end][0:(P - 1) * E].rearrange("(p c) -> p c", c=E)
                sp.dma_start(arr[0:112, 0:E], v[0:112, :]).then_inc(s_edges, 16)
                sp.dma_start(arr[112:127, 0:E], v[112:127, :]).then_inc(s_edges, 16)
                sp.dma_start(arr[127:128, 0:LASTE],
                             io[end][(P - 1) * E:EDGES].rearrange("(a n) -> a n", a=1)).then_inc(s_edges, 16)
            sp.wait_ge(s_zero, 1)
            sp.dma_start(slots_dram[0:TRASH, :].rearrange("(p c) a -> p (c a)", p=P),
                         slotZ[:, :]).then_inc(s_table, 16)
            sp.dma_start(xin, io["x"][0:P, :]).then_inc(s_x, 16)
            sp.dma_start(rows[0:1, SPARE, 0:64], io["L0_mix_bk"][0:64].rearrange("(a n) -> a n", a=1)).then_inc(s_xT, 16)
            for name, dst in (("L0_mix_Wq", Wq), ("L0_mix_Wk", Wk), ("L0_mix_Wv", Wv), ("L0_mix_Wfc", Wfc),
                              ("L0_gnn_W0_0", W0s), ("L0_gnn_W1_0", W1s),
                              ("L0_gnn_W1_1", Wc[:, :, 0:D]), ("L0_gnn_W0_1", Wc[:, :, D:2 * D])):
                sp.dma_start(dst, io[name].rearrange("(k p) n -> p k n", p=P)).then_inc(s_w, 16)
            for name, r in (("L0_mix_bk", BK), ("L0_mix_bv", BV), ("L0_mix_bfc", BFC),
                            ("L0_gnn_b0_1", B01), ("L0_gnn_b1_1", B11)):
                sp.dma_start(rows[0:1, r, :], io[name].rearrange("(a n) -> a n", a=1)).then_inc(s_w, 16)
            sp.dma_start(bqc, io["L0_mix_bq"].rearrange("(k p) -> p k", p=P)).then_inc(s_w, 16)
            sp.dma_start(bh[:, 0, :], io["L0_gnn_b0_0"].rearrange("(k p) -> p k", p=P)).then_inc(s_w, 16)
            sp.dma_start(bh[:, 1, :], io["L0_gnn_b1_0"].rearrange("(k p) -> p k", p=P)).then_inc(s_w, 16)
            with sp.Fori(1, T - 1) as t:
                sp.wait_ge(s_xn, t)
                sp.dma_start(xin, io["x"][bass.ds(t * P, P), :]).then_inc(s_x, 16)
                sp.wait_ge(s_xtc, t + 1)
                sp.dma_start(xT_dram[bass.ds(t * P - P, P), :], xst).then_inc(s_xT, 16)
            sp.wait_ge(s_xn, T - 1)
            sp.dma_start(xin[LAST:P, :], zeros32[LAST:P, :]).then_inc(s_xz, 16)
            sp.wait_ge(s_xz, 16)
            sp.dma_start(xin[0:LAST, :], io["x"][(T - 1) * P:N, :]).then_inc(s_x, 16)
            for t in (T - 2, T - 1):
                sp.wait_ge(s_xtc, t + 2)
                sp.dma_start(xT_dram[t * P:(t + 1) * P, :], xst).then_inc(s_xT, 16)
            sp.wait_ge(s_sc[0], 16 + 16 * G * (GROUPS // 2))
            sp.wait_ge(s_sc[1], 16 + 16 * G * (GROUPS // 2))
            sp.wait_ge(s_vm, 12)
            sp.wait_ge(s_pm, 10)
            sp.wait_ge(s_sr, 1)
            sp.wait_ge(s_xT, 16 + 16 * T)
            sp.dma_start(slotI, slots_dram[0:TRASH, :].rearrange("(p c) a -> p (c a)", p=P)).then_inc(s_slot, 16)
            def load4(g, par):
                rows4 = xT_dram[g * (W * P):(g + 1) * (W * P), :] if isinstance(g, int) else \
                    xT_dram[bass.ds(g * (W * P), W * P), :]
                sp.dma_start(xT4[par].rearrange("p (t c) -> p t c", t=W),
                             rows4.rearrange("(t p) c -> p t c", p=P)).then_inc(s_x4[par], 16)

            sp.wait_ge(s_ac, 1 + T)
            load4(0, 0)
            load4(1, 1)
            with sp.Fori(1, T // W // 2) as k:
                for par in range(2):
                    sp.wait_ge(s_yp, k * (2 * W) + par * W)
                    load4(2 * k + par, par)
            sp.wait_ge(s_yp, T - W)
            load4(T // W - 1, 0)
            sp.wait_ge(s_yp, W + T)
            sp.wait_ge(s_wst, 16 * EXPERTS)
            sp.dma_start(graw, io["L0_ffn_Wg"].rearrange("(k p) n -> p k n", p=P)).then_inc(s_gl, 16)
            for r, name in enumerate(("L0_ffn_bg", "L0_ffn_bias")):
                sp.dma_start(grows[0:1, r, :], io[name].rearrange("(a n) -> a n", a=1)).then_inc(s_wg, 16)
            for e in range(2):
                sp.dma_start(wslot[e], w_dram[e, :, :]).then_inc(s_we[e], 16)
            sp.dma_start(b2s[0:EXPERTS, :], io["L0_ffn_b2"]).then_inc(s_st, 16)
            sp.dma_start(xres, io["x"][0:P, :]).then_inc(s_xr, 16)
            with sp.Fori(1, T - 1) as t:
                sp.wait_ge(s_xrf, t + 1)
                sp.dma_start(xres, io["x"][bass.ds(t * P, P), :]).then_inc(s_xr, 16)
                sp.dma_start(x2_dram[bass.ds(t * P - P, P), :], x2b).then_inc(s_x2, 16)
            sp.wait_ge(s_xrf, T)
            sp.dma_start(xres[0:LAST, :], io["x"][(T - 1) * P:N, :]).then_inc(s_xr, 16)
            sp.dma_start(x2_dram[(T - 2) * P:(T - 1) * P, :], x2b).then_inc(s_x2, 16)
            sp.wait_ge(s_xrf, T + 1)
            sp.dma_start(x2_dram[(T - 1) * P:T * P, :], x2b).then_inc(s_x2, 16)
            sp.wait_ge(s_ap[1], Q + T * Q)
            for e in range(2, EXPERTS):
                sp.dma_start(wslot[e], w_dram[e, :, :]).then_inc(s_we[e], 16)
            sp.wait_ge(s_lp, T)
            sp.wait_ge(s_lr, 1 + T)
            sp.wait_ge(s_x2, 16 * T)
            sp.dma_start(xr5, x2_dram[0:W * P, :].rearrange("(t p) c -> p t c", p=P)).then_inc(s_xr5, 16)
            with sp.Fori(1, T // W) as g:
                sp.wait_ge(s_da, g * 32 - 24)
                sp.dma_start(xr5, x2_dram[bass.ds(g * (W * P), W * P), :].rearrange("(t p) c -> p t c", p=P))\
                  .then_inc(s_xr5, 16)
                sp.wait_ge(s_da, g * 32 + 4)
                sp.dma_start(io["out"][bass.ds(g * (W * P) - W * P, W * P), :].rearrange("(t p) c -> p t c", p=P),
                             acc).then_inc(s_st, 16)
            sp.wait_ge(s_da, 4 + 32 * (T // W))
            sp.dma_start(io["out"][(T - W) * P:(T - 1) * P, :].rearrange("(t p) c -> p t c", p=P),
                         acc[:, 0:W - 1, :]).then_inc(s_o5, 16)
            sp.dma_start(io["out"][(T - 1) * P:N, :], acc[0:LAST, W - 1, :]).then_inc(s_o5, 16)
            sp.wait_ge(s_st, 16 * (T // W))
            sp.wait_ge(s_o5, 32)

        @block.gpsimd
        def _(pool):
            allow = dict(allow_small_or_imprecise_dtypes=True)
            nc.gpsimd.iota(iota128[:, :, :], [[1, P], [0, G]], base=0, channel_multiplier=0, **allow)
            nc.gpsimd.iota(iota49[:, :, :], [[1, T], [0, G]], base=0, channel_multiplier=0, **allow)
            nc.gpsimd.iota(iotaB[:, :, :], [[1, P], [0, QB]], base=1, channel_multiplier=0, **allow)
            nc.gpsimd.iota(trash[:, :], [[1, EP]], base=TRASH, channel_multiplier=EP)
            nc.gpsimd.iota(iota8[:, :], [[1, 8]], base=0, channel_multiplier=0, **allow)
            nc.gpsimd.iota(zrow[:, :], [[0, 1]], base=OVROW, channel_multiplier=1, **allow)
            nc.gpsimd.memset(zeros32[:, :], 0.0)
            nc.gpsimd.memset(zeros16[:, :], 0.0)
            nc.gpsimd.memset(ident[:, :], 0.0)
            nc.gpsimd.memset(ident16[:, :], 0.0)
            nc.gpsimd.memset(ones[:, :], 1.0)
            nc.gpsimd.memset(epsc[:, :], EPS)
            nc.gpsimd.memset(neg4[:, :, :], -1.0)
            nc.gpsimd.memset(hmask, 1.0)
            pool.drain()
            for m in (ident, ident16):
                nc.gpsimd.affine_select(out=m[:, :], in_=m[:, :], compare_op=ALU.not_equal, fill=1.0,
                                        base=0, pattern=[[-1, P]], channel_multiplier=1)
            nc.gpsimd.affine_select(out=neg4[:, :, :], in_=neg4[:, :, :], compare_op=ALU.is_ge, fill=0.0,
                                    base=0, pattern=[[0, 4], [-1, P]], channel_multiplier=1)
            hv = hmask.rearrange("p k (b c) -> p k b c", c=D // HEADS)
            nc.gpsimd.affine_select(out=hv, in_=hv, compare_op=ALU.is_ge, fill=0.0, base=0,
                                    pattern=[[P, 2], [-(D // HEADS), HEADS], [0, D // HEADS]], channel_multiplier=1)
            pool.drain()
            nc.gpsimd.affine_select(out=hv, in_=hv, compare_op=ALU.is_ge, fill=0.0, base=D // HEADS - 1,
                                    pattern=[[-P, 2], [D // HEADS, HEADS], [0, D // HEADS]],
                                    channel_multiplier=-1).then_inc(s_const, 1)
            for i in range(2):
                pool.dma_start(rows[0:1, SPARE, 64 * (i + 1):64 * (i + 2)],
                               io["L0_mix_bk"][0:64].rearrange("(a n) -> a n", a=1)).then_inc(s_sc[i], 16)
            nc.gpsimd.memset(pwait[:, :], 0.0).then_inc(s_stage, 1)
            pool.wait_ge(s_table, 16)

            with pool.Fori(0, GROUPS // 2) as k:
                for par in range(2):
                    pool.wait_ge(s_pos, 2 * k + par + 1)
                    pool.wait_ge(s_stage, 2 * k + par + 1)
                    nc.gpsimd.tensor_tensor(pwait[:, 0:1], ones[:, 0:1], ones[:, 0:1], ALU.add).then_inc(s_stage, 1)
                    for c in range(G):
                        pool.indirect_dma_start(
                            out=slots_dram, out_offset=bass.IndirectOffsetOnAxis(ap=stP[par][:, c:c + 1], axis=0),
                            in_=stR[par][:, c:c + 1], in_offset=None).then_inc(s_sc[par], 16)
            pool.wait_ge(s_flag, 2)
            for i, ends in enumerate((eS, eD)):
                pool.dma_start(ends_dram[i, :, :], ends).then_inc(s_ends, 16)
            pool.wait_ge(s_ends, 32)
            nc.gpsimd.memset(R3[:, :], 0.0).then_inc(s_r3, 1)

            def wait(s, n):
                pool.drain()
                pool.wait_ge(s, n)
                nc.gpsimd.tensor_tensor(pwait[:, 0:1], ones[:, 0:1], ones[:, 0:1], ALU.add)

            def overflow(L):
                pool.dma_start(feat_dram[0:T * P, :].rearrange("(t p) c -> p t c", p=P),
                               R2[:, :].rearrange("p (t c) -> p t c", t=T)).then_inc(s_of[L], 16)
                pool.dma_start(feat_dram[T * P:(T + 1) * P, :], zeros32[:, :].bitcast(F16)).then_inc(s_of[L], 16)
                for i in range(2):
                    pool.dma_start(sum_dram[:, i * D:(i + 1) * D].rearrange("(t p) c -> p t c", p=P),
                                   zeros32[:, :].rearrange("p (a c) -> p a c", a=1).to_broadcast([P, T + 2, D]))\
                        .then_inc(s_of[L], 16)
                wait(s_of[L], 64)
                with pool.Fori(0, E) as c:
                    for i in range(2):
                        m = 2 * c + i
                        pool.dma_start(oa, ends_dram[i, :, bass.ds(c, 1)]).then_inc(s_oi[L], 16)
                        pool.dma_start(ob, ends_dram[1 - i, :, bass.ds(c, 1)]).then_inc(s_oj[L], 16)
                        wait(s_oi[L], m * 16 + 16)
                        wait(s_oj[L], m * 16 + 16)
                        pool.indirect_dma_start(out=oX, out_offset=None, in_=feat_dram,
                                                in_offset=bass.IndirectOffsetOnAxis(ap=oa, axis=0)).then_inc(s_ox[L], 16)
                        pool.indirect_dma_start(out=oA, out_offset=None, in_=sum_dram,
                                                in_offset=bass.IndirectOffsetOnAxis(ap=ob, axis=0)).then_inc(s_oy[L], 16)
                        wait(s_o5v[L], m + 1)
                        pool.indirect_dma_start(out=sum_dram, out_offset=bass.IndirectOffsetOnAxis(ap=ow, axis=0),
                                                in_=oN, in_offset=None).then_inc(s_os[L], 16)
                        wait(s_os[L], m * 16 + 16)
                with pool.Fori(0, T) as t:
                    pool.dma_start(oA, sum_dram[bass.ds(t * P, P), :]).then_inc(s_ol[L], 16)
                    wait(s_o6[L], t + 1)

            lacking = pool.value_load(flag[0:1, 0:1])
            pool.wait_ge(s_xlo, 1 + T)
            pool.wait_ge(s_tabs, 1)
            with pool.If(lacking > 0):
                overflow(0)
            pool.wait_ge(s_ac, 1 + T)

            def expert(e, first):
                if not first:
                    wait(s_wst, e * 16)
                if first:
                    w1s, w2s, b1s = (io[f"L0_ffn_{n}"][0:1] for n in ("W1", "W2", "b1"))
                else:
                    w1s, w2s, b1s = (io[f"L0_ffn_{n}"][bass.ds(e, 1)] for n in ("W1", "W2", "b1"))
                pool.dma_start(wraw[:, 0:2 * F].rearrange("p (k n) -> p k n", k=2),
                               w1s.rearrange("a (k p) n -> p (a k) n", p=P)).then_inc(s_wl, 16)
                pool.dma_start(wraw[:, 2 * F:4 * F].rearrange("p (k n) -> p k n", k=4),
                               w2s.rearrange("a (k p) n -> p (a k) n", p=P)).then_inc(s_wl, 16)
                pool.dma_start(braw, b1s.rearrange("a (f p) -> p (a f)", p=P)).then_inc(s_wl, 16)
                wait(s_wq, e + 1)
                nc.gpsimd.partition_all_reduce(nr3, sq3, P, RADD).then_inc(s_wr, 1)
                wait(s_wh, e + 1)
                wait(s_wo, e + 1)
                dst = w_dram[0, :, :] if first else w_dram[bass.ds(e, 1), :, :].rearrange("a p c -> (a p) c")
                pool.dma_start(dst, wout).then_inc(s_wst, 16)

            expert(0, True)
            with pool.Fori(1, EXPERTS) as e:
                expert(e, False)
            pool.wait_ge(s_yl, 1 + T)
            pool.wait_ge(s_zc, 3 + T)
            with pool.If(lacking > 0):
                overflow(1)

        @block.vector
        def _(dve):
            v = nc.vector
            v.memset(R3i[:, 0:2 * EP], PADNODE)
            v.memset(Tsn[0], 0.0)
            v.memset(Tsn[1], 0.0).then_inc(s_blank, 1)
            v.memset(slotZ, 0).then_inc(s_zero, 1)
            v.memset(small[:, 0:1], 0.0).then_inc(s_t, 1)
            v.memset(small[:, 1:2], 0.0).then_inc(s_rk, 1)
            v.memset(small[:, 2:3], 0.0).then_inc(s_xtc, 1)
            v.memset(small[:, 3:4], 0.0).then_inc(s_ac, 1)
            v.memset(small[:, 4:5], 0.0).then_inc(s_an[0], 1)
            v.memset(small[:, 5:6], 0.0).then_inc(s_an[1], 1)
            v.memset(small[:, 6:7], 0.0).then_inc(s_zc, 3)
            v.memset(small[:, 7:8], 0.0).then_inc(s_xrf, 1)
            v.memset(small[:, 8:9], 0.0).then_inc(s_da, 4)
            v.memset(small[:, 9:10], 0.0).then_inc(s_us, 4)
            v.memset(small[:, 11:12], 0.0).then_inc(s_lr, 1)
            v.memset(small[:, 12:13], 0.0).then_inc(s_hl, 4)
            dve.wait_ge(s_edges, 96)
            v.tensor_tensor(eHi, eS, eD, ALU.max)
            v.tensor_tensor(eLo, eS, eD, ALU.min)
            dve.drain()
            v.tensor_scalar(eTi, eHi, 7, None, ALU.logical_shift_right)
            v.tensor_scalar(eTj, eLo, 7, None, ALU.logical_shift_right)
            dve.drain()
            v.tensor_scalar(eHi, eHi, P - 1, None, ALU.bitwise_and)
            v.tensor_scalar(eLo, eLo, P - 1, None, ALU.bitwise_and)
            v.tensor_copy(fTi, eTi)
            v.tensor_copy(fTj, eTj)
            dve.drain()
            v.tensor_copy(fHi, eHi)
            v.tensor_copy(fLo, eLo)
            v.scalar_tensor_tensor(out=rec, in0=eHi, scalar=256.0, in1=eLo, op0=ALU.mult, op1=ALU.add)
            v.scalar_tensor_tensor(out=binb, in0=eTi, scalar=float(T), in1=eTj, op0=ALU.mult, op1=ALU.add)
            v.tensor_tensor(diag, eTi, eTj, ALU.is_equal)
            v.tensor_scalar(delta, eTi, -float(T), float(BINS), ALU.mult, ALU.add)
            v.tensor_scalar(inval, eTi, float(T), None, ALU.is_ge)
            dve.drain()
            v.tensor_scalar(rec, rec, 257.0, None, ALU.add)
            dve.drain()
            dve.wait_ge(s_const, 1)

            def onehots(par, g):
                dve.wait_ge(s_r, g + 1)
                for out, key, pat, m in ((OHi, fTi, iota49, T), (OHj, fTj, iota49, T),
                                         (LHi, fHi, iota128, P), (LLo, fLo, iota128, P)):
                    kb = key[:, bass.ds(g * G, G)].rearrange("p (a b) -> p a b", a=1).to_broadcast([P, m, G])
                    last = v.tensor_tensor(out[par], pat[:, :, :], kb, ALU.is_equal)
                last.then_inc(s_oh, 1)

            def counts(par, g):
                dve.wait_ge(s_h, g + 1)
                v.tensor_copy(Tsn[par][0:T, 0, :], Tsn[1 - par][0:T, G, :])
                t0 = Tsn[1 - par][0:T, G, :].rearrange("p (a j) -> p a j", a=1).to_broadcast([T, G, T])
                v.scalar_tensor_tensor(out=Tsn[par][0:T, 1:G + 1, :], in0=t0, scalar=1024.0,
                                       in1=banks[3][0:T, 0:G * T].rearrange("p (g j) -> p g j", j=T),
                                       op0=ALU.min, op1=ALU.add).then_inc(s_t, 1)

            def ranks(par, g, k):
                sl = bass.ds(g * G, G)
                dve.wait_ge(s_r, g + 3)
                v.tensor_tensor(prod, banks[4][:, 0:G * T].rearrange("p (g j) -> p g j", j=T),
                                OHj[par].rearrange("p j g -> p g j"), ALU.mult).then_inc(s_rk, 1)
                dve.drain()
                v.tensor_reduce(rank[:, sl], prod, AX.X, ALU.add)
                dve.drain()
                v.scalar_tensor_tensor(out=d1, in0=rank[:, sl], scalar=float(P), in1=diag[:, sl],
                                       op0=ALU.is_ge, op1=ALU.mult)
                dve.drain()
                v.scalar_tensor_tensor(out=rr, in0=d1, scalar=-float(P), in1=rank[:, sl],
                                       op0=ALU.mult, op1=ALU.add)
                v.tensor_tensor(ee, d1, delta[:, sl], ALU.mult)
                dve.drain()
                v.tensor_tensor(bb, ee, binb[:, sl], ALU.add)
                v.scalar_tensor_tensor(out=ov, in0=rr, scalar=float(P), in1=inval[:, sl],
                                       op0=ALU.is_ge, op1=ALU.max)
                dve.drain()
                v.tensor_copy(delta[:, sl], ov)
                v.scalar_tensor_tensor(out=pp, in0=rr, scalar=float(COLS), in1=bb, op0=ALU.mult, op1=ALU.add)
                dve.drain()
                v.scalar_tensor_tensor(out=tq, in0=pp, scalar=-1.0, in1=trash[:, sl], op0=ALU.mult, op1=ALU.add)
                dve.drain()
                v.tensor_tensor(tr, tq, ov, ALU.mult)
                dve.drain()
                dve.wait_ge(s_sc[par], 16 * G * k + 16)
                v.tensor_copy(stR[par][:, :], rec[:, sl])
                v.tensor_tensor(stP[par][:, :], tr, pp, ALU.add).then_inc(s_pos, 1)

            def variance(t):
                dve.wait_ge(s_x, 16 * t + 16)
                v.bn_stats(stats[:, :], xin)
                dve.drain()
                v.bn_aggr(mv[:, :], stats[:, :]).then_inc(s_stat, 1)

            def normal(t):
                dve.wait_ge(s_std, t + 1)
                v.reciprocal(rstd[:, :], rstd[:, :])
                dve.drain()
                dve.wait_ge(s_xt, t + 1)
                v.tensor_scalar(xs[:, 0:D], xin, mv[:, 0:1], rstd[:, 0:1],
                                ALU.subtract, ALU.mult).then_inc(s_xn, 1)

            def low(t):
                dve.wait_ge(s_xhi, t + 1)
                dve.wait_ge(s_xlo, t + 1)
                v.scalar_tensor_tensor(out=xlo, in0=xs[:, 0:D], scalar=S, in1=R2[:, bass.ds(t * 2 * D, D)],
                                       op0=ALU.mult, op1=ALU.subtract).then_inc(s_xl, 1)

            def place(t):
                dve.wait_ge(s_xt, t + 2)
                dve.wait_ge(s_xT, 16 * t + 16)
                v.tensor_copy(xst, banks[5][:, 0:D]).then_inc(s_xtc, 1)

            def two_groups(k, norm):
                onehots(1, 2 * k + 1)
                if norm:
                    variance(k)
                counts(0, 2 * k)
                ranks(0, 2 * k, k)
                if norm:
                    normal(k)
                onehots(0, 2 * k + 2)
                if norm:
                    low(k)
                counts(1, 2 * k + 1)
                ranks(1, 2 * k + 1, k)
                if norm:
                    place(k)

            v.memset(xs[:, D:D + 1], 1.0)
            onehots(0, 0)
            with dve.Fori(0, T) as k:
                two_groups(k, True)
            with dve.Fori(T, GROUPS // 2) as k:
                two_groups(k, False)

            def copied(ins):
                ins.then_inc(s_vm, 1)

            def k2(ap):
                return ap.rearrange("p (k n) -> p k n", k=2)

            dve.wait_ge(s_pm, 1)
            v.tensor_copy(Gs[:, 0, :], banks[6][:, 0:D + 1])
            copied(v.tensor_copy(Gs[:, 1, :], banks[7][:, 0:D + 1]))
            for i, dst in enumerate((WkT, WvT, WfT)):
                dve.wait_ge(s_pm, 2 + i)
                copied(v.tensor_copy(dst, k2(banks[i][:, :])))
            dve.wait_ge(s_pm, 5)
            v.tensor_copy(B1s, k2(banks[3][:, :]))
            v.tensor_copy(rows[0:1, SV, :], banks[4][0:1, 0:D])
            copied(v.scalar_tensor_tensor(out=rows[0:1, SK, :], in0=rows[0:1, BK, :], scalar=float(N),
                                          in1=banks[4][0:1, D:2 * D], op0=ALU.mult, op1=ALU.add))
            dve.wait_ge(s_pm, 6)
            copied(v.scalar_tensor_tensor(out=PTs, in0=k2(banks[0][:, :]), scalar=1.0 / N, in1=hmask,
                                          op0=ALU.mult, op1=ALU.mult))
            dve.wait_ge(s_pm, 7)
            copied(v.tensor_copy(Rs, k2(banks[1][:, :])))
            dve.wait_ge(s_pm, 8)
            v.tensor_copy(Ms[:, :, :], k2(banks[2][:, :]))
            v.tensor_tensor(rows[0:1, ZB, :], banks[3][0:1, 0:D], rows[0:1, BFC, :], ALU.add)
            v.tensor_tensor(bhs[:, :], bh[:, 0, :], bh[:, 1, :], ALU.add)
            dve.drain()
            v.tensor_tensor(rows[0:1, SPARE, :], rows[0:1, ZB, :], rows[0:1, B01, :], ALU.add)
            dve.drain()
            copied(v.tensor_tensor(rows[0:1, ZB, :], rows[0:1, SPARE, :], rows[0:1, B11, :], ALU.add))
            dve.wait_ge(s_pm, 9)
            copied(v.tensor_copy(zb[:, :], banks[4][:, 0:D]))
            copied(v.tensor_copy(degT[0:T, :], banks[6][0:T, DEG:DEG + P]))
            dve.wait_ge(s_pm, 10)
            v.tensor_scalar(deg[:, :], banks[1][:, 0:T], 1.0, None, ALU.max)
            dve.drain()
            copied(v.reciprocal(rdeg[:, :], deg[:, :]))
            dve.drain()
            copied(v.tensor_scalar(rd1[:, :], rdeg[:, :], 1.0 / S, None, ALU.mult))

            dve.wait_ge(s_sr, 1)
            v.tensor_tensor(small[:, 45:46], small[:, 40:41], small[:, 41:42], ALU.add)
            v.tensor_tensor(vals[:, 1:2], small[:, 43:44], small[:, 44:45], ALU.add)
            dve.drain()
            v.scalar_tensor_tensor(out=vals[:, 0:1], in0=small[:, 45:46], scalar=float(D) ** 0.5,
                                   in1=small[:, 42:43], op0=ALU.mult, op1=ALU.add)
            dve.drain()
            v.tensor_tensor(vals[:, 2:3], vals[:, 0:1], small[:, 43:44], ALU.mult)
            dve.drain()
            v.tensor_scalar(small[:, 20:23], vals, 2.0 ** -40, 2.0 ** 60, ALU.max, ALU.min)
            dve.drain()
            v.tensor_scalar(smalli[:, 24:27], smalli[:, 20:23], 23, None, ALU.logical_shift_right)
            dve.drain()
            v.tensor_scalar(smalli[:, 28:31], smalli[:, 24:27], -1.0, 267.0, ALU.mult, ALU.add)
            v.tensor_scalar(smalli[:, 32:35], smalli[:, 24:27], -13.0, None, ALU.add)
            dve.drain()
            v.tensor_scalar(smalli[:, 48:51], smalli[:, 28:31], 23, None, ALU.logical_shift_left)
            v.tensor_scalar(smalli[:, 51:54], smalli[:, 32:35], 23, None, ALU.logical_shift_left)
            dve.drain()
            v.tensor_tensor(unsc, small[:, 51:52], small[:, 52:53], ALU.mult)
            v.tensor_tensor(small[:, 58:59], small[:, 48:49], small[:, 49:50], ALU.mult)
            v.tensor_scalar(sbh, bhs[:, :], hsc, None, ALU.mult)
            dve.drain()
            v.tensor_tensor(ysc, unsc, small[:, 50:51], ALU.mult)
            v.tensor_scalar(Ms[:, :, :], Ms[:, :, :], small[:, 58:59], None, ALU.mult)
            v.tensor_scalar(rd2[:, :], rdeg[:, :], small[:, 53:54], None, ALU.mult).then_inc(s_sc2, 1)

            v.tensor_tensor(rank, delta, inval, ALU.subtract)
            dve.drain()
            v.tensor_reduce(small[:, 56:57], rank[:, 0:E], AX.X, ALU.add)
            v.memset(rank[:, E:EP], 0.0)
            for ends, t1, t2 in ((eS, binb, diag), (eD, delta, inval)):
                v.tensor_scalar(t1, ends, zrow[:, 0:1], None, ALU.subtract)
                dve.drain()
                v.tensor_tensor(t2, t1, rank, ALU.mult)
                dve.drain()
                v.tensor_scalar(ends, t2, zrow[:, 0:1], None, ALU.add)
            dve.drain()
            v.memset(small[:, 57:58], 0.0).then_inc(s_flag, 1)
            dve.wait_ge(s_fp, 1)
            v.tensor_copy(flag[:, :], banks[2][:, 0:1]).then_inc(s_flag, 1)

            dve.wait_ge(s_slot, 16)
            v.tensor_scalar(hiI, slotI, 8, None, ALU.logical_shift_right)
            dve.drain()
            v.tensor_copy(HI, hiI)
            v.tensor_scalar(slotI, slotI, 255, None, ALU.bitwise_and)
            dve.drain()
            v.tensor_copy(LO, slotI)
            v.memset(TT[:, T * TC:(T + 1) * TC], 0.0)
            v.memset(TU[:, T * TC:(T + 1) * TC], 0.0)
            dve.drain()
            tv, uv = (x[:, 0:T * TC].rearrange("p (t u) -> p t u", u=TC) for x in (TT, TU))
            hv, lv = (x[:, 0:BINS].rearrange("p (t u) -> p t u", u=T) for x in (HI, LO))
            v.tensor_tensor(tv[:, :, 0:T], hv, lv.rearrange("p t u -> p u t"), ALU.max)
            v.tensor_tensor(uv[:, :, 0:T], lv, hv.rearrange("p t u -> p u t"), ALU.max)
            dve.drain()
            hd, ld = (x[:, 0:BINS:T + 1] for x in (HI, LO))
            v.tensor_copy(TT[:, 0:T * TC:TC + 1], hd)
            v.tensor_copy(TU[:, 0:T * TC:TC + 1], ld)
            v.tensor_copy(tv[:, :, T], ld)
            v.tensor_copy(uv[:, :, T], hd)
            v.tensor_copy(tv[:, :, T + 1], HI[:, BINS:COLS])
            v.tensor_copy(uv[:, :, T + 1], LO[:, BINS:COLS])
            v.tensor_copy(tv[:, :, T + 2], LO[:, BINS:COLS])
            v.tensor_copy(uv[:, :, T + 2], HI[:, BINS:COLS])
            dve.drain()
            v.memset(small[:, 10:11], 0.0).then_inc(s_tabs, 1)

            def pairs(L, n, q, col):
                dve.wait_ge(s_bl[L], n + 1)
                for out, tab in ((OT, TT), (OU, TU)):
                    kb = tab[:, bass.ds(col, QB)].rearrange("p (a b) -> p a b", a=1).to_broadcast([P, P, QB])
                    last = v.tensor_tensor(out[q], iotaB[:, :, :], kb, ALU.is_equal)
                last.then_inc(s_oo[L], 1)

            def finish1(t):
                dve.wait_ge(s_ag[0], t + 3)
                v.scalar_tensor_tensor(out=aggc, in0=aggr[:, D:2 * D], scalar=1.0 / S, in1=aggr[:, 0:D],
                                       op0=ALU.mult, op1=ALU.add)
                dve.drain()
                v.scalar_tensor_tensor(out=aggn, in0=aggc, scalar=rd1[:, bass.ds(t, 1)],
                                       in1=R3[:, bass.ds(t * D, D)],
                                       op0=ALU.mult, op1=ALU.add).then_inc(s_an[0], 1)

            def place1(t):
                dve.wait_ge(s_at, t + 1)
                v.tensor_copy(R3[:, bass.ds(t * D, D)], banks[6][:, 0:D]).then_inc(s_ac, 1)

            def finish2(t):
                dve.wait_ge(s_ag[1], t + 3)
                v.scalar_tensor_tensor(out=aggc, in0=aggr[:, D:2 * D], scalar=1.0 / S, in1=aggr[:, 0:D],
                                       op0=ALU.mult, op1=ALU.add)
                dve.drain()
                v.scalar_tensor_tensor(out=aggn, in0=aggc, scalar=rd2[:, bass.ds(t, 1)],
                                       in1=R3[:, bass.ds(t * D, D)],
                                       op0=ALU.mult, op1=ALU.add).then_inc(s_an[1], 1)
                dve.drain()
                dve.wait_ge(s_xr, t * 16 + 16)
                v.tensor_tensor(x2b, aggn, xres, ALU.add).then_inc(s_xrf, 1)
                dve.drain()
                v.bn_stats(x2s, x2b)
                dve.drain()
                v.bn_aggr(x2m, x2s).then_inc(s_v2, 1)

            def normal2(t):
                dve.wait_ge(s_d2, t + 1)
                v.reciprocal(x2r, x2r)
                dve.drain()
                v.tensor_scalar(x2n, x2b, x2m[:, 0:1], x2r, ALU.subtract, ALU.mult).then_inc(s_n2, 1)

            def low2(t):
                dve.wait_ge(s_h2, t + 1)
                v.scalar_tensor_tensor(out=R3t(t, 1), in0=banks[6][:, 0:D], scalar=S, in1=R3t(t, 0),
                                       op0=ALU.mult, op1=ALU.subtract).then_inc(s_l2, 1)

            def logits2(t):
                dve.wait_ge(s_lp, t + 1)
                v.tensor_reduce(lraw, banks[6][:, D:D + 24].rearrange("p (g n) -> p n g", g=3),
                                AX.X, ALU.add).then_inc(s_lr, 1)
                dve.drain()
                v.scalar_tensor_tensor(out=lgt, in0=lraw, scalar=1.0 / S, in1=gb, op0=ALU.mult, op1=ALU.add)
                dve.drain()
                v.max(mxt, lgt)
                dve.drain()
                v.tensor_copy(mx[:, bass.ds(t, 1), :], mxt[:, 0:2].rearrange("p (a n) -> p a n", a=1))
                v.max_index(mit, mxt, lgt)
                dve.drain()
                v.tensor_copy(mif[:, bass.ds(t, 1), :], mit[:, 0:2].rearrange("p (a n) -> p a n", a=1))

            def overflow(L, rd):
                with dve.Fori(0, E) as c:
                    for i in range(2):
                        m = 2 * c + i
                        dve.wait_ge(s_oj[L], m * 16 + 16)
                        v.tensor_copy(obf, ob)
                        dve.drain()
                        v.tensor_copy(oB, obf.to_broadcast([P, P])).then_inc(s_o1[L], 1)
                        dve.wait_ge(s_o2[L], m + 1)
                        v.tensor_scalar(oSel, banks[0][:, 0:P], obf, None, ALU.is_equal).then_inc(s_o3[L], 1)
                        dve.drain()
                        v.tensor_tensor(oM, oSel, neg4[:, 0, :], ALU.mult)
                        dve.drain()
                        v.tensor_reduce(oc, oM, AX.X, ALU.add)
                        v.scalar_tensor_tensor(out=od, in0=zrow[:, 0:1], scalar=float(P), in1=obf,
                                               op0=ALU.add, op1=ALU.subtract)
                        dve.drain()
                        v.scalar_tensor_tensor(out=oe, in0=oc, scalar=-1.5, in1=od, op0=ALU.is_lt, op1=ALU.mult)
                        dve.drain()
                        v.tensor_tensor(ow, oe, obf, ALU.add)
                        dve.wait_ge(s_oy[L], m * 16 + 16)
                        dve.wait_ge(s_o4[L], m + 1)
                        v.tensor_tensor(oN, banks[1][:, :], oA, ALU.add).then_inc(s_o5v[L], 1)
                with dve.Fori(0, T) as t:
                    dve.wait_ge(s_ol[L], t * 16 + 16)
                    v.scalar_tensor_tensor(out=oN[:, 0:D], in0=oA[:, D:2 * D], scalar=1.0 / S, in1=oA[:, 0:D],
                                           op0=ALU.mult, op1=ALU.add)
                    dve.drain()
                    v.scalar_tensor_tensor(out=oN[:, D:2 * D], in0=oN[:, 0:D], scalar=rd[:, bass.ds(t, 1)],
                                           in1=R3[:, bass.ds(t * D, D)], op0=ALU.mult, op1=ALU.add)
                    dve.drain()
                    v.tensor_copy(R3[:, bass.ds(t * D, D)], oN[:, D:2 * D]).then_inc(s_o6[L], 1)
                dve.drain()

            dve.wait_ge(s_r3, 1)
            dve.drain()
            lacking = dve.value_load(flag[0:1, 0:1])
            with dve.If(lacking > 0):
                overflow(0, rd1)

            for q in range(Q):
                pairs(0, q, q, q * QB)
            for q in range(Q):
                pairs(0, Q + q, q, TC + q * QB)
            finish1(0)
            with dve.Fori(1, T) as t:
                for q in range(Q):
                    pairs(0, (t + 1) * Q + q, q, (t + 1) * TC + q * QB)
                place1(t - 1)
                finish1(t)
            place1(T - 1)

            def tile4(n, i):
                dve.wait_ge(s_yh, n + 1)
                bank = banks[Y4(i)]
                v.scalar_tensor_tensor(out=R3[:, bass.ds(n * D, D)], in0=bank[:, D:2 * D], scalar=unsc,
                                       in1=zb[:, :], op0=ALU.mult, op1=ALU.add)
                dve.wait_ge(s_yl, n + 1)
                v.scalar_tensor_tensor(out=ylo, in0=bank[:, 0:D], scalar=ysc, in1=R2[:, bass.ds(n * 2 * D, D)],
                                       op0=ALU.mult, op1=ALU.subtract).then_inc(s_zc, 1)

            def low4(g):
                for h, (t0, tn) in enumerate(HALF):
                    for f in range(4):
                        dve.wait_ge(s_hr, g * 8 + 4 * h + f + 5)
                        v.tensor_tensor(hlo4[:, f, t0 * P:(t0 + tn) * P], h4[f][:, 0:tn * P],
                                        hhi4[:, f, t0 * P:(t0 + tn) * P], ALU.subtract).then_inc(s_hl, 1)

            def scales(e):
                dve.wait_ge(s_wt, e + 1)
                v.tensor_copy(nv3[:, 0:2], nr3[:, 0:2])
                v.scalar_tensor_tensor(out=nv3[:, 2:3], in0=nr3[:, 0:1], scalar=float(D) ** 0.5, in1=nr3[:, 2:3],
                                       op0=ALU.mult, op1=ALU.add)
                dve.drain()
                v.tensor_scalar(cl3, nv3, 2.0 ** -60, None, ALU.max)
                dve.drain()
                v.tensor_scalar(ex3, cl3.bitcast(I32), 23, None, ALU.logical_shift_right)
                dve.drain()
                v.tensor_scalar(ab6[:, 0:3], ex3, -1.0, 267.0, ALU.mult, ALU.add)
                v.tensor_scalar(ab6[:, 3:6], ex3, -13.0, None, ALU.add)
                dve.drain()
                v.tensor_scalar(sc6, ab6, 23, None, ALU.logical_shift_left)
                dve.drain()
                sf = sc6.bitcast(F32)
                v.scalar_tensor_tensor(out=iscA[:, bass.ds(e, 1)], in0=sf[:, 2:3], scalar=1.0 / S, in1=sf[:, 3:4],
                                       op0=ALU.mult, op1=ALU.mult)
                v.scalar_tensor_tensor(out=csA[:, bass.ds(e, 1)], in0=sf[:, 5:6], scalar=1.0, in1=sf[:, 4:5],
                                       op0=ALU.mult, op1=ALU.mult)
                v.tensor_scalar(b1A[:, bass.ds(e * 4, 4)], braw, sf[:, 2:3], None, ALU.mult).then_inc(s_wc, 1)

            def lows(e):
                dve.wait_ge(s_wh, e + 1)
                sf = sc6.bitcast(F32)
                for j in range(2):
                    last = v.scalar_tensor_tensor(
                        out=wout[:, (2 * j + 1) * 2 * F:(2 * j + 2) * 2 * F], in0=wraw[:, j * 2 * F:(j + 1) * 2 * F],
                        scalar=sf[:, j:j + 1], in1=wout[:, 2 * j * 2 * F:(2 * j + 1) * 2 * F],
                        op0=ALU.mult, op1=ALU.subtract)
                last.then_inc(s_wo, 1)

            dve.wait_ge(s_ch, 1)
            v.scalar_tensor_tensor(out=WcP[1], in0=Wc[:, :, :], scalar=csc, in1=WcP[0],
                                   op0=ALU.mult, op1=ALU.subtract).then_inc(s_cl, 1)
            scales(0)
            lows(0)
            with dve.Fori(0, T // W) as g:
                low4(g)
                for i in range(W):
                    tile4(g * W + i, i)
                    if i == 2:
                        scales(g + 1)
                    if i == 4:
                        lows(g + 1)

            dve.wait_ge(s_wg, 32)
            v.tensor_tensor(grows[0:1, 2, :], grows[0:1, 0, :], grows[0:1, 1, :], ALU.add).then_inc(s_gv, 1)
            dve.wait_ge(s_gl, 16)
            v.tensor_copy(gpart[:, :, 0, :], graw)
            dve.drain()
            v.tensor_tensor(gres, graw, gpart[:, :, 0, :], ALU.subtract)
            dve.drain()
            v.tensor_copy(gpart[:, :, 1, :], gres)
            dve.drain()
            v.tensor_tensor(gres2, gres, gpart[:, :, 1, :], ALU.subtract)
            dve.drain()
            v.tensor_copy(gpart[:, :, 2, :], gres2).then_inc(s_gs, 1)

            dve.wait_ge(s_yp, W + T)
            dve.wait_ge(s_yl, 1 + T)
            dve.drain()
            with dve.If(lacking > 0):
                overflow(1, rd2)
            for q in range(Q):
                pairs(1, q, q, q * QB)
            dve.wait_ge(s_gp, 1)
            v.tensor_copy(gb, banks[7][:, 0:8])

            def iterate2(t, before):
                for q in range(Q):
                    pairs(1, (t + 1) * Q + q, q, (t + 1) * TC + q * QB)
                    if before and q == 2:
                        normal2(t - 1)
                    if before and q == 8:
                        low2(t - 1)
                if before:
                    logits2(t - 1)
                    dve.wait_ge(s_x2, t * 16)
                finish2(t)

            iterate2(0, False)
            with dve.Fori(1, T) as t:
                iterate2(t, True)
            normal2(T - 1)
            low2(T - 1)
            logits2(T - 1)

            dve.drain()
            v.tensor_tensor(gw[:, :, 0:1], mx[:, :, 1:2], mx[:, :, 0:1], ALU.subtract).then_inc(s_lv, 1)
            dve.drain()
            dve.wait_ge(s_le, 1)
            v.tensor_scalar(gw[:, :, 2:3], gw[:, :, 1:2], 1.0, None, ALU.add)
            dve.drain()
            v.reciprocal(gw[:, :, 3:4], gw[:, :, 2:3])
            dve.drain()
            v.tensor_tensor(gw[:, :, 2:3], gw[:, :, 3:4], gw[:, :, 1:2], ALU.mult)
            i8 = iota8[:, :].rearrange("p (a n) -> p a n", a=1).to_broadcast([P, T, 8])
            v.tensor_tensor(c0, i8, mif[:, :, 0:1].to_broadcast([P, T, 8]), ALU.is_equal)
            v.tensor_tensor(c1, i8, mif[:, :, 1:2].to_broadcast([P, T, 8]), ALU.is_equal)
            dve.drain()
            v.tensor_tensor(comb, c0, gw[:, :, 3:4].to_broadcast([P, T, 8]), ALU.mult)
            v.tensor_tensor(combs, c1, gw[:, :, 2:3].to_broadcast([P, T, 8]), ALU.mult)
            dve.drain()
            v.tensor_tensor(comb, comb, combs, ALU.add)
            dve.drain()
            csb = csA[:, :].rearrange("p (a n) -> p a n", a=1).to_broadcast([P, T, 8])
            v.tensor_tensor(combs, comb, csb, ALU.mult)
            dve.drain()

            def lowh(g, e):
                for h, (t0, tn) in enumerate(HALF):
                    for f in range(4):
                        j = 4 * h + f
                        dve.wait_ge(s_ua, g * 64 + 8 * e + j + 5)
                        v.tensor_tensor(hlo[e % 2][:, f, t0 * P:(t0 + tn) * P], h32[j % 4][:, 0:tn * P],
                                        hhi[e % 2][:, f, t0 * P:(t0 + tn) * P], ALU.subtract).then_inc(s_us, 1)

            def add(g, e):
                if e == 0:
                    dve.wait_ge(s_xr5, g * 16 + 16)
                    dve.wait_ge(s_st, g * 16 + 16)
                for j in range(4):
                    dve.wait_ge(s_dp, g * 32 + 4 * e + j + 9)
                    for i in range(2 * j, min(2 * j + 2, W)):
                        last = v.scalar_tensor_tensor(
                            out=acc[:, i, :], in0=banks[4 + j][:, (i % 2) * D:(i % 2 + 1) * D],
                            scalar=combs[:, bass.ds(g * W + i, 1), e],
                            in1=xr5[:, i, :] if e == 0 else acc[:, i, :], op0=ALU.mult, op1=ALU.add)
                    last.then_inc(s_da, 1)
                dve.drain()

            def add_biases(g):
                for j in range(4):
                    w = min(2, W - 2 * j)
                    dve.wait_ge(s_bp, 4 * g + j + 1)
                    v.tensor_tensor(acc[:, 2 * j:2 * j + w, :],
                                    banks[4 + j][:, 0:w * D].rearrange("p (t n) -> p t n", n=D),
                                    acc[:, 2 * j:2 * j + w, :], ALU.add).then_inc(s_ai, 1)
                dve.drain()

            with dve.Fori(0, T // W) as g:
                dve.wait_ge(s_cc, g + 1)
                v.tensor_copy(combg.rearrange("p (t n) -> p t n", n=8), comb[:, bass.ds(g * W, W), :]).then_inc(s_cb, 1)
                lowh(g, 0)
                for e in range(EXPERTS):
                    if e + 1 < EXPERTS:
                        lowh(g, e + 1)
                    add(g, e)
                    if e == 2:
                        add_biases(g)

        @block.scalar
        def _(act):
            a = nc.scalar
            act.wait_ge(s_const, 1)
            for n, c in ((1, s_ot), (1, s_m), (1, s_xlo), (4, s_ab[0]), (4, s_ab[1]), (2, s_ag[0]), (2, s_ag[1]),
                         (4, s_hr), (1, s_yl), (4, s_ua), (1, s_cc)):
                a.activation(cred[:, 0:1], ones[:, 0:1], ACT.Copy).then_inc(c, n)
                act.drain()

            def group1(par, g):
                act.wait_ge(s_tp, g + 1)
                act.wait_ge(s_r, g + 1)
                a.activation(OHiT[par][0:T, :], bank0h[0:T, :], ACT.Copy).then_inc(s_ot, 1)
                act.wait_ge(s_eq, g + 1)
                for h in range(2):
                    last = a.activation(Mm[par][:, 4 * h:4 * h + 4, :],
                                        banks[1 + h][:, :].rearrange("p (g e) -> p g e", e=P), ACT.Relu)
                last.then_inc(s_m, 1)

            def deviation1(t):
                act.wait_ge(s_stat, t + 1)
                a.activation(rstd[:, :], mv[:, 1:2], ACT.Sqrt, bias=epsc[:, :]).then_inc(s_std, 1)

            def parts1(t):
                act.wait_ge(s_xn, t + 1)
                a.activation(R2[:, bass.ds(t * 2 * D, D)], xs[:, 0:D], ACT.Copy, scale=S).then_inc(s_xhi, 1)
                act.wait_ge(s_xl, t + 1)
                a.activation(R2[:, bass.ds(t * 2 * D + D, D)], xlo, ACT.Copy, scale=S).then_inc(s_xlo, 1)

            act.wait_ge(s_table, 16)
            with act.Fori(0, T) as k:
                group1(0, 2 * k)
                deviation1(k)
                group1(1, 2 * k + 1)
                parts1(k)
            with act.Fori(T, GROUPS // 2) as k:
                group1(0, 2 * k)
                group1(1, 2 * k + 1)
            group1(0, GROUPS)

            act.wait_ge(s_w, 16 * 16)
            act.wait_ge(s_vm, 8)
            for j, src in enumerate((W0s, W1s, bhs[:, :], Wc[:, :, 0:D], Wc[:, :, D:2 * D])):
                dst = sqs[:, 0:4] if j == 2 else sqs.rearrange("p (k n) -> p k n", k=2 if j < 2 else 4)
                last = a.activation(dst, src, ACT.Square, accum_out=small[:, 35 + j:36 + j])
                act.drain()
            a.activation(cred[:, 1:2], ones[:, 0:1], ACT.Copy).then_inc(s_sq, 1)
            act.wait_ge(s_sp, 1)
            a.activation(small[:, 40:45], banks[3][:, 0:5], ACT.Sqrt).then_inc(s_sr, 1)

            def evac(L, n, q):
                act.wait_ge(s_bl[L], n + 1 + Q)
                act.wait_ge(s_ap[L], n + 1)
                n = blocks(q) * P
                a.activation(Ab[q][:, 0:n], banks[BB(q)][:, 0:n], ACT.Copy).then_inc(s_ab[L], 1)

            def copy(L, t, bank):
                act.wait_ge(s_ap[L], (t + 1) * Q + Q)
                act.wait_ge(s_an[L], t + 1)
                a.activation(aggr, bank[:, :], ACT.Copy).then_inc(s_ag[L], 1)

            def deviation(t):
                act.wait_ge(s_v2, t + 1)
                a.activation(x2r, x2m[:, 1:2], ACT.Sqrt, bias=epsc[:, :]).then_inc(s_d2, 1)

            def high2(t):
                act.wait_ge(s_t2, t + 1)
                a.activation(R3t(t, 0), banks[6][:, 0:D], ACT.Copy, scale=S).then_inc(s_h2, 1)

            def iterate(L, t, before, bank):
                for q in range(Q):
                    evac(L, t * Q + q + LEAD, (q + LEAD) % Q)
                    if before and q == 0:
                        deviation(t - 1)
                    if before and q == 7:
                        high2(t - 1)
                copy(L, t, bank)

            def aggregate(L):
                for q in range(LEAD):
                    evac(L, q, q)
                iterate(L, 0, False, banks[5])
                with act.Fori(0, T // 2) as k:
                    iterate(L, 2 * k + 1, L == 1, banks[7])
                    iterate(L, 2 * k + 2, L == 1, banks[5])
                if L == 1:
                    deviation(T - 1)
                    high2(T - 1)

            aggregate(0)

            def squares(e):
                act.wait_ge(s_wl, 48 * e + 48)
                a.activation(wsq, wraw[:, 0:2 * F], ACT.Square, accum_out=sq3[:, 0:1])
                act.drain()
                a.activation(wsq, wraw[:, 2 * F:4 * F], ACT.Square, accum_out=sq3[:, 1:2])
                act.drain()
                a.activation(wsq[:, 0:4], braw, ACT.Square, accum_out=sq3[:, 2:3])
                act.drain()
                a.activation(cred[:, 1:2], ones[:, 0:1], ACT.Copy).then_inc(s_wq, 1)
                act.drain()

            def norms(e):
                act.wait_ge(s_wr, e + 1)
                a.activation(nr3, nr3, ACT.Sqrt).then_inc(s_wt, 1)

            def highs(e):
                act.wait_ge(s_wc, e + 1)
                sf = sc6.bitcast(F32)
                for j in range(2):
                    last = a.activation(wout[:, 2 * j * 2 * F:(2 * j + 1) * 2 * F], wraw[:, j * 2 * F:(j + 1) * 2 * F],
                                        ACT.Copy, scale=sf[:, j:j + 1])
                last.then_inc(s_wh, 1)

            act.wait_ge(s_ac, 1 + T)
            act.wait_ge(s_sc2, 1)
            a.activation(WcP[0], Wc[:, :, :], ACT.Copy, scale=csc).then_inc(s_ch, 1)
            squares(0)
            norms(0)
            highs(0)
            with act.Fori(0, T // W) as g:
                for h, (t0, tn) in enumerate(HALF):
                    for f in range(4):
                        j = 4 * h + f
                        act.wait_ge(s_hp, g * 8 + j + 1)
                        if j == 0:
                            act.wait_ge(s_yp, g * W + W)
                        act.wait_ge(s_hl, g * 8 + j + 1)
                        a.activation(hhi4[:, f, t0 * P:(t0 + tn) * P], banks[f][:, 0:tn * P], ACT.Relu,
                                     bias=sbh[:, f:f + 1], scale=hsc)
                        a.activation(h4[f][:, 0:tn * P], banks[f][:, 0:tn * P], ACT.Relu,
                                     bias=sbh[:, f:f + 1], scale=hsc).then_inc(s_hr, 1)
                for i in range(W):
                    n = g * W + i
                    act.wait_ge(s_yp, n + 1 + W)
                    a.activation(R2[:, bass.ds(n * 2 * D, D)],
                                 banks[Y4(i)][:, 0:D], ACT.Copy, scale=ysc).then_inc(s_yh, 1)
                    act.wait_ge(s_zc, n + 4)
                    a.activation(R2[:, bass.ds(n * 2 * D + D, D)], ylo, ACT.Copy, scale=S).then_inc(s_yl, 1)
                    if i == 0:
                        squares(g + 1)
                    if i == 2:
                        norms(g + 1)
                    if i == 4:
                        highs(g + 1)
            act.wait_ge(s_yp, W + T)
            aggregate(1)

            act.wait_ge(s_lv, 1)
            a.activation(gw[:, :, 1:2], gw[:, :, 0:1], ACT.Exp).then_inc(s_le, 1)
            with act.Fori(0, T // W) as g:
                for e in range(EXPERTS):
                    for h, (t0, tn) in enumerate(HALF):
                        for f in range(4):
                            j = 4 * h + f
                            act.wait_ge(s_up, g * 64 + 8 * e + j + 1)
                            if j == 0:
                                act.wait_ge(s_dp, g * 32 + 4 * e + 4)
                            act.wait_ge(s_us, g * 64 + 8 * e + j + 1)
                            sc, bi = iscA[:, e:e + 1], b1A[:, 4 * e + f:4 * e + f + 1]
                            a.activation(hhi[e % 2][:, f, t0 * P:(t0 + tn) * P], banks[j % 4][:, 0:tn * P],
                                         ACT.Relu, bias=bi, scale=sc)
                            a.activation(h32[j % 4][:, 0:tn * P], banks[j % 4][:, 0:tn * P],
                                         ACT.Relu, bias=bi, scale=sc).then_inc(s_ua, 1)
                    if e == 3:
                        for j in range(2):
                            act.wait_ge(s_ct, 2 * g + j + 1)
                            n = 4 if j == 0 else 3
                            last = a.activation(combT[0:8, 4 * j:4 * j + n, :],
                                                banks[6 + j][0:8, 0:n * P].rearrange("p (t n) -> p t n", n=P), ACT.Copy)
                        last.then_inc(s_cc, 1)

        @block.tensor
        def _(pe):
            mm = nc.tensor.matmul
            pe.wait_ge(s_const, 1)
            for n, c in ((2, s_r), (1, s_xt), (Q, s_bl[0]), (Q, s_bl[1]), (Q, s_ap[0]), (Q, s_ap[1]),
                         (W, s_yp), (8, s_dp)):
                mm(banks[6][:, 0:P], zeros16[:, :], zeros16[:, :], start=True, stop=True).then_inc(c, n)
            for h in range(2):
                mm(banks[6 + h][:, :], zeros16[:, :], zeros16[:, 0:1].to_broadcast([P, 512]), start=True, stop=False)

            def groupA(par, g):
                pe.wait_ge(s_ot, g + 1)
                pe.wait_ge(s_oh, g + 1)
                pe.wait_ge(s_t, g + 1)
                for c in range(G):
                    mm(banks[3][0:T, c * T:G * T], OHi[par][:, :, c],
                       OHj[par][:, :, c].rearrange("p (a j) -> p a j", a=1).to_broadcast([P, G - c, T]),
                       start=(c == 0), stop=(c == G - 1))
                for c in range(G):
                    last = nc.tensor.transpose(bank0h[0:T, c * P:(c + 1) * P], OHi[par][:, :, c], ident16[:, :])
                last.then_inc(s_tp, 1)
                for c in range(G):
                    mm(banks[6][0:T, DEG:DEG + P], OHi[par][:, :, c], LHi[par][:, :, c], start=False, stop=False)
                    last = mm(banks[6][0:T, DEG:DEG + P], OHj[par][:, :, c], LLo[par][:, :, c], start=False, stop=False)
                last.then_inc(s_h, 1)
                pe.wait_ge(s_m, g + 1)
                for h in range(2):
                    mm(banks[1 + h][:, :], ident16[:, :], neg4[:, :, :].rearrange("p c e -> p (c e)"),
                       start=True, stop=False)
                pe.wait_ge(s_ot, g + 2)
                for c in range(G):
                    ot = OHiT[par][0:T, c * P:(c + 1) * P]
                    last = mm(banks[1 + c // 4][:, (c % 4) * P:(c % 4 + 1) * P], ot, ot, start=False, stop=(c % 4 == 3))
                last.then_inc(s_eq, 1)

            def groupF(par, g):
                pe.wait_ge(s_m, g + 2)
                pe.wait_ge(s_t, g + 2)
                pe.wait_ge(s_rk, g + 1)
                for c in range(G):
                    o = banks[4][:, c * T:(c + 1) * T]
                    mm(o, Mm[par][:, c, :], OHj[par][:, :, c], start=True, stop=False)
                    last = mm(o, OHiT[par][0:T, c * P:(c + 1) * P], Tsn[par][0:T, c, :], start=False, stop=True)
                last.then_inc(s_r, 1)

            def gram(t):
                pe.wait_ge(s_xn, t + 1)
                pe.wait_ge(s_xtc, t + 1)
                for h in range(2):
                    nc.tensor.transpose(banks[5][:, h * P:(h + 1) * P], xs[:, h * P:(h + 1) * P], ident[:, :])
                for h in range(2):
                    last = mm(banks[6 + h][:, 0:D + 1], xs[:, h * P:(h + 1) * P], xs[:, 0:D + 1],
                              start=False, stop=False)
                last.then_inc(s_xt, 1)

            def two_groups(k, norm):
                groupF(0, 2 * k)
                groupA(1, 2 * k + 1)
                if norm:
                    gram(k)
                groupF(1, 2 * k + 1)
                groupA(0, 2 * k + 2)

            groupA(0, 0)
            with pe.Fori(0, T) as k:
                two_groups(k, True)
            with pe.Fori(T, GROUPS // 2) as k:
                two_groups(k, False)
            pe.wait_ge(s_ot, GROUPS + 2)
            pe.wait_ge(s_m, GROUPS + 2)
            pe.wait_ge(s_rk, GROUPS + 1)

            pe.wait_ge(s_w, 16 * 16)
            mm(banks[6][:, 0:P], zeros16[:, :], zeros16[:, :], start=False, stop=True)
            mm(banks[7][:, 0:P], zeros16[:, :], zeros16[:, :], start=False, stop=True).then_inc(s_pm, 1)
            for i, wgt in enumerate((Wk, Wv, Wfc)):
                if i == 0:
                    pe.wait_ge(s_xtc, T + 1)
                for kt in range(2):
                    for dt in range(2):
                        last = nc.tensor.transpose(banks[i][:, dt * D + kt * P:dt * D + (kt + 1) * P],
                                                   wgt[:, kt, dt * P:(dt + 1) * P], ident[:, :])
                last.then_inc(s_pm, 1)
            pe.wait_ge(s_vm, 3)
            for gt in range(2):
                for dt in range(2):
                    mm(banks[3][:, gt * D:(gt + 1) * D], Gs[:, dt, gt * P:(gt + 1) * P], WvT[:, dt, :],
                       start=(dt == 0), stop=(dt == 1))
            for r, wt in ((0, WvT), (1, WkT)):
                for dt in range(2):
                    last = mm(banks[4][0:1, r * D:(r + 1) * D], Gs[:, dt, D:D + 1], wt[:, dt, :],
                              start=(dt == 0), stop=(dt == 1))
            last.then_inc(s_pm, 1)
            pe.wait_ge(s_vm, 5)
            for vt in range(2):
                o = banks[0][:, vt * D:(vt + 1) * D]
                for gt in range(2):
                    mm(o, B1s[:, gt, vt * P:(vt + 1) * P], WkT[:, gt, :], start=(gt == 0), stop=False)
                mm(o, rows[0:1, SV, vt * P:(vt + 1) * P], rows[0:1, BK, :], start=False, stop=False)
                last = mm(o, rows[0:1, BV, vt * P:(vt + 1) * P], rows[0:1, SK, :], start=False, stop=True)
            last.then_inc(s_pm, 1)
            pe.wait_ge(s_vm, 6)
            for dt in range(2):
                for et in range(2):
                    last = mm(banks[1][:, dt * D:(dt + 1) * D], PTs[:, et, dt * P:(dt + 1) * P], WfT[:, et, :],
                              start=(et == 0), stop=(et == 1))
            last.then_inc(s_pm, 1)
            pe.wait_ge(s_vm, 7)
            for xt in range(2):
                for dt in range(2):
                    mm(banks[2][:, xt * D:(xt + 1) * D], Wq[:, dt, xt * P:(xt + 1) * P], Rs[:, dt, :],
                       start=(dt == 0), stop=(dt == 1))
            for dt in range(2):
                last = mm(banks[3][0:1, 0:D], bqc[:, dt:dt + 1], Rs[:, dt, :], start=(dt == 0), stop=(dt == 1))
            last.then_inc(s_pm, 1)
            pe.wait_ge(s_vm, 8)
            mm(banks[4][:, 0:D], ones[0:1, :], rows[0:1, ZB, :], start=True, stop=True).then_inc(s_pm, 1)
            pe.wait_ge(s_vm, 10)
            nc.tensor.transpose(banks[1][:, 0:T], degT[0:T, :], ident[0:T, 0:T]).then_inc(s_pm, 1)
            pe.wait_ge(s_sq, 1)
            mm(banks[3][:, 0:5], ones[:, :], small[:, 35:40], start=True, stop=True).then_inc(s_sp, 1)
            pe.wait_ge(s_vm, 12)
            pe.wait_ge(s_sr, 1)
            pe.wait_ge(s_flag, 1)
            mm(banks[2][:, 0:1], ones[:, :], small[:, 56:57], start=True, stop=True).then_inc(s_fp, 1)
            pe.wait_ge(s_flag, 2)
            lacking = pe.value_load(flag[0:1, 0:1])

            def overflow(L):
                with pe.Fori(0, E) as c:
                    for i in range(2):
                        m = 2 * c + i
                        pe.wait_ge(s_o1[L], m + 1)
                        nc.tensor.transpose(banks[0][:, 0:P], oB, ident[:, :]).then_inc(s_o2[L], 1)
                        pe.wait_ge(s_ox[L], m * 16 + 16)
                        pe.wait_ge(s_o3[L], m + 1)
                        mm(banks[1][:, :], oSel, oX, start=True, stop=True).then_inc(s_o4[L], 1)

            def build(L, n, q):
                pe.wait_ge(s_oo[L], n + 1)
                pe.wait_ge(s_ab[L], n + 1)
                for c in range(QB):
                    own = q == Q - 1 and c >= 1
                    o = 1 if own else c
                    last = mm(banks[BB(q)][:, o * P:(o + 1) * P], OU[q][:, :, c], OT[q][:, :, c],
                              start=(not own or c == 1), stop=(not own or c == QB - 1))
                last.then_inc(s_bl[L], 1)

            def apply(L, t, q, bank):
                if q == 0:
                    pe.wait_ge(s_ag[L], t + 1)
                pe.wait_ge(s_ab[L], t * Q + q + 5)
                for c in range(blocks(q)):
                    u = q * QB + c
                    src = R2[:, u * 2 * D:(u + 1) * 2 * D] if u < T else R2[:, bass.ds(t * (2 * D), 2 * D)]
                    last = mm(bank[:, :], Ab[q][:, c * P:(c + 1) * P], src, start=(u == 0), stop=(u == T))
                last.then_inc(s_ap[L], 1)

            def transposed(t):
                pe.wait_ge(s_an[0], t + 2)
                pe.wait_ge(s_ac, t + 1)
                for h in range(2):
                    last = nc.tensor.transpose(banks[6][:, h * P:(h + 1) * P], aggn[:, h * P:(h + 1) * P], ident[:, :])
                last.then_inc(s_at, 1)

            def transposed2(t):
                pe.wait_ge(s_n2, t + 1)
                pe.wait_ge(s_lr, t + 1)
                for k in range(2):
                    last = nc.tensor.transpose(banks[6][:, k * P:(k + 1) * P], x2n[:, k * P:(k + 1) * P], ident[:, :])
                last.then_inc(s_t2, 1)

            def gate(t):
                pe.wait_ge(s_l2, t + 1)
                for part in range(2):
                    for k in range(2):
                        last = mm(banks[6][:, D:D + 24], R3t(t, part)[:, k * P:(k + 1) * P],
                                  gpart[:, k, :, :].rearrange("p g n -> p (g n)"),
                                  start=(part + k == 0), stop=(part + k == 2))
                last.then_inc(s_lp, 1)

            def tile3(L, t, before, bank):
                for q in range(Q):
                    build(L, t * Q + q + LEAD, (q + LEAD) % Q)
                    apply(L, t, q, bank)
                    if q == 6 and before and L == 0:
                        transposed(t - 1)
                    if q == 5 and before and L == 1:
                        transposed2(t - 1)
                    if q == 11 and before and L == 1:
                        gate(t - 1)

            def tiles3(L):
                tile3(L, 0, False, banks[5])
                with pe.Fori(0, T // 2) as k:
                    tile3(L, 2 * k + 1, True, banks[7])
                    tile3(L, 2 * k + 2, True, banks[5])

            pe.wait_ge(s_xhi, T)
            pe.wait_ge(s_xlo, 1 + T)
            with pe.If(lacking > 0):
                overflow(0)
            for q in range(LEAD):
                build(0, q, q)
            tiles3(0)
            transposed(T - 1)

            pe.wait_ge(s_ac, 1 + T)
            pe.wait_ge(s_sc2, 1)
            pe.wait_ge(s_ab[0], T * Q + LEAD + 4)
            pe.wait_ge(s_ag[0], 2 + T)
            def hidden(g, par, need):
                pe.wait_ge(s_x4[par], need)
                for h, (t0, tn) in enumerate(HALF):
                    xv = xT4[par][:, t0 * D:(t0 + tn) * D].rearrange("p (t k n) -> p t k n", t=tn, k=2)
                    av = R3[:, bass.ds(g * (W * D) + t0 * D, tn * D)].rearrange("p (t k n) -> p t k n", t=tn, k=2)
                    for f in range(4):
                        j = 4 * h + f
                        pe.wait_ge(s_hr, g * 8 + j + 1)
                        o = banks[f][:, 0:tn * P].rearrange("p (t n) -> p t n", n=P)
                        for k in range(2):
                            mm(o, W0s[:, k, f * P:(f + 1) * P], xv[:, :, k, :], start=(k == 0), stop=False)
                        for k in range(2):
                            last = mm(o, W1s[:, k, f * P:(f + 1) * P], av[:, :, k, :], start=False, stop=(k == 1))
                        last.then_inc(s_hp, 1)
                pe.wait_ge(s_cl, 1)
                for i in range(W):
                    n = g * W + i
                    if i in (0, 4):
                        pe.wait_ge(s_hl, g * 8 + 8 + i)
                    pe.wait_ge(s_zc, n + 1)
                    o = banks[Y4(i)]
                    for f in range(4):
                        for n2, (hp, wp) in enumerate(((hhi4, 0), (hhi4, 1), (hlo4, 0))):
                            mm(o[:, :], hp[:, f, i * P:(i + 1) * P], WcP[wp][:, f, :],
                               start=(f == 0 and n2 == 0), stop=False)
                    for k in range(2):
                        last = mm(o[:, D:2 * D], xT4[par][:, i * D + k * P:i * D + (k + 1) * P], Ms[:, k, :],
                                  start=False, stop=(k == 1))
                    last.then_inc(s_yp, 1)

            with pe.Fori(0, T // W // 2) as k2:
                for par in range(2):
                    hidden(2 * k2 + par, par, 16 * k2 + 16)
            hidden(T // W - 1, 0, 16 * (T // W // 2 + 1))

            pe.wait_ge(s_yl, 1 + T)
            pe.wait_ge(s_zc, 3 + T)
            with pe.If(lacking > 0):
                overflow(1)
            for q in range(LEAD):
                build(1, q, q)
            pe.wait_ge(s_gs, 1)
            pe.wait_ge(s_gv, 1)
            mm(banks[7][:, 0:8], ones[0:1, :], grows[0:1, 2, :], start=True, stop=True).then_inc(s_gp, 1)
            tiles3(1)
            transposed2(T - 1)
            gate(T - 1)

            pe.wait_ge(s_ab[1], T * Q + LEAD + 4)
            pe.wait_ge(s_ag[1], 2 + T)
            pe.wait_ge(s_lr, 1 + T)
            pe.wait_ge(s_st, 16)
            with pe.Fori(0, T // W) as g:
                def up(e):
                    pe.wait_ge(s_we[e], 16)
                    for h, (t0, tn) in enumerate(HALF):
                        xv = R3h[:, bass.ds(g * (W * 2 * D) + t0 * 2 * D, tn * 2 * D)]\
                            .rearrange("p (t s k n) -> p t s k n", t=tn, s=2, k=2)
                        for f in range(4):
                            j = 4 * h + f
                            pe.wait_ge(s_ua, g * 64 + 8 * e + j + 1)
                            o = banks[j % 4][:, 0:tn * P].rearrange("p (t n) -> p t n", n=P)
                            n = 0
                            for k in range(2):
                                for wp, xp in ((0, 0), (0, 1), (1, 0)):
                                    last = mm(o, w1(e, wp, k)[:, f * P:(f + 1) * P], xv[:, :, xp, k, :],
                                              start=(n == 0), stop=(n == 5))
                                    n += 1
                            last.then_inc(s_up, 1)

                def down(e):
                    pe.wait_ge(s_us, g * 64 + 8 * e + 8 + 4)
                    for j in range(4):
                        pe.wait_ge(s_da, g * 32 + 4 * e + j + 1)
                        if e == 2 and j == 2:
                            pe.wait_ge(s_cc, g + 2)
                        if e == 3:
                            pe.wait_ge(s_ai, 4 * g + j + 1)
                        for i in range(2 * j, min(2 * j + 2, W)):
                            o = banks[4 + j][:, (i % 2) * D:(i % 2 + 1) * D]
                            n = 0
                            for f in range(4):
                                for hp, wp in ((hhi, 0), (hhi, 1), (hlo, 0)):
                                    last = mm(o, hp[e % 2][:, f, i * P:(i + 1) * P], w2(e, wp, f),
                                              start=(n == 0), stop=(n == 11))
                                    n += 1
                        last.then_inc(s_dp, 1)

                def turned():
                    pe.wait_ge(s_cb, g + 1)
                    pe.wait_ge(s_da, g * 32 + 12)
                    for i in range(W):
                        last = nc.tensor.transpose(banks[6 + i // 4][0:8, (i % 4) * P:(i % 4 + 1) * P],
                                                   combg[:, i * 8:(i + 1) * 8], ident[:, :])
                        if i in (3, 6):
                            last.then_inc(s_ct, 1)

                def biases():
                    pe.wait_ge(s_cc, g + 2)
                    for j in range(4):
                        pe.wait_ge(s_da, g * 32 + 12 + j + 1)
                        for i in range(2 * j, min(2 * j + 2, W)):
                            last = mm(banks[4 + j][:, (i % 2) * D:(i % 2 + 1) * D], combT[0:8, i, :], b2s[0:8, :],
                                      start=True, stop=True)
                        last.then_inc(s_bp, 1)

                up(0)
                for e in range(EXPERTS):
                    if e + 1 < EXPERTS:
                        up(e + 1)
                    if e == 2:
                        turned()
                    if e == 3:
                        biases()
                    down(e)


_INS = ["x", "src", "dst", "L0_gnn_W0_0", "L0_gnn_b0_0", "L0_gnn_W1_0", "L0_gnn_b1_0", "L0_gnn_W0_1",
        "L0_gnn_b0_1", "L0_gnn_W1_1", "L0_gnn_b1_1", "L0_mix_Wq", "L0_mix_bq", "L0_mix_Wk", "L0_mix_bk",
        "L0_mix_Wv", "L0_mix_bv", "L0_mix_Wfc", "L0_mix_bfc", "L0_ffn_Wg", "L0_ffn_bg", "L0_ffn_bias",
        "L0_ffn_W1", "L0_ffn_b1", "L0_ffn_W2", "L0_ffn_b2"]


def kernel(**inputs):
    import numpy as _np
    import concourse.bacc as _bacc
    from concourse import mybir as _mybir
    from concourse.bass_utils import run_bass_kernel_spmd as _run

    nc = _bacc.Bacc("TRN2", target_bir_lowering=False, num_devices=1)
    arrays, io = {}, {}
    for name in _INS:
        a = _np.ascontiguousarray(inputs[name])
        arrays[f"in_{name}_dram"] = a
        io[name] = nc.dram_tensor(f"in_{name}_dram", a.shape, _mybir.dt.from_np(a.dtype), kind="ExternalInput").ap()
    io["out"] = nc.dram_tensor("out_dram", (N, D), _mybir.dt.float32, kind="ExternalOutput").ap()
    gps_layer(nc, io)
    r = _run(nc, [arrays], core_ids=[0])
    return r.results[0]["out_dram"]
```
